# Optimizing a Trainium2 kernel written in Bass

```python
import numpy as np
import jax
import jax.numpy as jnp

def _softmax(x, axis=-1):
    return jax.nn.softmax(x, axis=axis)

def _gelu(x):
    return jax.nn.gelu(x, approximate=True)

def _silu(x):
    return jax.nn.silu(x)

def _sigmoid(x):
    return jax.nn.sigmoid(x)

def _layernorm(x, axis=-1, eps=1e-05):
    m = jnp.mean(x, axis=axis, keepdims=True)
    v = jnp.var(x, axis=axis, keepdims=True)
    return (x - m) / jnp.sqrt(v + eps)

def _scatter_add(tgt, idx, src, axis=0):
    return tgt.at[idx].add(src)

def _segment_sum(src, seg, n):
    return jax.ops.segment_sum(src, seg, n)
kernel_name = 'mk_vit_tower_postln_d4_tok_img1024_r4_0de6cd'

def setup_inputs(seed: int=0):
    np.random.seed(seed)
    _w = jnp.asarray

    def _rec_inputs():
        import jax
        import jax.numpy as jnp
        _rk = jax.random.key(seed)
        x = -0.00016672 + 0.999947 * jax.random.normal(jax.random.fold_in(_rk, 1), (32, 3, 96, 96), jnp.float32)
        return x
    x = _rec_inputs()

    def _L0_tok_setup():
        import jax, jax.numpy as jnp
        import numpy as np
        B, C, H, Wd = (64, 3, 96, 96)
        PH, PW, D = (16, 16, 256)
        PATCH_DIM = C * PH * PW
        N_TOK = H // PH * (Wd // PW)
        key = jax.random.key(seed)
        k1, k2, k3, k4, k5 = jax.random.split(key, 5)
        x = jax.random.normal(k1, (B, C, H, Wd), dtype=jnp.float32)
        W = jax.random.normal(k2, (D, PATCH_DIM), dtype=jnp.float32) * PATCH_DIM ** (-0.5)
        b = jax.random.normal(k3, (D,), dtype=jnp.float32) * 0.02
        cls_token = jax.random.normal(k4, (1, 1, D), dtype=jnp.float32)
        pos_embedding = jax.random.normal(k5, (1, N_TOK + 1, D), dtype=jnp.float32) * 0.02
        return {'x': x, 'W': W, 'b': b, 'cls_token': cls_token, 'pos_embedding': pos_embedding}
    _L0_tok_all = _L0_tok_setup()
    _L0_tok_in = {k: v for k, v in _L0_tok_all.items() if k in ('W', 'b', 'cls_token', 'pos_embedding')}
    del _L0_tok_all

    def _L0_attn_setup():
        import jax, jax.numpy as jnp
        import numpy as np
        HEADS = 16
        key = jax.random.key(seed)
        ks = jax.random.split(key, 6)
        b, n, c = (4, 512, 256)
        h = 256
        s = 0.02
        return {'x': jax.random.normal(ks[0], (b, n, c), jnp.float32), 'Wq': jax.random.normal(ks[1], (h, c), jnp.float32) * s, 'Wk': jax.random.normal(ks[2], (h, c), jnp.float32) * s, 'Wv': jax.random.normal(ks[3], (h, c), jnp.float32) * s, 'Wout': jax.random.normal(ks[4], (c, h), jnp.float32) * s, 'bout': jnp.zeros((c,), jnp.float32)}
    _L0_attn_all = _L0_attn_setup()
    _L0_attn_in = {k: v for k, v in _L0_attn_all.items() if k in ('Wq', 'Wk', 'Wv', 'Wout', 'bout')}
    del _L0_attn_all

    def _L0_ffn_setup():
        import jax, jax.numpy as jnp
        import numpy as np
        D_MODEL = 256
        HIDDEN = 512
        N_EXPERTS = 8
        TOP_K = 2
        key = jax.random.key(seed)
        ks = jax.random.split(key, 5)
        s_in = 1.0 / np.sqrt(D_MODEL)
        s_h = 1.0 / np.sqrt(HIDDEN)
        x = jax.random.normal(ks[0], (4, 512, D_MODEL), dtype=jnp.float32)
        Wr = jax.random.uniform(ks[1], (D_MODEL, N_EXPERTS), minval=-s_in, maxval=s_in, dtype=jnp.float32)
        Wg = jax.random.uniform(ks[2], (N_EXPERTS, D_MODEL, HIDDEN), minval=-s_in, maxval=s_in, dtype=jnp.float32)
        Wu = jax.random.uniform(ks[3], (N_EXPERTS, D_MODEL, HIDDEN), minval=-s_in, maxval=s_in, dtype=jnp.float32)
        Wd = jax.random.uniform(ks[4], (N_EXPERTS, HIDDEN, D_MODEL), minval=-s_h, maxval=s_h, dtype=jnp.float32)
        return {'x': x, 'Wr': Wr, 'Wg': Wg, 'Wu': Wu, 'Wd': Wd}
    _L0_ffn_all = _L0_ffn_setup()
    _L0_ffn_in = {k: v for k, v in _L0_ffn_all.items() if k in ('Wr', 'Wg', 'Wu', 'Wd')}
    del _L0_ffn_all

    def _L1_attn_setup():
        import jax, jax.numpy as jnp
        import numpy as np
        B, T, D, S = (4, 512, 256, 64)
        EPS = 1e-08
        key = jax.random.key(seed)
        ks = jax.random.split(key, 6)
        return {'token_embeddings': jax.random.normal(ks[0], (B, T, D), dtype=jnp.float32), 'splat_positions': jax.random.normal(ks[1], (S, D), dtype=jnp.float32), 'splat_log_scales': jax.random.uniform(ks[2], (S,), dtype=jnp.float32), 'splat_amplitudes': jax.random.uniform(ks[3], (S,), dtype=jnp.float32), 'Wv': jax.random.normal(ks[4], (D, D), dtype=jnp.float32) / np.sqrt(D).astype(np.float32), 'Wo': jax.random.normal(ks[5], (D, D), dtype=jnp.float32) / np.sqrt(D).astype(np.float32)}
    _L1_attn_all = _L1_attn_setup()
    _L1_attn_in = {k: v for k, v in _L1_attn_all.items() if k in ('splat_positions', 'splat_log_scales', 'splat_amplitudes', 'Wv', 'Wo')}
    del _L1_attn_all

    def _L1_ffn_setup():
        import jax, jax.numpy as jnp
        import numpy as np
        B, S, H = (2, 256, 256)
        E, F = (16, 128)
        G, TOPK_G, TOPK = (4, 2, 4)
        N_SHARED = 2
        ROUTE_SCALE = 1.0
        FS = N_SHARED * F

        def _gate(x, w_gate):
            T = x.shape[0]
            scores = jax.nn.sigmoid(x @ w_gate.T)
            sv = scores.reshape(T, G, E // G)
            group_scores = jax.lax.top_k(sv, 2)[0].sum(-1)
            top_groups = jax.lax.top_k(group_scores, TOPK_G)[1]
            allowed = jnp.zeros((T, G), dtype=bool).at[jnp.arange(T)[:, None], top_groups].set(True)
            masked = jnp.where(allowed[:, :, None], sv, -jnp.inf).reshape(T, E)
            _, idx = jax.lax.top_k(masked, TOPK)
            w = jnp.take_along_axis(scores, idx, axis=1)
            w = w / (w.sum(-1, keepdims=True) + 1e-06) * ROUTE_SCALE
            return (w, idx)

        def _swiglu(x, w1, w3, w2):
            return jax.nn.silu(x @ w1.T) * (x @ w3.T) @ w2.T
        key = jax.random.key(seed)
        ks = jax.random.split(key, 8)
        scale = 0.02
        return {'hidden_states': jax.random.normal(ks[0], (B, S, H), dtype=jnp.float32), 'w_gate': jax.random.normal(ks[1], (E, H), dtype=jnp.float32) * scale, 'w1_e': jax.random.normal(ks[2], (E, F, H), dtype=jnp.float32) * scale, 'w3_e': jax.random.normal(ks[3], (E, F, H), dtype=jnp.float32) * scale, 'w2_e': jax.random.normal(ks[4], (E, H, F), dtype=jnp.float32) * scale, 'w1_s': jax.random.normal(ks[5], (FS, H), dtype=jnp.float32) * scale, 'w3_s': jax.random.normal(ks[6], (FS, H), dtype=jnp.float32) * scale, 'w2_s': jax.random.normal(ks[7], (H, FS), dtype=jnp.float32) * scale}
    _L1_ffn_all = _L1_ffn_setup()
    _L1_ffn_in = {k: v for k, v in _L1_ffn_all.items() if k in ('w_gate', 'w1_e', 'w3_e', 'w2_e', 'w1_s', 'w3_s', 'w2_s')}
    del _L1_ffn_all

    def _L2_attn_setup():
        import jax, jax.numpy as jnp
        import numpy as np
        B, N, D = (2, 512, 256)
        H, M = (8, 64)
        DK = D // H
        EPS = 1e-05

        def _gsa(q, k, v, s, g):
            b = q.shape[1]

            def step1(hk, t):
                q_t, k_t, s_t, g_t = t
                hk = hk * jnp.exp(g_t)[:, :, None, :] + k_t[..., :, None] * s_t[..., None, :]
                ok = jnp.einsum('bhk,bhkm->bhm', q_t, hk)
                return (hk, ok)
            hk0 = jnp.zeros((b, H, DK, M), q.dtype)
            _, ok = jax.lax.scan(step1, hk0, (q, k, s, g))
            qv = jax.nn.softmax(ok, axis=-1)

            def step2(hv, t):
                qv_t, s_t, v_t, g_t = t
                hv = hv * jnp.exp(g_t)[..., :, None] + s_t[..., :, None] * v_t[..., None, :]
                ov = jnp.einsum('bhm,bhmv->bhv', qv_t, hv)
                return (hv, ov)
            hv0 = jnp.zeros((b, H, M, DK), q.dtype)
            _, ov = jax.lax.scan(step2, hv0, (qv, s, v, g))
            return ov
        key = jax.random.key(seed)
        ks = jax.random.split(key, 9)
        std = 0.02
        return {'x': jax.random.normal(ks[0], (B, N, D), jnp.float32), 'Wq': jax.random.normal(ks[1], (D, D), jnp.float32) * std, 'Wk': jax.random.normal(ks[2], (D, D), jnp.float32) * std, 'Wv': jax.random.normal(ks[3], (D, D), jnp.float32) * std, 'Wf1': jax.random.normal(ks[4], (D, DK), jnp.float32) * std, 'Wf2': jax.random.normal(ks[5], (DK, H * M), jnp.float32) * std, 'Wg1': jax.random.normal(ks[6], (D, DK), jnp.float32) * std, 'Wg2': jax.random.normal(ks[7], (DK, D), jnp.float32) * std, 'Wo': jax.random.normal(ks[8], (D, D), jnp.float32) * std, 'norm_w': jnp.ones((D,), jnp.float32)}
    _L2_attn_all = _L2_attn_setup()
    _L2_attn_in = {k: v for k, v in _L2_attn_all.items() if k in ('Wq', 'Wk', 'Wv', 'Wf1', 'Wf2', 'Wg1', 'Wg2', 'Wo', 'norm_w')}
    del _L2_attn_all

    def _L2_ffn_setup():
        import jax, jax.numpy as jnp
        import numpy as np
        DIM = 256
        HIDDEN = 768
        SCALE = 1.0 / 127.0

        def _dequant(w_int, dtype):
            return w_int.astype(dtype) * jnp.asarray(SCALE, dtype)
        key = jax.random.key(seed)
        k_x, k_g, k_u, k_d = jax.random.split(key, 4)
        x = jax.random.normal(k_x, (4, 512, DIM), dtype=jnp.float32)
        w_gate = jax.random.randint(k_g, (HIDDEN, DIM), -127, 128, dtype=jnp.int32)
        w_up = jax.random.randint(k_u, (HIDDEN, DIM), -127, 128, dtype=jnp.int32)
        w_down = jax.random.randint(k_d, (DIM, HIDDEN), -127, 128, dtype=jnp.int32)
        return {'x': x, 'w_gate': w_gate, 'w_up': w_up, 'w_down': w_down}
    _L2_ffn_all = _L2_ffn_setup()
    _L2_ffn_in = {k: v for k, v in _L2_ffn_all.items() if k in ('w_gate', 'w_up', 'w_down')}
    del _L2_ffn_all

    def _L3_attn_setup():
        import jax, jax.numpy as jnp
        import numpy as np
        import math
        D_MODEL = 256
        NUM_HEADS = 16
        HEAD_DIM = D_MODEL // NUM_HEADS
        B, S = (2, 512)

        def _causal_attn(q, k, v):
            scale = 1.0 / math.sqrt(q.shape[-1])
            scores = jnp.einsum('bthd,bshd->bhts', q, k) * scale
            t = q.shape[1]
            mask = jnp.tril(jnp.ones((t, t), dtype=bool))
            scores = jnp.where(mask, scores, -jnp.inf)
            attn = jax.nn.softmax(scores, axis=-1)
            return jnp.einsum('bhts,bshd->bthd', attn, v)
        key = jax.random.key(seed)
        ks = jax.random.split(key, 7)
        sc = 0.02
        return {'x': jax.random.normal(ks[0], (B, S, D_MODEL), dtype=jnp.float32), 'Wqkv_w': jax.random.normal(ks[1], (3 * D_MODEL, D_MODEL), dtype=jnp.float32) * sc, 'Wqkv_b': jnp.zeros((3 * D_MODEL,), dtype=jnp.float32), 'conv_w': jax.random.normal(ks[2], (D_MODEL, D_MODEL, 3), dtype=jnp.float32) * sc, 'conv_b': jnp.zeros((D_MODEL,), dtype=jnp.float32), 'out_w': jax.random.normal(ks[3], (D_MODEL, D_MODEL), dtype=jnp.float32) * sc, 'out_b': jnp.zeros((D_MODEL,), dtype=jnp.float32)}
    _L3_attn_all = _L3_attn_setup()
    _L3_attn_in = {k: v for k, v in _L3_attn_all.items() if k in ('Wqkv_w', 'Wqkv_b', 'conv_w', 'conv_b', 'out_w', 'out_b')}
    del _L3_attn_all

    def _L3_ffn_setup():
        import jax, jax.numpy as jnp
        import numpy as np
        E, G, TOPK = (32, 16, 2)
        HID, INTER, A_INTER = (256, 512, 128)
        CAP_FACTOR = 1.25
        SCALE = 0.05

        def _stats(x):
            mean = x.mean(-1, keepdims=True)
            std = jnp.std(x, axis=-1, keepdims=True, ddof=1)
            mn = x.min(-1, keepdims=True)
            mx = x.max(-1, keepdims=True)
            l2 = jnp.linalg.norm(x, axis=-1, keepdims=True)
            sp = (jnp.abs(x) < 1e-06).astype(x.dtype).mean(-1, keepdims=True)
            return jnp.concatenate([mean, std, mn, mx, l2, sp], -1)
        key = jax.random.key(seed)
        ks = jax.random.split(key, 8)
        B, N = (4, 256)
        s = lambda k, shape, sc: jax.random.normal(k, shape, jnp.float32) * sc
        return {'x': jax.random.normal(ks[0], (B, N, HID), jnp.float32), 'r1_w': s(ks[1], (HID // 2, HID + 6), 0.02), 'r1_b': jnp.zeros((HID // 2,), jnp.float32), 'r2_w': s(ks[2], (E, HID // 2), 0.02), 'w_up': s(ks[3], (E, 2 * INTER, HID), 0.02), 'w_down': s(ks[4], (E, HID, INTER), 0.02), 'a_up': s(ks[5], (G, 2 * A_INTER, HID), 0.02), 'a_down': s(ks[6], (G, HID, A_INTER), 0.02)}
    _L3_ffn_all = _L3_ffn_setup()
    _L3_ffn_in = {k: v for k, v in _L3_ffn_all.items() if k in ('r1_w', 'r1_b', 'r2_w', 'w_up', 'w_down', 'a_up', 'a_down')}
    del _L3_ffn_all
    return {'x': x, 'L0_tok_W': _L0_tok_in['W'], 'L0_tok_b': _L0_tok_in['b'], 'L0_tok_cls_token': _L0_tok_in['cls_token'], 'L0_tok_pos_embedding': _L0_tok_in['pos_embedding'], 'L0_attn_Wq': _L0_attn_in['Wq'], 'L0_attn_Wk': _L0_attn_in['Wk'], 'L0_attn_Wv': _L0_attn_in['Wv'], 'L0_attn_Wout': _L0_attn_in['Wout'], 'L0_attn_bout': _L0_attn_in['bout'], 'L0_ffn_Wr': _L0_ffn_in['Wr'], 'L0_ffn_Wg': _L0_ffn_in['Wg'], 'L0_ffn_Wu': _L0_ffn_in['Wu'], 'L0_ffn_Wd': _L0_ffn_in['Wd'], 'L1_attn_splat_positions': _L1_attn_in['splat_positions'], 'L1_attn_splat_log_scales': _L1_attn_in['splat_log_scales'], 'L1_attn_splat_amplitudes': _L1_attn_in['splat_amplitudes'], 'L1_attn_Wv': _L1_attn_in['Wv'], 'L1_attn_Wo': _L1_attn_in['Wo'], 'L1_ffn_w_gate': _L1_ffn_in['w_gate'], 'L1_ffn_w1_e': _L1_ffn_in['w1_e'], 'L1_ffn_w3_e': _L1_ffn_in['w3_e'], 'L1_ffn_w2_e': _L1_ffn_in['w2_e'], 'L1_ffn_w1_s': _L1_ffn_in['w1_s'], 'L1_ffn_w3_s': _L1_ffn_in['w3_s'], 'L1_ffn_w2_s': _L1_ffn_in['w2_s'], 'L2_attn_Wq': _L2_attn_in['Wq'], 'L2_attn_Wk': _L2_attn_in['Wk'], 'L2_attn_Wv': _L2_attn_in['Wv'], 'L2_attn_Wf1': _L2_attn_in['Wf1'], 'L2_attn_Wf2': _L2_attn_in['Wf2'], 'L2_attn_Wg1': _L2_attn_in['Wg1'], 'L2_attn_Wg2': _L2_attn_in['Wg2'], 'L2_attn_Wo': _L2_attn_in['Wo'], 'L2_attn_norm_w': _L2_attn_in['norm_w'], 'L2_ffn_w_gate': _L2_ffn_in['w_gate'], 'L2_ffn_w_up': _L2_ffn_in['w_up'], 'L2_ffn_w_down': _L2_ffn_in['w_down'], 'L3_attn_Wqkv_w': _L3_attn_in['Wqkv_w'], 'L3_attn_Wqkv_b': _L3_attn_in['Wqkv_b'], 'L3_attn_conv_w': _L3_attn_in['conv_w'], 'L3_attn_conv_b': _L3_attn_in['conv_b'], 'L3_attn_out_w': _L3_attn_in['out_w'], 'L3_attn_out_b': _L3_attn_in['out_b'], 'L3_ffn_r1_w': _L3_ffn_in['r1_w'], 'L3_ffn_r1_b': _L3_ffn_in['r1_b'], 'L3_ffn_r2_w': _L3_ffn_in['r2_w'], 'L3_ffn_w_up': _L3_ffn_in['w_up'], 'L3_ffn_w_down': _L3_ffn_in['w_down'], 'L3_ffn_a_up': _L3_ffn_in['a_up'], 'L3_ffn_a_down': _L3_ffn_in['a_down']}

def reference(x, L0_tok_W, L0_tok_b, L0_tok_cls_token, L0_tok_pos_embedding, L0_attn_Wq, L0_attn_Wk, L0_attn_Wv, L0_attn_Wout, L0_attn_bout, L0_ffn_Wr, L0_ffn_Wg, L0_ffn_Wu, L0_ffn_Wd, L1_attn_splat_positions, L1_attn_splat_log_scales, L1_attn_splat_amplitudes, L1_attn_Wv, L1_attn_Wo, L1_ffn_w_gate, L1_ffn_w1_e, L1_ffn_w3_e, L1_ffn_w2_e, L1_ffn_w1_s, L1_ffn_w3_s, L1_ffn_w2_s, L2_attn_Wq, L2_attn_Wk, L2_attn_Wv, L2_attn_Wf1, L2_attn_Wf2, L2_attn_Wg1, L2_attn_Wg2, L2_attn_Wo, L2_attn_norm_w, L2_ffn_w_gate, L2_ffn_w_up, L2_ffn_w_down, L3_attn_Wqkv_w, L3_attn_Wqkv_b, L3_attn_conv_w, L3_attn_conv_b, L3_attn_out_w, L3_attn_out_b, L3_ffn_r1_w, L3_ffn_r1_b, L3_ffn_r2_w, L3_ffn_w_up, L3_ffn_w_down, L3_ffn_a_up, L3_ffn_a_down):
    import jax
    import jax.numpy as jnp

    def _L0_tok_ref(x, W, b, cls_token, pos_embedding):
        import jax, jax.numpy as jnp
        import numpy as np
        B, C, H, Wd = (64, 3, 96, 96)
        PH, PW, D = (16, 16, 256)
        PATCH_DIM = C * PH * PW
        N_TOK = H // PH * (Wd // PW)
        Bc = x.shape[0]
        nh, nw = (H // PH, Wd // PW)
        patches = x.reshape(Bc, C, nh, PH, nw, PW)
        patches = patches.transpose(0, 2, 4, 1, 3, 5).reshape(Bc, nh * nw, PATCH_DIM)
        tokens = jnp.einsum('bnp,dp->bnd', patches, W) + b
        cls = jnp.broadcast_to(cls_token, (Bc, 1, D))
        tokens = jnp.concatenate([cls, tokens], axis=1)
        return tokens + pos_embedding

    def _L0_attn_ref(x, Wq, Wk, Wv, Wout, bout):
        import jax, jax.numpy as jnp
        import numpy as np
        HEADS = 16
        b, n, c = x.shape
        m = HEADS
        d = Wq.shape[0] // m
        q = jnp.einsum('bnc,hc->bnh', x, Wq).reshape(b, n, m, d)
        k = jnp.einsum('bnc,hc->bnh', x, Wk).reshape(b, n, m, d)
        v = jnp.einsum('bnc,hc->bnh', x, Wv).reshape(b, n, m, d)
        scale = d ** (-0.25)
        weight = jnp.einsum('bimd,bjmd->bmij', q * scale, k * scale)
        weight = jax.nn.softmax(weight, axis=-1)
        a = jnp.einsum('bmij,bjmd->bimd', weight, v).reshape(b, n, m * d)
        return jnp.einsum('bnh,ch->bnc', a, Wout) + bout

    def _L0_ffn_ref(x, Wr, Wg, Wu, Wd):
        import jax, jax.numpy as jnp
        import numpy as np
        D_MODEL = 256
        HIDDEN = 512
        N_EXPERTS = 8
        TOP_K = 2
        bsz, seq_len, d_model = x.shape
        flat = x.reshape(-1, d_model)
        logits = flat @ Wr
        topk_vals, topk_idx = jax.lax.top_k(logits, TOP_K)
        topk_w = jax.nn.softmax(topk_vals, axis=-1)
        combine = jnp.sum(jax.nn.one_hot(topk_idx, N_EXPERTS, dtype=flat.dtype) * topk_w[..., None], axis=1)
        out = jnp.zeros_like(flat)
        for e in range(N_EXPERTS):
            g = flat @ Wg[e]
            u = flat @ Wu[e]
            y = jax.nn.silu(g) * u @ Wd[e]
            out = out + y * combine[:, e:e + 1]
        return out.reshape(bsz, seq_len, d_model)

    def _L1_attn_ref(token_embeddings, splat_positions, splat_log_scales, splat_amplitudes, Wv, Wo):
        import jax, jax.numpy as jnp
        import numpy as np
        B, T, D, S = (4, 512, 256, 64)
        EPS = 1e-08
        x = token_embeddings
        p = splat_positions
        x2 = jnp.sum(x * x, axis=-1, keepdims=True)
        p2 = jnp.sum(p * p, axis=-1)
        xp = jnp.einsum('btd,sd->bts', x, p)
        d2 = jnp.maximum(x2 + p2[None, None, :] - 2.0 * xp, 0.0)
        scales = jnp.exp(splat_log_scales)
        gauss = splat_amplitudes * jnp.exp(-0.5 * d2 / (scales * scales))
        attn = jnp.einsum('bis,bjs->bij', gauss, gauss)
        attn = attn / (jnp.sum(attn, axis=-1, keepdims=True) + EPS)
        v = jnp.einsum('btd,de->bte', x, Wv)
        out = jnp.einsum('bij,bjd->bid', attn, v)
        return jnp.einsum('btd,de->bte', out, Wo)

    def _L1_ffn_ref(hidden_states, w_gate, w1_e, w3_e, w2_e, w1_s, w3_s, w2_s):
        import jax, jax.numpy as jnp
        import numpy as np
        B, S, H = (2, 256, 256)
        E, F = (16, 128)
        G, TOPK_G, TOPK = (4, 2, 4)
        N_SHARED = 2
        ROUTE_SCALE = 1.0
        FS = N_SHARED * F

        def _gate(x, w_gate):
            T = x.shape[0]
            scores = jax.nn.sigmoid(x @ w_gate.T)
            sv = scores.reshape(T, G, E // G)
            group_scores = jax.lax.top_k(sv, 2)[0].sum(-1)
            top_groups = jax.lax.top_k(group_scores, TOPK_G)[1]
            allowed = jnp.zeros((T, G), dtype=bool).at[jnp.arange(T)[:, None], top_groups].set(True)
            masked = jnp.where(allowed[:, :, None], sv, -jnp.inf).reshape(T, E)
            _, idx = jax.lax.top_k(masked, TOPK)
            w = jnp.take_along_axis(scores, idx, axis=1)
            w = w / (w.sum(-1, keepdims=True) + 1e-06) * ROUTE_SCALE
            return (w, idx)

        def _swiglu(x, w1, w3, w2):
            return jax.nn.silu(x @ w1.T) * (x @ w3.T) @ w2.T
        shape = hidden_states.shape
        x = hidden_states.reshape(-1, H)
        weights, idx = _gate(x, w_gate)
        combine = (jax.nn.one_hot(idx, E, dtype=x.dtype) * weights[..., None]).sum(1)
        g = jax.nn.silu(jnp.einsum('th,efh->tef', x, w1_e))
        u = jnp.einsum('th,efh->tef', x, w3_e)
        routed = jnp.einsum('tef,ehf,te->th', g * u, w2_e, combine)
        shared = _swiglu(x, w1_s, w3_s, w2_s)
        return (routed + shared).reshape(shape)

    def _L2_attn_ref(x, Wq, Wk, Wv, Wf1, Wf2, Wg1, Wg2, Wo, norm_w):
        import jax, jax.numpy as jnp
        import numpy as np
        B, N, D = (2, 512, 256)
        H, M = (8, 64)
        DK = D // H
        EPS = 1e-05

        def _gsa(q, k, v, s, g):
            b = q.shape[1]

            def step1(hk, t):
                q_t, k_t, s_t, g_t = t
                hk = hk * jnp.exp(g_t)[:, :, None, :] + k_t[..., :, None] * s_t[..., None, :]
                ok = jnp.einsum('bhk,bhkm->bhm', q_t, hk)
                return (hk, ok)
            hk0 = jnp.zeros((b, H, DK, M), q.dtype)
            _, ok = jax.lax.scan(step1, hk0, (q, k, s, g))
            qv = jax.nn.softmax(ok, axis=-1)

            def step2(hv, t):
                qv_t, s_t, v_t, g_t = t
                hv = hv * jnp.exp(g_t)[..., :, None] + s_t[..., :, None] * v_t[..., None, :]
                ov = jnp.einsum('bhm,bhmv->bhv', qv_t, hv)
                return (hv, ov)
            hv0 = jnp.zeros((b, H, M, DK), q.dtype)
            _, ov = jax.lax.scan(step2, hv0, (qv, s, v, g))
            return ov
        b, n, d = x.shape
        q = jax.nn.silu(x @ Wq).reshape(b, n, H, DK)
        k = jax.nn.silu(x @ Wk).reshape(b, n, H, DK)
        v = (x @ Wv).reshape(b, n, H, DK)
        f = x @ Wf1 @ Wf2
        log_f = jax.nn.log_sigmoid(f).reshape(b, n, H, M)
        s = 1.0 - jnp.exp(log_f)
        tm = lambda a: jnp.swapaxes(a, 0, 1)
        ov = _gsa(tm(q), tm(k), tm(v), tm(s), tm(log_f))
        out = tm(ov).reshape(b, n, d)
        gate = x @ Wg1 @ Wg2
        out = out * jax.nn.sigmoid(gate)
        og = out.reshape(b, n, H, DK)
        og = og * jax.lax.rsqrt(jnp.mean(og * og, axis=-1, keepdims=True) + EPS)
        out = og.reshape(b, n, d) * norm_w
        return out @ Wo

    def _L2_ffn_ref(x, w_gate, w_up, w_down):
        import jax, jax.numpy as jnp
        import numpy as np
        DIM = 256
        HIDDEN = 768
        SCALE = 1.0 / 127.0

        def _dequant(w_int, dtype):
            return w_int.astype(dtype) * jnp.asarray(SCALE, dtype)
        wg = _dequant(w_gate, x.dtype)
        wu = _dequant(w_up, x.dtype)
        wd = _dequant(w_down, x.dtype)
        gate = jnp.einsum('bsd,hd->bsh', x, wg)
        up = jnp.einsum('bsd,hd->bsh', x, wu)
        h = jax.nn.silu(gate) * up
        return jnp.einsum('bsh,dh->bsd', h, wd)

    def _L3_attn_ref(x, Wqkv_w, Wqkv_b, conv_w, conv_b, out_w, out_b):
        import jax, jax.numpy as jnp
        import numpy as np
        import math
        D_MODEL = 256
        NUM_HEADS = 16
        HEAD_DIM = D_MODEL // NUM_HEADS
        B, S = (2, 512)

        def _causal_attn(q, k, v):
            scale = 1.0 / math.sqrt(q.shape[-1])
            scores = jnp.einsum('bthd,bshd->bhts', q, k) * scale
            t = q.shape[1]
            mask = jnp.tril(jnp.ones((t, t), dtype=bool))
            scores = jnp.where(mask, scores, -jnp.inf)
            attn = jax.nn.softmax(scores, axis=-1)
            return jnp.einsum('bhts,bshd->bthd', attn, v)
        b, s, d = x.shape
        qkv = x @ Wqkv_w.T + Wqkv_b
        qkv = qkv.reshape(b, s, 3, NUM_HEADS, HEAD_DIM)
        q, k, v = (qkv[:, :, 0], qkv[:, :, 1], qkv[:, :, 2])
        ctx = _causal_attn(q, k, v)
        ctx_c = ctx.reshape(b, s, d).transpose(0, 2, 1)
        conv_out = jax.lax.conv_general_dilated(ctx_c, conv_w, window_strides=(1,), padding=[(1, 1)], dimension_numbers=('NCH', 'OIH', 'NCH')) + conv_b[None, :, None]
        q2 = conv_out.transpose(0, 2, 1).reshape(b, s, NUM_HEADS, HEAD_DIM)
        ctx2 = _causal_attn(q2, k, v)
        out = ctx2.reshape(b, s, d) @ out_w.T + out_b
        return out

    def _L3_ffn_ref(x, r1_w, r1_b, r2_w, w_up, w_down, a_up, a_down):
        import jax, jax.numpy as jnp
        import numpy as np
        E, G, TOPK = (32, 16, 2)
        HID, INTER, A_INTER = (256, 512, 128)
        CAP_FACTOR = 1.25
        SCALE = 0.05

        def _stats(x):
            mean = x.mean(-1, keepdims=True)
            std = jnp.std(x, axis=-1, keepdims=True, ddof=1)
            mn = x.min(-1, keepdims=True)
            mx = x.max(-1, keepdims=True)
            l2 = jnp.linalg.norm(x, axis=-1, keepdims=True)
            sp = (jnp.abs(x) < 1e-06).astype(x.dtype).mean(-1, keepdims=True)
            return jnp.concatenate([mean, std, mn, mx, l2, sp], -1)
        B, N, C = x.shape
        xf = x.reshape(-1, C)
        T = xf.shape[0]
        cap = int(CAP_FACTOR * T / E)
        ri = jnp.concatenate([xf, _stats(xf)], -1)
        h = jax.nn.gelu(ri @ r1_w.T + r1_b, approximate=False)
        probs = jax.nn.softmax(h @ r2_w.T, -1)
        topp, topi = jax.lax.top_k(probs, TOPK)
        wnorm = topp / topp.sum(-1, keepdims=True)
        eids = jnp.arange(E)
        hit = topi[..., None] == eids
        routed = hit.any(1)
        Wc = jnp.where(hit, wnorm[..., None], 0.0).sum(1)
        score = jnp.where(routed, probs, -jnp.inf)
        idx = jnp.argsort(-score, axis=0)[:cap].T
        valid = jnp.take_along_axis(routed.T, idx, 1)
        w = jnp.take_along_axis(Wc.T, idx, 1) * valid
        xe = xf[idx]
        up = jnp.einsum('eci,eji->ecj', xe, w_up)
        gate, upv = jnp.split(up, 2, axis=-1)
        hact = jax.nn.silu(gate) * upv
        ye = jnp.einsum('ecj,eoj->eco', hact, w_down)
        out = jnp.zeros((T, C), xf.dtype).at[idx.reshape(-1)].add((w[..., None] * ye).reshape(-1, C))
        Wmask = jnp.zeros((T, E), xf.dtype).at[idx, eids[:, None]].add(w)
        gw = SCALE * Wmask.reshape(T, G, E // G).sum(-1)
        aup = jnp.einsum('tc,gjc->tgj', xf, a_up)
        ag, av = jnp.split(aup, 2, axis=-1)
        ah = jax.nn.silu(ag) * av
        ay = jnp.einsum('tgj,goj->tgo', ah, a_down)
        out = out + jnp.einsum('tg,tgo->to', gw, ay)
        return out.reshape(B, N, C)
    h = _L0_tok_ref(x, L0_tok_W, L0_tok_b, L0_tok_cls_token, L0_tok_pos_embedding)
    h = _layernorm(h + _L0_attn_ref(h, L0_attn_Wq, L0_attn_Wk, L0_attn_Wv, L0_attn_Wout, L0_attn_bout), axis=-1)
    h = _layernorm(h + _L0_ffn_ref(h, L0_ffn_Wr, L0_ffn_Wg, L0_ffn_Wu, L0_ffn_Wd), axis=-1)
    h = _layernorm(h + _L1_attn_ref(h, L1_attn_splat_positions, L1_attn_splat_log_scales, L1_attn_splat_amplitudes, L1_attn_Wv, L1_attn_Wo), axis=-1)
    h = _layernorm(h + _L1_ffn_ref(h, L1_ffn_w_gate, L1_ffn_w1_e, L1_ffn_w3_e, L1_ffn_w2_e, L1_ffn_w1_s, L1_ffn_w3_s, L1_ffn_w2_s), axis=-1)
    h = _layernorm(h + _L2_attn_ref(h, L2_attn_Wq, L2_attn_Wk, L2_attn_Wv, L2_attn_Wf1, L2_attn_Wf2, L2_attn_Wg1, L2_attn_Wg2, L2_attn_Wo, L2_attn_norm_w), axis=-1)
    h = _layernorm(h + _L2_ffn_ref(h, L2_ffn_w_gate, L2_ffn_w_up, L2_ffn_w_down), axis=-1)
    h = _layernorm(h + _L3_attn_ref(h, L3_attn_Wqkv_w, L3_attn_Wqkv_b, L3_attn_conv_w, L3_attn_conv_b, L3_attn_out_w, L3_attn_out_b), axis=-1)
    h = _layernorm(h + _L3_ffn_ref(h, L3_ffn_r1_w, L3_ffn_r1_b, L3_ffn_r2_w, L3_ffn_w_up, L3_ffn_w_down, L3_ffn_a_up, L3_ffn_a_down), axis=-1)
    return h

_drawn_inputs = setup_inputs


def setup_inputs(seed=0):
    import zlib

    import numpy as np

    out = dict(_drawn_inputs(seed))
    spreads = {'L0_attn_bout': (0.0, 0.1),
     'L2_attn_norm_w': (1.0, 0.2),
     'L3_attn_Wqkv_b': (0.0, 0.1),
     'L3_attn_conv_b': (0.0, 0.8),
     'L3_attn_out_b': (0.0, 0.1),
     'L3_ffn_r1_b': (0.0, 0.8)}
    factors = {'L0_attn_Wq': 8.0,
     'L0_attn_Wk': 8.0,
     'L1_ffn_w_gate': 7.583,
     'L1_ffn_w1_e': 6.607,
     'L1_ffn_w3_e': 6.587,
     'L1_ffn_w2_e': 6.534,
     'L2_attn_Wq': 8.0,
     'L2_attn_Wk': 8.0,
     'L2_attn_Wf1': 8.0,
     'L2_attn_Wf2': 8.0,
     'L2_attn_Wg1': 7.312,
     'L2_attn_Wg2': 7.47,
     'L3_attn_conv_w': 8.0,
     'L3_ffn_r1_w': 5.97,
     'L3_ffn_r2_w': 5.978,
     'L3_ffn_w_up': 5.766,
     'L3_ffn_w_down': 5.77,
     'L3_ffn_a_up': 8.0,
     'L3_ffn_a_down': 8.0}
    for name, (base, spread) in spreads.items():
        noise = np.random.default_rng([zlib.crc32(name.encode()), seed]).standard_normal(out[name].shape)
        drawn = base * np.exp(spread * noise) if base else spread * noise
        out[name] = jnp.asarray(drawn.astype(out[name].dtype))
    for name, factor in factors.items():
        out[name] = (out[name] * factor).astype(out[name].dtype)
    return out
```

```python
from contextlib import ExitStack

import numpy as np

import concourse.bass as bass
from concourse import mybir

F32 = mybir.dt.float32
I32 = mybir.dt.int32
U32 = mybir.dt.uint32
ALU = mybir.AluOpType
ACT = mybir.ActivationFunctionType
AX = mybir.AxisListType.X

LAYERS = 8
P = 128
B = 32
T = 37
SP = 64
D = 256
KD = D // P
NG = 4
GI = B // NG
GN = GI * T
NT = B * T
NP = B // 2
HEADS = 16
HD = 16
CP = T + 2
UNIT = 6 * P
RING = 4 * UNIT
AR = 19600
LEVELS = 6
LN_EPS = 1e-5

FFNS = {"L0": (8, 4), "L1": (18, 1), "L3": (16, 1)}

CONST = {}


def build_constants():
    parts = {}
    r = np.arange(P)
    t = r % SP
    img = r // SP
    valid = t < T
    parts["ident"] = np.eye(P)
    parts["ones"] = np.ones((P, P))
    parts["mean"] = np.full((P, P), 1.0 / D)
    parts["blk"] = (img[:, None] == img[None, :]) & valid[None, :]
    parts["i2"] = t[:, None] == np.arange(T)[None, :]
    parts["negi"] = np.where(np.arange(T)[None, :] <= t[:, None], 0.0, -1e30)
    parts["negj"] = np.where(np.arange(T)[None, :] >= t[:, None], 0.0, -1e30)
    masks, sums = [], []
    for lv in range(LEVELS):
        b = 2 ** (LEVELS - 1 - lv)
        c = (t // (2 * b)) * 2 * b + b
        tt = np.arange(T)
        masks.append((t[:, None] // (2 * b) == tt[None, :] // (2 * b)) & (t < c)[:, None] & (tt[None, :] >= c[:, None]))
        u = t[:, None]
        x, cx = t[None, :], c[None, :]
        same = img[:, None] == img[None, :]
        sums.append(same & valid[:, None] & np.where(x >= cx, (u >= cx) & (u <= x), (u > x) & (u < cx)))
    masks.append(t[:, None] == np.arange(T)[None, :])
    parts["lmask"] = np.concatenate(masks, 1)
    parts["lsum"] = np.concatenate(sums, 1)
    cols = np.concatenate([i * SP + np.arange(T) for i in range(2)])
    parts["lsumc"] = np.concatenate([s[:, cols] for s in sums], 1)
    parts["iota"] = np.broadcast_to(np.arange(46), (P, 46))
    parts["slotno"] = (r % SP)[:, None]
    two = np.zeros((P, 16))
    two[np.arange(32), np.arange(32) // 2] = 1.0
    parts["two"] = two
    parts["tril4"] = np.broadcast_to((np.arange(4)[None, :] < np.arange(4)[:, None]).reshape(1, 16), (P, 16))
    at = 0
    out = []
    for name, a in parts.items():
        a = np.asarray(a, np.float32)
        CONST[name] = (at, a.shape[1])
        at += a.shape[1]
        out.append(a)
    return np.ascontiguousarray(np.concatenate(out, 1))


CONSTS = build_constants()
PAIRS = np.repeat(np.eye(32, dtype=np.float32), SP, axis=1)


def bcast(ap, at, n):
    dims = list(ap.ap)
    return bass.AP(ap.tensor, ap.offset, dims[:at + 1] + [[0, n]] + dims[at + 1:])


def tower(nc, inp, out, scratch):
    ctx = ExitStack()
    with ctx:
        def sb(name, shape, dt=F32):
            return ctx.enter_context(nc.sbuf_tensor(name, shape, dt))

        def sem(name):
            return ctx.enter_context(nc.semaphore(name))

        hP = sb("hP", [P, KD, B, SP])
        acc = sb("acc", [P, KD, NT])
        xc = sb("xc", [P, KD, NT])
        rs = sb("rs", [P, NT])
        aT = sb("aT", [P, KD, B, CP])
        ring = sb("ring", [P, 2, RING])
        cst = sb("cst", [P, CONSTS.shape[1]])
        wA = sb("wA", [P, 6656])
        arena = sb("arena", [P, AR])
        zcol = sb("zcol", [P, 1])
        epscol = sb("epscol", [P, 1])
        PS = ctx.enter_context(nc.psum_tensor("PS", [P, 8, 512], F32))

        def const(name):
            at, n = CONST[name]
            return cst[:, at:at + n]

        ident = const("ident")

        class carve:
            def __init__(self, tile, size):
                self.tile, self.size, self.at = tile, size, 0

            def __call__(self, n):
                self.at += n
                assert self.at <= self.size, (self.at, self.size)
                return self.tile[:, self.at - n:self.at]

        def hgroup(k, g):
            return hP[:, k, g * GI:(g + 1) * GI, 0:T]

        def hpair(k, p):
            return hP[:, k, 2 * p:2 * p + 2, :].rearrange("q a t -> q (a t)")

        def agroup(k, g):
            return aT[:, k, g * GI:(g + 1) * GI, 1:T + 1]

        def compact(ap):
            return ap.rearrange("q (a t) -> q a t", t=T)

        cst_loaded = sem("cst_loaded")
        wA_loaded = sem("wA_loaded")
        pads_zeroed = sem("pads_zeroed")
        dve_step = sem("dve_step")
        act_step = sem("act_step")
        res_ready = sem("res_ready")
        mean_ready = sem("mean_ready")
        xc_ready = sem("xc_ready")
        sq_ready = sem("sq_ready")
        var_ready = sem("var_ready")
        rstd_ready = sem("rstd_ready")
        h_ready = sem("h_ready")
        all_stored = sem("all_stored")

        block = ctx.enter_context(nc.Block())
        steps = {"dve": 0, "act": 0}

        def dve_then(ins):
            steps["dve"] += 1
            ins.then_inc(dve_step, 1)
            nc.vector.wait_ge(dve_step, steps["dve"])

        def act_then(ins):
            steps["act"] += 1
            ins.then_inc(act_step, 1)
            nc.scalar.wait_ge(act_step, steps["act"])

        def block_before(eng, n):
            eng.wait_ge(h_ready, NG * (n + 1))

        def ln_pe(layer):
            pe = nc.tensor
            if layer % 2:
                pe.wait_ge(ffn_acc, FFN_END[layer])
            else:
                pe.wait_ge(res_ready, NG * (layer // 2 + 1))
            for g in range(NG):
                for k in range(KD):
                    mm = pe.matmul(PS[:, g, 0:GN], const("mean"), acc[:, k, g * GN:(g + 1) * GN],
                                   start=(k == 0), stop=(k == KD - 1))
                mm.then_inc(mean_ready, 1)
            for g in range(NG):
                pe.wait_ge(sq_ready, NG * layer + g + 1)
                for k in range(KD):
                    mm = pe.matmul(PS[:, NG + g, 0:GN], const("mean"), acc[:, k, g * GN:(g + 1) * GN],
                                   start=(k == 0), stop=(k == KD - 1))
                mm.then_inc(var_ready, 1)

        def ln_dve(layer):
            v = nc.vector
            for g in range(NG):
                n = NG * layer + g + 1
                sl = slice(g * GN, (g + 1) * GN)
                v.wait_ge(mean_ready, n)
                v.tensor_tensor(xc[:, :, sl], acc[:, :, sl], bcast(PS[:, g, 0:GN], 0, KD),
                                ALU.subtract).then_inc(xc_ready, 1)
            for g in range(NG):
                n = NG * layer + g + 1
                sl = slice(g * GN, (g + 1) * GN)
                v.wait_ge(xc_ready, n)
                v.wait_ge(rstd_ready, n)
                for k in range(KD):
                    ins = v.tensor_tensor(hgroup(k, g), compact(xc[:, k, sl]), compact(rs[:, sl]), ALU.mult)
                ins.then_inc(h_ready, 1)

        def ln_act(layer):
            a = nc.scalar
            for g in range(NG):
                n = NG * layer + g + 1
                sl = slice(g * GN, (g + 1) * GN)
                a.wait_ge(xc_ready, n)
                a.activation(acc[:, :, sl], xc[:, :, sl], ACT.Square).then_inc(sq_ready, 1)
            for g in range(NG):
                n = NG * layer + g + 1
                sl = slice(g * GN, (g + 1) * GN)
                a.wait_ge(var_ready, n)
                ins = a.activation(rs[:, sl], PS[:, NG + g, 0:GN], ACT.Ln, bias=epscol[:, 0:1])
            act_then(ins)
            for g in range(NG):
                sl = slice(g * GN, (g + 1) * GN)
                a.activation(rs[:, sl], rs[:, sl], ACT.Exp, scale=-0.5).then_inc(rstd_ready, 1)

        def start_sync():
            nc.sync.dma_start(cst[:, :], inp["consts"]).then_inc(cst_loaded, 16)

        def start_pool():
            pool = nc.gpsimd
            pool.memset(hP[:, :, :, :], 0.0).then_inc(pads_zeroed, 1)
            pool.memset(aT[:, :, :, :], 0.0).then_inc(pads_zeroed, 1)
            pool.memset(zcol[:, :], 0.0).then_inc(pads_zeroed, 1)
            pool.memset(epscol[:, :], LN_EPS).then_inc(pads_zeroed, 1)

        def start_engine(eng):
            eng.wait_ge(cst_loaded, 16)
            eng.wait_ge(pads_zeroed, 4)

        GT = GI * (T - 1)
        tw = carve(wA, 6656)
        tok_w = tw(6 * D).rearrange("q (k n) -> q k n", k=6)
        tok_side = tw(2 * (T + 2)).rearrange("q (k n) -> q k n", k=2)
        tok_pos = arena[:, 4 * 6 * GT:4 * 6 * GT + 2 * T].rearrange("q (k n) -> q k n", k=2)
        tok_x = arena[:, 0:4 * 6 * GT].rearrange("q (g k n) -> q g k n", g=4, k=6)
        x_loaded = [sem(f"x_loaded{g}") for g in range(NG)]
        tok_ready = sem("tok_ready")

        def tok_sync():
            sp = nc.sync
            sp.dma_start(wA[:, 0:6 * D + 2 * (T + 2)], inp["tok_w"]).then_inc(wA_loaded, 16)
            for g in range(NG):
                sp.dma_start(tok_x[:, g].rearrange("q k n -> q (k n)"), inp["patches"][g]).then_inc(x_loaded[g], 16)

        def tok_pe():
            pe = nc.tensor
            pe.wait_ge(wA_loaded, 16)
            for g in range(NG):
                pe.wait_ge(x_loaded[g], 16)
                for c in range(KD):
                    for k in range(6):
                        mm = pe.matmul(PS[:, 2 * g + c, 0:GT], tok_w[:, k, c * P:(c + 1) * P], tok_x[:, g, k, :],
                                       start=(k == 0), stop=(k == 5))
                mm.then_inc(tok_ready, 1)

        def tok_dve():
            v = nc.vector
            v.wait_ge(wA_loaded, 16)
            for c in range(KD):
                v.tensor_scalar(tok_pos[:, c, 1:T], tok_side[:, c, 1:T], tok_side[:, c, T:T + 1], None, ALU.add)
                dve_then(v.tensor_scalar(tok_pos[:, c, 0:1], tok_side[:, c, 0:1], tok_side[:, c, T + 1:T + 2], None,
                                         ALU.add))
            for g in range(NG):
                v.wait_ge(tok_ready, g + 1)
                for c in range(KD):
                    hg = hP[:, c, g * GI:(g + 1) * GI, :]
                    v.tensor_copy(hg[:, :, 0:1], bcast(tok_pos[:, c, 0:1], 0, GI))
                    ins = v.tensor_tensor(hg[:, :, 1:T], PS[:, 2 * g + c, 0:GT].rearrange("q (a t) -> q a t", a=GI),
                                          bcast(tok_pos[:, c, 1:T], 0, GI), ALU.add)
                ins.then_inc(h_ready, 1)

        proj_ready = sem("proj_ready")
        proj_count = {"n": 0}

        def project_pe(w, ready):
            pe = nc.tensor
            ready(pe)
            for g in range(NG):
                for c in range(KD):
                    for k in range(KD):
                        mm = pe.matmul(PS[:, 2 * g + c, 0:GN], w[:, k, c * P:(c + 1) * P], agroup(k, g),
                                       start=(k == 0), stop=(k == KD - 1))
                mm.then_inc(proj_ready, 1)

        def project_dve(bias):
            v = nc.vector
            for g in range(NG):
                proj_count["n"] += 1
                v.wait_ge(proj_ready, proj_count["n"])
                for c in range(KD):
                    ins = v.scalar_tensor_tensor(out=compact(acc[:, c, g * GN:(g + 1) * GN]),
                                                 in0=compact(PS[:, 2 * g + c, 0:GN]), scalar=bias[c],
                                                 in1=hgroup(c, g), op0=ALU.add, op1=ALU.add)
                ins.then_inc(res_ready, 1)

        ma = carve(arena, AR)
        q_s = ma(4 * NT).rearrange("q (c n) -> q c n", c=4)
        k_s = ma(4 * NT).rearrange("q (c n) -> q c n", c=4)
        v_s = ma(NP * HEADS * 17).rearrange("q (p h d) -> q p h d", p=NP, h=HEADS)
        pt_s = ma(2 * 592).rearrange("q (s r n) -> q s r n", s=2, r=4)
        dg_s = ma(2 * 592).rearrange("q (s r n) -> q s r n", s=2, r=4)
        sm_s = ma(592).rearrange("q (r n) -> q r n", r=4)
        st_s = ma(2 * 592).rearrange("q (s r n) -> q s r n", s=2, r=4)
        o_s = ma(2 * D).rearrange("q (s n) -> q s n", s=2)
        mx2_s = ma(32).rearrange("q (s h) -> q s h", s=2)
        rec_s = ma(16)
        qk_evac = sem("qk_evac")
        qk_ready = sem("qk_ready")
        v_ready = sem("v_ready")
        v_evac = sem("v_evac")
        ones_set = sem("ones_set")
        psum_set = sem("psum_set")
        s_ready = sem("s_ready")
        s_read = sem("s_read")
        dg_ready = sem("dg_ready")
        st_ready = sem("st_ready")
        st_masked = sem("st_masked")
        pt_ready = sem("pt_ready")
        o_ready = sem("o_ready")
        on_ready = sem("on_ready")
        ot_ready = sem("ot_ready")
        aT_ready = sem("aT_ready")
        NQK = 8 * NG
        row_tile_done = sem("row_tile_done")
        tile_count = {"n": 0}

        def heads_pe(m, wq, wk, wv):
            pe = nc.tensor
            n = 0
            for g in range(NG):
                for w in (wq, wk):
                    for c in range(4):
                        if n >= 4:
                            pe.wait_ge(qk_evac, m * NQK + n - 3)
                        for k in range(KD):
                            mm = pe.matmul(PS[:, n % 4, 0:GN], w[:, k, c * P:(c + 1) * P], hgroup(k, g),
                                           start=(k == 0), stop=(k == KD - 1))
                        mm.then_inc(qk_ready, 1)
                        n += 1
                for p in range(4 * g, 4 * g + 4):
                    if p >= 4:
                        pe.wait_ge(v_evac, m * NP + p - 3)
                    for k in range(KD):
                        mm = pe.matmul(PS[:, 4 + p % 4, 0:D], hpair(k, p), wv[:, k, :],
                                       start=(k == 0), stop=(k == KD - 1))
                    mm.then_inc(v_ready, 1)

        def heads_act(m, qbias, kbias):
            a = nc.scalar
            n = 0
            for g in range(NG):
                for dst, bias, scale in ((q_s, qbias, 0.25), (k_s, kbias, 1.0)):
                    for c in range(4):
                        a.wait_ge(qk_ready, m * NQK + n + 1)
                        a.activation(dst[:, c, g * GN:(g + 1) * GN], PS[:, n % 4, 0:GN], ACT.Identity,
                                     bias=bias[c], scale=scale).then_inc(qk_evac, 1)
                        n += 1

        def heads_dve(m, vbias):
            v = nc.vector
            v.memset(v_s[:, :, :, 16:17], 1.0).then_inc(ones_set, 1)
            for p in range(NP):
                v.wait_ge(v_ready, m * NP + p + 1)
                src = PS[:, 4 + p % 4, 0:D].rearrange("q (h d) -> q h d", h=HEADS)
                if vbias is None:
                    ins = v.tensor_copy(v_s[:, p, :, 0:16], src)
                else:
                    ins = v.tensor_tensor(v_s[:, p, :, 0:16], src, vbias.rearrange("q (h d) -> q h d", h=HEADS),
                                          ALU.add)
                ins.then_inc(v_evac, 1)

        def head(ap, h, img):
            return ap[32 * (h % 4):32 * (h % 4) + HD, h // 4, img * T:(img + 1) * T]

        def attend_pe(a, m):
            pe = nc.tensor
            pe.wait_ge(qk_evac, NQK * (m + 1) + (16 if a == 2 else 0))
            pe.wait_ge(v_evac, NP * (m + 1))
            pe.wait_ge(psum_set, a + 1)

            def head_products(p, bank, left, right, fresh):
                for r in (0, 2, 1, 3):
                    if r % 2:
                        pe.wait_ge(row_tile_done, tile_count["n"] - 1)
                    for i in range(2):
                        for c in range(4):
                            at = (r % 2) * 148 + c * T
                            mm = pe.matmul(PS[i * SP:i * SP + T, bank + r // 2, at:at + T],
                                           head(left, 4 * c + r, 2 * p + i), head(right, 4 * c + r, 2 * p + i),
                                           start=fresh, stop=True, skip_group_check=True)
                    if r % 2 == 0:
                        mm.then_inc(row_tile_done, 1)
                        tile_count["n"] += 1
                    if r == 1:
                        mm.then_inc(row_tile_done, 1)
                        tile_count["n"] += 1
                return mm

            def scores(p):
                n = a * NP + p
                if p >= 2:
                    pe.wait_ge(s_read, n - 1)
                head_products(p, 2 * (p % 2), q_s, k_s, True).then_inc(s_ready, 1)

            def transposed(p):
                n = a * NP + p
                pe.wait_ge(dg_ready, n + 1)
                if p:
                    pe.wait_ge(st_masked if a else pt_ready, (n - NP if a else n))
                for c in range(2):
                    pe.matmul(PS[:, 4 + c, 0:8 * T], const("blk"),
                              dg_s[:, p % 2, 2 * c:2 * c + 2, :].rearrange("q r n -> q (r n)"),
                              start=True, stop=False, skip_group_check=True)
                head_products(p, 4, k_s, q_s, False).then_inc(st_ready, 1)

            def values(p):
                n = a * NP + p
                pe.wait_ge(pt_ready, n + 1)
                if p:
                    pe.wait_ge(on_ready, n)
                for i in range(2):
                    for h in range(HEADS):
                        rows = slice(i * SP, i * SP + T)
                        mm = pe.matmul(PS[rows, 6, h * 17:(h + 1) * 17],
                                       pt_s[rows, p % 2, h % 4, (h // 4) * T:(h // 4 + 1) * T], v_s[rows, p, h, :],
                                       start=True, stop=True)
                mm.then_inc(o_ready, 1)

            def turn(p):
                n = a * NP + p
                pe.wait_ge(on_ready, n + 1)
                if p:
                    pe.wait_ge(aT_ready, n)
                for c in range(KD):
                    mm = pe.transpose(PS[:, 7, c * P:(c + 1) * P], o_s[:, p % 2, c * P:(c + 1) * P], ident)
                mm.then_inc(ot_ready, 1)

            scores(0)
            for p in range(NP):
                if p + 1 < NP:
                    scores(p + 1)
                if p:
                    values(p - 1)
                transposed(p)
                if p:
                    turn(p - 1)
            values(NP - 1)
            turn(NP - 1)

        def attend_dve(a, m):
            v = nc.vector
            v.wait_ge(qk_evac, NQK * (m + 1) + (16 if a == 2 else 0))
            v.wait_ge(ones_set, m + 1)
            v.wait_ge(v_evac, NP * (m + 1))
            v.memset(PS[:, 0:4, :], 1.0)
            v.memset(PS[:, 6, :], 1.0).then_inc(psum_set, 1)
            v.wait_ge(psum_set, a + 1)
            ident2 = const("i2")

            def maxima(p):
                n = a * NP + p
                mx_s = mx2_s[:, p % 2]
                v.wait_ge(s_ready, n + 1)
                if n >= 2:
                    v.wait_ge(dg_ready, n - 1)
                src = PS[:, 2 * (p % 2):2 * (p % 2) + 2, 0:8 * T].rearrange("q b (h j) -> q b h j", h=8)
                if a:
                    v.tensor_tensor(sm_s.rearrange("q (b r) (c j) -> q b (r c) j", b=2, c=4), src,
                                    bcast(bcast(const("negi"), 0, 8), 0, 2), ALU.add).then_inc(s_read, 1)
                    v.wait_ge(s_read, n + 1)
                    dve_then(v.tensor_reduce(mx_s, sm_s.rearrange("q r (c j) -> q (r c) j", c=4), AX, ALU.max))
                else:
                    ins = v.tensor_reduce(mx_s.rearrange("q (b h) -> q b h", b=2), src, AX, ALU.max)
                    ins.then_inc(s_read, 1)
                    v.wait_ge(s_read, n + 1)
                if p >= 2:
                    v.wait_ge(st_ready, n - 1)
                mx = mx_s
                v.scalar_tensor_tensor(
                    out=dg_s[:, p % 2].rearrange("q r (c j) -> q (r c) j", c=4),
                    in0=bass.AP(mx.tensor, mx.offset, list(mx.ap) + [[0, T]]), scalar=-1.0,
                    in1=bcast(ident2, 0, HEADS), op0=ALU.mult, op1=ALU.mult).then_inc(dg_ready, 1)

            def mask(p):
                n = (a - 1) * NP + p
                v.wait_ge(st_ready, a * NP + p + 1)
                if p >= 2:
                    v.wait_ge(pt_ready, a * NP + p - 1)
                v.tensor_tensor(st_s[:, p % 2].rearrange("q (b r) (c j) -> q b (r c) j", b=2, c=4),
                                PS[:, 4:6, 0:8 * T].rearrange("q b (h j) -> q b h j", h=8),
                                bcast(bcast(const("negj"), 0, 8), 0, 2), ALU.add).then_inc(st_masked, 1)

            def normalize(p):
                n = a * NP + p
                v.wait_ge(o_ready, n + 1)
                if n:
                    v.wait_ge(on_ready, n)
                o = PS[:, 6, 0:HEADS * 17].rearrange("q (h d) -> q h d", h=HEADS)
                dve_then(v.reciprocal(rec_s, o[:, :, 16]))
                if p >= 2:
                    v.wait_ge(ot_ready, n - 1)
                v.tensor_tensor(o_s[:, p % 2].rearrange("q (h d) -> q h d", h=HEADS), o[:, :, 0:16],
                                bass.AP(rec_s.tensor, rec_s.offset, list(rec_s.ap) + [[0, 16]]),
                                ALU.mult).then_inc(on_ready, 1)

            maxima(0)
            for p in range(NP):
                if p + 1 < NP:
                    maxima(p + 1)
                if a:
                    mask(p)
                if p:
                    normalize(p - 1)
            normalize(NP - 1)

        def attend_act(a):
            s = nc.scalar

            def evacuate(p):
                s.wait_ge(ot_ready, a * NP + p + 1)
                src = PS[:, 7, 0:D].rearrange("q (c i t) -> q c i t", c=2, i=2)
                for c in range(KD):
                    ins = s.activation(aT[:, c, 2 * p:2 * p + 2, 1:T + 1], src[:, c, :, 0:T], ACT.Copy)
                ins.then_inc(aT_ready, 1)

            for p in range(NP):
                n = a * NP + p
                if a:
                    s.wait_ge(st_masked, n - NP + 1)
                    src = st_s[:, p % 2].rearrange("q (b r) n -> q b (r n)", b=2)
                else:
                    s.wait_ge(st_ready, n + 1)
                    src = PS[:, 4:6, 0:8 * T]
                if p >= 2:
                    s.wait_ge(o_ready, n - 1)
                dst = pt_s[:, p % 2].rearrange("q (b r) n -> q b (r n)", b=2)
                s.activation(dst, src, ACT.Exp).then_inc(pt_ready, 1)
                if p:
                    evacuate(p - 1)
            evacuate(NP - 1)

        w0 = carve(wA, 6656)
        a0_wq = w0(1024).rearrange("q (k n) -> q k n", k=2)
        a0_wk = w0(1024).rearrange("q (k n) -> q k n", k=2)
        a0_wv = w0(512).rearrange("q (k n) -> q k n", k=2)
        a0_wo = w0(512).rearrange("q (k n) -> q k n", k=2)
        a0_b = w0(2)

        def block0_loads():
            block_before(nc.sync, 0)
            nc.sync.dma_start(wA[:, 0:w0.at], inp["attn0"]).then_inc(wA_loaded, 16)

        def block0_pe():
            block_before(nc.tensor, 0)
            nc.tensor.wait_ge(wA_loaded, 32)
            heads_pe(0, a0_wq, a0_wk, a0_wv)
            attend_pe(0, 0)
            project_pe(a0_wo, lambda pe: pe.wait_ge(aT_ready, NP))
            ln_pe(0)

        def block0_act():
            block_before(nc.scalar, 0)
            heads_act(0, [zcol[:, 0:1]] * 4, [zcol[:, 0:1]] * 4)
            attend_act(0)
            ln_act(0)

        def block0_dve():
            block_before(nc.vector, 0)
            heads_dve(0, None)
            attend_dve(0, 0)
            project_dve([a0_b[:, c:c + 1] for c in range(KD)])
            ln_dve(0)

        fa = carve(arena, AR)
        hact = fa(2 * GN).rearrange("q (s n) -> q s n", s=2)
        sg = fa(2 * GN).rearrange("q (s n) -> q s n", s=2)
        tmp = fa(4 * GN).rearrange("q (s c n) -> q s c n", s=2, c=2)
        cb = fa(2 * NT).rearrange("q (s n) -> q s n", s=2)
        FA = fa.at
        ffn_up = sem("ffn_up")
        ffn_sg = sem("ffn_sg")
        ffn_hid = sem("ffn_hid")
        ffn_down = sem("ffn_down")
        ffn_out = sem("ffn_out")
        ffn_acc = sem("ffn_acc")
        ring_full = [sem(f"ring_full{i}") for i in range(2)]
        cb_full = [sem(f"cb_full{i}") for i in range(2)]
        acc_begun = sem("acc_begun")
        FFN = {1: (8, 4, "ffn0", 0), 3: (18, 1, "ffn1", 1), 5: (2, 3, None, None), 7: (16, 1, "ffn3", 2)}
        FFN_STEP, FFN_OG, FFN_RING, FFN_CB, FFN_END = {}, {}, {}, {}, {}
        count = [0, 0, 0, 0]
        for n, (e, u, w, r) in FFN.items():
            FFN_STEP[n], FFN_OG[n], FFN_RING[n], FFN_CB[n] = count
            count[0] += e * NG * u
            count[1] += e * NG
            count[2] += e // 2 if w else 0
            count[3] += e // 2 if w else 0
            FFN_END[n] = count[1]

        def ffn_order(n):
            return [(s, g, u) for s in range(2) for g in range(NG) for u in range(FFN[n][1])]

        def ffn_loop(eng, n, body, last=None):
            body(0, True)
            if FFN[n][0] > 2:
                with eng.Fori(1, FFN[n][0] // 2) as i:
                    body(i, False)

        def ffn_sync(n, wait_combine):
            sp = nc.sync
            E, U, w, r = FFN[n]
            S = 2 * NG * U

            def weights(i, s):
                if n > 1 or not isinstance(i, int):
                    before = FFN_STEP[n] if isinstance(i, int) else FFN_STEP[n] + i * S - S + (s + 1) * NG * U
                    sp.wait_ge(ffn_down, before)
                src = inp[w][bass.ds(2 * i + s, 1)].rearrange("a q n -> q (a n)")
                sp.dma_start(ring[:, s, 0:U * UNIT], src).then_inc(ring_full[s], 16)

            def combine(i, s):
                if not isinstance(i, int):
                    sp.wait_ge(ffn_out, FFN_OG[n] + i * 2 * NG - 2 * NG + (s + 1) * NG)
                row = scratch[r, bass.ds(2 * i + s, 1), :]
                sp.dma_start(cb[:, s, :], row.broadcast_to([P, NT])).then_inc(cb_full[s], 16)

            for s in range(2):
                weights(0, s)
            wait_combine(sp)
            for s in range(2):
                combine(0, s)
            with sp.Fori(1, E // 2) as i:
                for s in range(2):
                    weights(i, s)
                    combine(i, s)

        def ffn_pe(n, weights_ready=None):
            pe = nc.tensor
            U = FFN[n][1]
            order = ffn_order(n)
            S = len(order)

            def body(i, first):
                base = FFN_STEP[n] + i * S
                ogs = FFN_OG[n] + i * 2 * NG

                def out_product(x, step, ogs):
                    s, g, u = order[x]
                    pe.wait_ge(ffn_hid, step + 1)
                    if u == 0 and not (isinstance(ogs, int) and ogs + s * NG + g < 2):
                        pe.wait_ge(ffn_out, ogs + s * NG + g - 1)
                    for c in range(KD):
                        at = u * UNIT + 4 * P + c * P
                        mm = pe.matmul(PS[:, 4 + 2 * (g % 2) + c, 0:GN], ring[:, s, at:at + P], hact[:, x % 2, :],
                                       start=(u == 0), stop=(u == U - 1))
                    mm.then_inc(ffn_down, 1)

                for x, (s, g, u) in enumerate(order):
                    step = base + x
                    if g == 0 and u == 0:
                        if weights_ready:
                            weights_ready(pe)
                        else:
                            pe.wait_ge(ring_full[s], 16 * (FFN_RING[n] + i + 1))
                    if not (isinstance(step, int) and step < 2):
                        pe.wait_ge(ffn_hid, step - 1)
                    for b in range(2):
                        for k in range(KD):
                            at = u * UNIT + (2 * b + k) * P
                            mm = pe.matmul(PS[:, 2 * (x % 2) + b, 0:GN], ring[:, s, at:at + P], hgroup(k, g),
                                           start=(k == 0), stop=(k == KD - 1))
                    mm.then_inc(ffn_up, 1)
                    if x:
                        out_product(x - 1, step - 1, ogs)
                    elif not first:
                        out_product(S - 1, step - 1, ogs - 2 * NG)
                body.last = lambda: out_product(S - 1, FFN_STEP[n] + FFN[n][0] // 2 * S - 1,
                                                FFN_END[n] - 2 * NG)

            ffn_loop(pe, n, body)
            body.last()

        def ffn_act(n):
            a = nc.scalar
            order = ffn_order(n)

            def body(i, first):
                for x in range(len(order)):
                    step = FFN_STEP[n] + i * len(order) + x
                    a.wait_ge(ffn_up, step + 1)
                    if not (isinstance(step, int) and step < 2):
                        a.wait_ge(ffn_hid, step - 1)
                    a.activation(sg[:, x % 2, :], PS[:, 2 * (x % 2), 0:GN], ACT.Silu).then_inc(ffn_sg, 1)

            ffn_loop(a, n, body)

        def ffn_begin_dve():
            v = nc.vector
            for k in range(KD):
                ins = v.tensor_copy(acc[:, k, :].rearrange("q (a t) -> q a t", t=T), hP[:, k, :, 0:T])
            ins.then_inc(acc_begun, 1)

        def ffn_dve(n):
            v = nc.vector
            E, U, w, r = FFN[n]
            order = ffn_order(n)
            S = len(order)
            v.wait_ge(acc_begun, (n + 1) // 2)

            def body(i, first):
                def hidden(x):
                    step = FFN_STEP[n] + i * S + x
                    v.wait_ge(ffn_sg, step + 1)
                    if not (isinstance(step, int) and step < 2):
                        v.wait_ge(ffn_down, step - 1)
                    v.tensor_tensor(hact[:, x % 2, :], sg[:, x % 2, :], PS[:, 2 * (x % 2) + 1, 0:GN],
                                    ALU.mult).then_inc(ffn_hid, 1)

                def add_output(s, g, i, peeled):
                    og = FFN_OG[n] + i * 2 * NG + s * NG + g
                    sl = slice(g * GN, (g + 1) * GN)
                    v.wait_ge(ffn_down, FFN_STEP[n] + i * S + (s * NG + g + 1) * U)
                    if not (isinstance(og, int) and og < 2):
                        v.wait_ge(ffn_acc, og - 1)
                    src = PS[:, 4 + 2 * (g % 2):6 + 2 * (g % 2), 0:GN]
                    if r is None:
                        if s:
                            v.wait_ge(ffn_acc, og - 3)
                        v.tensor_tensor(tmp[:, g % 2], src, acc[:, :, sl], ALU.add).then_inc(ffn_out, 1)
                        v.wait_ge(ffn_out, og + 1)
                        v.tensor_copy(acc[:, :, sl], tmp[:, g % 2]).then_inc(ffn_acc, 1)
                        return
                    if g == 0:
                        v.wait_ge(cb_full[s], 16 * (FFN_CB[n] + i + 1))
                    v.tensor_tensor(tmp[:, g % 2], src, bcast(cb[:, s, sl], 0, KD), ALU.mult).then_inc(ffn_out, 1)
                    v.wait_ge(ffn_out, og + 1)
                    v.tensor_tensor(acc[:, :, sl], acc[:, :, sl], tmp[:, g % 2], ALU.add).then_inc(ffn_acc, 1)

                for x, (s, g, u) in enumerate(order):
                    hidden(x)
                    if u == 0:
                        if x:
                            add_output(*order[x - 1][:2], i, first)
                        elif not first:
                            add_output(1, NG - 1, i - 1, False)
                body.last = lambda: add_output(1, NG - 1, E // 2 - 1, False)

            ffn_loop(v, n, body)
            body.last()

        def per(ap, n):
            return bass.AP(ap.tensor, ap.offset, list(ap.ap) + [[0, n]])

        def choose_dve(vals, R, E, k, sel, work, reset, before=None):
            v = nc.vector
            m8, gt, eq, pre, room = work
            v.memset(reset, 1.0).then_inc(dve_step, 1)
            steps["dve"] += 1
            for i in range(R):
                ins = v.max(m8[:, i, :], vals[:, i, :])
            dve_then(ins)
            dve_then(v.memset(reset[:, :, 0:1], 0.0))
            thr = per(m8[:, :, k - 1], E)
            v.tensor_tensor(eq, vals, thr, ALU.is_equal)
            dve_then(v.tensor_tensor(gt, vals, thr, ALU.is_gt))
            v.tensor_tensor_scan(pre.rearrange("q a b -> q (a b)"), reset.rearrange("q a b -> q (a b)"),
                                 eq.rearrange("q a b -> q (a b)"), 0.0, ALU.mult, ALU.add)
            dve_then(v.tensor_reduce(room, gt, AX, ALU.add))
            dve_then(v.tensor_scalar(room, room, -1.0, float(k), ALU.mult, ALU.add))
            dve_then(v.tensor_tensor(pre, pre, per(room, E), ALU.is_le))
            dve_then(v.tensor_tensor(eq, eq, pre, ALU.mult))
            dve_then(v.tensor_tensor(sel, gt, eq, ALU.add))

        gate_w = sb("gate_w", [P, 48])
        gate_loaded = sem("gate_loaded")
        gate_ready = sem("gate_ready")
        gate_shifted = sem("gate_shifted")
        gate_exp = sem("gate_exp")
        comb_ready = sem("comb_ready")
        combT_ready = sem("combT_ready")
        combT_copied = sem("combT_copied")
        comb_stored = sem("comb_stored")
        ga = carve(arena, AR)
        ga(FA)
        g_lg, g_gt, g_eq, g_pre, g_sel, g_rst, g_e, g_c = [ga(256) for _ in range(8)]
        g_m8 = ga(128).rearrange("q (a b) -> q a b", b=8)
        g_room, g_sum, g_rec = ga(64), ga(64), ga(64)
        g_T = ga(NT)

        def tile3(ap, E):
            return ap[:, 0:16 * E].rearrange("q (a b) -> q a b", b=E)

        def logits_pe(w, E):
            pe = nc.tensor
            for p in range(NP):
                for k in range(KD):
                    mm = pe.matmul(PS[:, 0, p * E:(p + 1) * E], hpair(k, p), w[:, k, :], start=(k == 0),
                                   stop=(k == KD - 1))
            mm.then_inc(gate_ready, 1)

        def combine_pe(c, E):
            pe = nc.tensor
            pe.wait_ge(comb_ready, c + 1)
            for p in range(NP):
                mm = pe.transpose(PS[0:E, p // 4, (p % 4) * P:(p % 4 + 1) * P], tile3(g_c, E)[:, p, :], ident)
            mm.then_inc(combT_ready, 1)

        def combine_dve(c, E):
            v = nc.vector
            v.wait_ge(combT_ready, c + 1)
            src = PS[0:E, 0:4, :].rearrange("q b (a t) -> q (b a) t", t=SP)[:, :, 0:T]
            v.tensor_copy(g_T[0:E].rearrange("q (a t) -> q a t", t=T), src).then_inc(combT_copied, 1)

        def combine_sync(c, E):
            nc.sync.wait_ge(combT_copied, c + 1)
            nc.sync.dma_start(scratch[c, 0:E, :], g_T[0:E]).then_inc(comb_stored, 16)
            nc.sync.wait_ge(comb_stored, 16 * (c + 1))

        g0_w = gate_w[:, 0:16].rearrange("q (k e) -> q k e", k=2)
        g1_w = gate_w[:, 16:48].rearrange("q (k e) -> q k e", k=2)

        def block1_sync():
            nc.sync.dma_start(gate_w[:, :], inp["gates"]).then_inc(gate_loaded, 16)
            ffn_sync(1, lambda sp: combine_sync(0, 8))

        def block1_pe():
            block_before(nc.tensor, 1)
            nc.tensor.wait_ge(gate_loaded, 16)
            logits_pe(g0_w, 8)
            combine_pe(0, 8)
            nc.tensor.wait_ge(combT_copied, 1)
            ffn_pe(1)
            ln_pe(1)

        def block1_act():
            a = nc.scalar
            block_before(a, 1)
            a.wait_ge(gate_shifted, 1)
            a.activation(tile3(g_e, 8), tile3(g_e, 8), ACT.Exp).then_inc(gate_exp, 1)
            ffn_act(1)
            ln_act(1)

        def block1_dve():
            v = nc.vector
            block_before(v, 1)
            ffn_begin_dve()
            v.wait_ge(gate_ready, 1)
            lg, gt, eq, pre, sel, rst, e, c = [tile3(x, 8) for x in (g_lg, g_gt, g_eq, g_pre, g_sel, g_rst, g_e, g_c)]
            dve_then(v.tensor_copy(lg, PS[:, 0, 0:128].rearrange("q (a b) -> q a b", b=8)))
            choose_dve(lg, 16, 8, 2, sel, (g_m8, gt, eq, pre, g_room[:, 0:16]), rst)
            v.tensor_tensor(e, lg, per(g_m8[:, :, 0], 8), ALU.subtract).then_inc(gate_shifted, 1)
            v.wait_ge(gate_exp, 1)
            dve_then(v.tensor_tensor(c, e, sel, ALU.mult))
            dve_then(v.tensor_reduce(g_sum[:, 0:16], c, AX, ALU.add))
            dve_then(v.reciprocal(g_rec[:, 0:16], g_sum[:, 0:16]))
            v.tensor_tensor(c, c, per(g_rec[:, 0:16], 8), ALU.mult).then_inc(comb_ready, 1)
            combine_dve(0, 8)
            ffn_dve(1)
            ln_dve(1)

        S2 = 64
        w2 = carve(wA, 6656)
        sp_pT = w2(2 * S2).rearrange("q (k n) -> q k n", k=2)
        sp_wv = w2(2 * D).rearrange("q (k n) -> q k n", k=2)
        sp_wo = w2(2 * D).rearrange("q (k n) -> q k n", k=2)
        sp_p = w2(D + 2)
        s2 = carve(arena, AR)
        sp_pm2 = s2(2 * S2).rearrange("q (k n) -> q k n", k=2)
        sp_sq = s2(2 * NT).rearrange("q (k n) -> q k n", k=2)
        sp_raw = s2(NT)
        sp_g = s2(B * SP).rearrange("q (a t) -> q a t", t=SP)
        sp_v = s2(NP * D).rearrange("q (p n) -> q p n", p=NP)
        sp_gt = s2(2 * S2).rearrange("q (s n) -> q s n", s=2)
        sp_m = s2(2 * 2 * D).rearrange("q (s i n) -> q s i n", s=2, i=2)
        sp_cb = s2(2 * 2 * P).rearrange("q (s i n) -> q s i n", s=2, i=2)
        sp_den = s2(2 * 2 * T).rearrange("q (s n) -> q s n", s=2)
        sp_c, sp_tmp, sp_col = s2(B), s2(D), s2(8)
        sp_sq_ready = sem("sp_sq_ready")
        sp_par_ready = sem("sp_par_ready")
        sp_scale_ready = sem("sp_scale_ready")
        sp_d_ready = sem("sp_d_ready")
        sp_d2_ready = sem("sp_d2_ready")
        sp_exp_ready = sem("sp_exp_ready")
        sp_g_ready = sem("sp_g_ready")
        sp_v_ready = sem("sp_v_ready")
        sp_v_evac = sem("sp_v_evac")
        sp_c_ready = sem("sp_c_ready")
        sp_t_ready = sem("sp_t_ready")
        sp_gt_ready = sem("sp_gt_ready")
        sp_m_ready = sem("sp_m_ready")
        sp_m_evac = sem("sp_m_evac")
        sp_u_ready = sem("sp_u_ready")
        sp_out_ready = sem("sp_out_ready")

        def block2_sync():
            nc.sync.wait_ge(h_ready, NG * 2)
            nc.sync.dma_start(wA[:, 0:w2.at - D - 2], inp["splat"]).then_inc(wA_loaded, 16)
            nc.sync.dma_start(sp_p[0:S2, :], inp["splat_side"]).then_inc(wA_loaded, 16)

        def block2_pe():
            pe = nc.tensor
            block_before(pe, 2)
            pe.wait_ge(wA_loaded, 64)
            pe.wait_ge(sp_par_ready, 1)
            for g in range(NG):
                pe.wait_ge(sp_sq_ready, g + 1)
                for k in range(KD):
                    pe.matmul(PS[0:S2, g, 0:GN], sp_pm2[:, k, :], hgroup(k, g), start=(k == 0), stop=False)
                for k in range(KD):
                    mm = pe.matmul(PS[0:S2, g, 0:GN], const("ones")[:, 0:S2], sp_sq[:, k, g * GN:(g + 1) * GN],
                                   start=False, stop=(k == 1))
                mm.then_inc(sp_d_ready, 1)
            for p in range(NP):
                if p >= 4:
                    pe.wait_ge(sp_v_evac, p - 3)
                for k in range(KD):
                    mm = pe.matmul(PS[:, 4 + p % 4, 0:D], hpair(k, p), sp_wv[:, k, :], start=(k == 0), stop=(k == 1))
                mm.then_inc(sp_v_ready, 1)
            pe.wait_ge(sp_g_ready, NG)
            pe.wait_ge(sp_v_evac, NP)

            def turn(p):
                if p >= 2:
                    pe.wait_ge(sp_gt_ready, p - 1)
                pe.transpose(PS[:, p % 2, 0:S2], sp_g[0:S2, 2 * p:2 * p + 2, :].rearrange("q a t -> q (a t)"),
                             ident[0:S2, 0:S2]).then_inc(sp_t_ready, 1)

            def moments(p):
                pe.wait_ge(sp_gt_ready, p + 1)
                if p:
                    pe.wait_ge(sp_m_evac, p)
                for i in range(2):
                    rws = slice(i * SP, i * SP + T)
                    mm = pe.matmul(PS[0:S2, 2 + i, 0:D], sp_gt[rws, p % 2, :], sp_v[rws, p, :], start=True, stop=True)
                mm.then_inc(sp_m_ready, 1)

            def outputs(p):
                pe.wait_ge(sp_m_evac, p + 1)
                pe.wait_ge(sp_c_ready, p + 2)
                if p >= 2:
                    pe.wait_ge(sp_out_ready, p - 1)
                for i in range(2):
                    g = sp_g[0:S2, 2 * p + i, 0:T]
                    for c in range(KD):
                        at = (2 * c + i) * T
                        pe.matmul(PS[:, 4 + p % 2, at:at + T], sp_m[0:S2, p % 2, i, c * P:(c + 1) * P], g,
                                  start=True, stop=True)
                    at = (4 + i) * T
                    mm = pe.matmul(PS[:, 4 + p % 2, at:at + T], sp_cb[0:S2, p % 2, i, :], g, start=True, stop=True)
                mm.then_inc(sp_u_ready, 1)

            turn(0)
            for p in range(NP):
                moments(p)
                if p + 1 < NP:
                    turn(p + 1)
                if p:
                    outputs(p - 1)
            outputs(NP - 1)
            project_pe(sp_wo, lambda e: e.wait_ge(sp_out_ready, NP))
            ln_pe(2)

        def block2_act():
            a = nc.scalar
            block_before(a, 2)
            for g in range(NG):
                for k in range(KD):
                    ins = a.activation(compact(sp_sq[:, k, g * GN:(g + 1) * GN]), hgroup(k, g), ACT.Square)
                ins.then_inc(sp_sq_ready, 1)
            a.wait_ge(wA_loaded, 64)
            a.activation(sp_col[0:S2, 0:1], sp_p[0:S2, D:D + 1], ACT.Exp).then_inc(sp_scale_ready, 1)
            for g in range(NG):
                a.wait_ge(sp_d2_ready, g + 1)
                sl = slice(g * GN, (g + 1) * GN)
                a.activation(sp_raw[0:S2, sl], sp_raw[0:S2, sl], ACT.Exp, scale=sp_col[0:S2, 3:4]).then_inc(sp_exp_ready, 1)
            for p in range(NP):
                a.wait_ge(sp_m_ready, p + 1)
                if p >= 2:
                    a.wait_ge(sp_u_ready, p - 1)
                a.activation(sp_m[0:S2, p % 2], PS[0:S2, 2:4, 0:D], ACT.Copy).then_inc(sp_m_evac, 1)
            ln_act(2)

        def block2_dve():
            v = nc.vector
            block_before(v, 2)
            v.wait_ge(wA_loaded, 64)
            v.tensor_scalar(sp_pm2, sp_pT, -2.0, None, ALU.mult).then_inc(sp_par_ready, 1)
            dve_then(v.tensor_tensor(sp_tmp[0:S2], sp_p[0:S2, 0:D], sp_p[0:S2, 0:D], ALU.mult))
            v.tensor_reduce(sp_col[0:S2, 1:2], sp_tmp[0:S2], AX, ALU.add)
            v.wait_ge(sp_scale_ready, 1)
            dve_then(v.tensor_tensor(sp_col[0:S2, 2:3], sp_col[0:S2, 0:1], sp_col[0:S2, 0:1], ALU.mult))
            dve_then(v.reciprocal(sp_col[0:S2, 4:5], sp_col[0:S2, 2:3]))
            dve_then(v.tensor_scalar(sp_col[0:S2, 3:4], sp_col[0:S2, 4:5], -0.5, None, ALU.mult))
            dve_then(v.memset(sp_g[0:S2], 0.0))
            for g in range(NG):
                v.wait_ge(sp_d_ready, g + 1)
                v.tensor_scalar(sp_raw[0:S2, g * GN:(g + 1) * GN], PS[0:S2, g, 0:GN], sp_col[0:S2, 1:2], 0.0, ALU.add,
                                ALU.max).then_inc(sp_d2_ready, 1)
            for p in range(NP):
                v.wait_ge(sp_v_ready, p + 1)
                v.tensor_copy(sp_v[:, p, :], PS[:, 4 + p % 4, 0:D]).then_inc(sp_v_evac, 1)
            for g in range(NG):
                v.wait_ge(sp_exp_ready, g + 1)
                v.tensor_scalar(sp_g[0:S2, g * GI:(g + 1) * GI, 0:T], compact(sp_raw[0:S2, g * GN:(g + 1) * GN]),
                                sp_p[0:S2, D + 1:D + 2], None, ALU.mult).then_inc(sp_g_ready, 1)
            v.wait_ge(sp_g_ready, NG)
            v.tensor_reduce(sp_c[0:S2], sp_g[0:S2, :, 0:T], AX, ALU.add).then_inc(sp_c_ready, 1)
            v.wait_ge(sp_c_ready, 1)

            def out_rows_of(p):
                v.wait_ge(sp_u_ready, p + 1)
                dve_then(v.tensor_scalar(sp_den[:, 0, :], PS[:, 4 + p % 2, 4 * T:6 * T], 1e-8, None, ALU.add))
                dve_then(v.reciprocal(sp_den[:, 1, :], sp_den[:, 0, :]))
                for c in range(KD):
                    ins = v.tensor_tensor(aT[:, c, 2 * p:2 * p + 2, 1:T + 1],
                                          compact(PS[:, 4 + p % 2, 2 * c * T:(2 * c + 2) * T]),
                                          compact(sp_den[:, 1, :]), ALU.mult)
                ins.then_inc(sp_out_ready, 1)
                v.wait_ge(sp_out_ready, p + 1)

            for p in range(NP):
                v.wait_ge(sp_t_ready, p + 1)
                if p >= 2:
                    v.wait_ge(sp_m_ready, p - 1)
                v.tensor_copy(sp_gt[:, p % 2, :], PS[:, p % 2, 0:S2]).then_inc(sp_gt_ready, 1)
                if p >= 2:
                    v.wait_ge(sp_u_ready, p - 1)
                v.tensor_copy(sp_cb[0:S2, p % 2], per(sp_c[0:S2, 2 * p:2 * p + 2], P)).then_inc(sp_c_ready, 1)
                if p >= 2:
                    out_rows_of(p - 2)
            out_rows_of(NP - 2)
            out_rows_of(NP - 1)
            project_dve([zcol[:, 0:1]] * 2)
            ln_dve(2)

        one_rows = sb("one_rows", [2, NT])
        one_set = sem("one_set")
        one_stored = sem("one_stored")

        def block3_pool():
            nc.gpsimd.memset(one_rows[:, :], 1.0).then_inc(one_set, 1)
            nc.gpsimd.wait_ge(one_set, 1)
            nc.gpsimd.dma_start(scratch[1, 16:18, :], one_rows[:, :]).then_inc(one_stored, 16)

        def block3_sync():
            def combined(sp):
                combine_sync(1, 16)
                sp.wait_ge(one_stored, 16)
            ffn_sync(3, combined)

        def block3_pe():
            block_before(nc.tensor, 3)
            logits_pe(g1_w, 16)
            combine_pe(1, 16)
            nc.tensor.wait_ge(combT_copied, 2)
            ffn_pe(3)
            ln_pe(3)

        def block3_act():
            a = nc.scalar
            block_before(a, 3)
            a.wait_ge(gate_ready, 2)
            a.activation(g_e, PS[:, 0, 0:256], ACT.Sigmoid).then_inc(gate_exp, 1)
            ffn_act(3)
            ln_act(3)

        def block3_dve():
            v = nc.vector
            block_before(v, 3)
            ffn_begin_dve()
            v.wait_ge(gate_exp, 2)
            E = 16
            sc, gt, eq, pre, sel, rst, c, mk = [tile3(x, E) for x in (g_e, g_gt, g_eq, g_pre, g_sel, g_rst, g_c, g_lg)]
            s4 = g_e.rearrange("q (a b) -> q a b", b=4)
            t1, gs = g_gt[:, 0:64], g_room
            dve_then(v.tensor_tensor(gs, s4[:, :, 0], s4[:, :, 1], ALU.add))
            for x, y in ((0, 2), (0, 3), (1, 2), (1, 3), (2, 3)):
                dve_then(v.tensor_tensor(t1, s4[:, :, x], s4[:, :, y], ALU.add))
                dve_then(v.tensor_tensor(gs, gs, t1, ALU.max))
            g3 = gs.rearrange("q (p g) -> q p g", g=4)
            other = bass.AP(g3.tensor, g3.offset, [g3.ap[0], g3.ap[1], [0, 4], g3.ap[2]])
            own = per(g3, 4)
            cmp4 = lambda x: x[:, 0:256].rearrange("q (p g o) -> q p g o", g=4, o=4)
            v.tensor_tensor(cmp4(g_eq), other, own, ALU.is_equal)
            dve_then(v.tensor_tensor(cmp4(g_pre), other, own, ALU.is_gt))
            dve_then(v.tensor_tensor(tile3(g_eq, 16), tile3(g_eq, 16), bcast(const("tril4"), 0, 16), ALU.mult))
            dve_then(v.tensor_tensor(g_pre, g_pre, g_eq, ALU.add))
            dve_then(v.tensor_reduce(g_sum, g_pre.rearrange("q (a b) -> q a b", b=4), AX, ALU.add))
            dve_then(v.tensor_scalar(g_sum, g_sum, 2.0, None, ALU.is_lt))
            dve_then(v.tensor_scalar(g_rec, g_sum, 2.0, -2.0, ALU.mult, ALU.add))
            m4 = g_lg.rearrange("q (a b) -> q a b", b=4)
            dve_then(v.tensor_tensor(m4, s4, per(g_sum, 4), ALU.mult))
            dve_then(v.tensor_tensor(m4, m4, per(g_rec, 4), ALU.add))
            choose_dve(mk, 16, E, 4, sel, (g_m8, gt, eq, pre, g_room[:, 0:16]), rst)
            dve_then(v.tensor_tensor(c, sc, sel, ALU.mult))
            dve_then(v.tensor_reduce(g_sum[:, 0:16], c, AX, ALU.add))
            dve_then(v.tensor_scalar(g_sum[:, 0:16], g_sum[:, 0:16], 1e-6, None, ALU.add))
            dve_then(v.reciprocal(g_rec[:, 0:16], g_sum[:, 0:16]))
            v.tensor_tensor(c, c, per(g_rec[:, 0:16], E), ALU.mult).then_inc(comb_ready, 1)
            combine_dve(1, 16)
            ffn_dve(3)
            ln_dve(3)

        H8, M, DK = 8, 64, 32
        LV = LEVELS + 1
        w4 = carve(wA, 6656)
        gs_wq, gs_wk, gs_wv, gs_wo = [w4(2 * D).rearrange("q (k n) -> q k n", k=2) for _ in range(4)]
        gs_w1 = w4(2 * M).rearrange("q (k n) -> q k n", k=2)
        gs_w2 = w4(H8 * M)
        gs_nw = w4(D)
        s4_ = carve(arena, AR)
        gs_q, gs_k = [s4_(2 * NT).rearrange("q (c n) -> q c n", c=2) for _ in range(2)]
        gs_v = s4_(NP * D).rearrange("q (p n) -> q p n", p=NP)
        gs_lf, gs_s = [s4_(4 * 512).rearrange("q (p n) -> q p n", p=4) for _ in range(2)]
        gs_E, gs_L = [s4_(2 * 512).rearrange("q (s n) -> q s n", s=2) for _ in range(2)]
        gs_A = s4_(2 * 8 * T).rearrange("q (s h t) -> q s h t", s=2, h=8)
        gs_t, gs_ok, gs_qv = [s4_(512) for _ in range(3)]
        gs_qT, gs_sT = [s4_(4 * 2 * T).rearrange("q (c n) -> q c n", c=4) for _ in range(2)]
        gs_Lf, gs_qR = [s4_(2 * 4 * 2 * T).rearrange("q (s c n) -> q s c n", s=2, c=4) for _ in range(2)]
        gs_B, gs_tB = [s4_(8 * T).rearrange("q (h t) -> q h t", h=8) for _ in range(2)]
        gs_col = s4_(32)
        gs_t12 = xc[0:M, :, :].rearrange("q k n -> q (k n)")[:, 0:B * SP].rearrange("q (a t) -> q a t", t=SP)
        accf = acc[:, :, :].rearrange("q k n -> q (k n)")
        gs_Ef = accf[:, 0:4 * LEVELS * 2 * T].rearrange("q (c l n) -> q c l n", c=4, l=LEVELS)
        gs_gt = accf[:, 4 * LEVELS * 2 * T:4 * LEVELS * 2 * T + D]
        (gs_pad, gs_o, gs_o_evac, gs_vr, gs_v_evac, gs_f, gs_ln, gs_lf_ready, gs_se, gs_s_ready, gs_at, gs_gate,
         gs_gt_ready, gs_zf, gs_ef, gs_st, gs_st_evac, gs_z, gs_e, gs_l, gs_a, gs_p1, gs_okm, gs_sub, gs_sexp,
         gs_qv_ready, gs_qt, gs_qt_evac, gs_lf2, gs_qr, gs_p2, gs_bm, gs_bacc, gs_ov, gs_ov_read, gs_ms, gs_rms,
         gs_og, gs_ogt, gs_aT) = [sem("gs_" + x) for x in (
             "pad_zeroed", "proj_ready", "proj_evac", "v_ready", "v_evac", "f_ready", "ln_ready", "logf_ready",
             "exp_logf_ready", "s_ready", "scores_ready", "gate_ready", "tanh_ready", "zf_ready", "ef_ready",
             "sT_ready", "sT_evac", "z_ready", "e_ready", "left_ready", "masked_ready", "slots_ready", "slots_read",
             "shifted", "exp_ready", "qv_ready", "qvT_ready", "qvT_evac", "leftT_ready", "qvdecay_ready",
             "pairs_ready", "pairs_read", "pairs_summed", "out_ready", "out_read", "squares_ready", "rms_ready",
             "normed", "normT_ready", "aT_ready")]

        def block4_sync():
            nc.sync.wait_ge(h_ready, NG * 4)
            nc.sync.dma_start(wA[:, 0:4 * 2 * D + 2 * M], inp["slots"]).then_inc(wA_loaded, 16)
            nc.sync.dma_start(gs_w2[0:M, :], inp["slots_2"]).then_inc(wA_loaded, 16)
            nc.sync.dma_start(gs_nw, inp["norm_w"].broadcast_to([P, D])).then_inc(wA_loaded, 16)

        def block4_pe():
            pe = nc.tensor
            block_before(pe, 4)
            pe.wait_ge(wA_loaded, 64 + 48)
            n = 0
            for g in range(NG):
                outs = [(w[:, :, c * P:(c + 1) * P], P) for w in (gs_wq, gs_wk) for c in range(2)] + [(gs_w1, M)]
                for w, m in outs:
                    if n >= 4:
                        pe.wait_ge(gs_o_evac, n - 3)
                    for k in range(KD):
                        mm = pe.matmul(PS[0:m, n % 4, 0:GN], w[:, k, :], hgroup(k, g), start=(k == 0), stop=(k == 1))
                    mm.then_inc(gs_o, 1)
                    n += 1
                for p in range(4 * g, 4 * g + 4):
                    if p >= 4:
                        pe.wait_ge(gs_v_evac, p - 3)
                    for k in range(KD):
                        mm = pe.matmul(PS[:, 4 + p % 4, 0:D], hpair(k, p), gs_wv[:, k, :], start=(k == 0),
                                       stop=(k == 1))
                    mm.then_inc(gs_vr, 1)
            pe.wait_ge(gs_o_evac, 5 * NG)
            pe.wait_ge(gs_v_evac, NP)
            pe.wait_ge(gs_pad, 2)

            def t12(p, at):
                return gs_t12[at:at + DK, 2 * p:2 * p + 2, :].rearrange("q a t -> q (a t)")

            def pair(p):
                i4 = p % 4
                if i4 == 0:
                    if p:
                        pe.wait_ge(gs_ov_read, p)
                    for x in range(4):
                        pe.matmul(PS[:, x, :], t12(p + x, 0), gs_w2[0:DK, :], start=True, stop=True).then_inc(gs_f, 1)
                    pe.wait_ge(gs_lf_ready, p + 4)
                if p:
                    pe.wait_ge(gs_ov_read, p)
                for r in (0, 2, 1, 3):
                    if r % 2:
                        pe.wait_ge(row_tile_done, tile_count["n"] - 1)
                    for i in range(2):
                        for c in range(2):
                            tok = slice((2 * p + i) * T, (2 * p + i + 1) * T)
                            at = ((r % 2) * 2 + c) * T
                            mm = pe.matmul(PS[i * SP:i * SP + T, 2 + r // 2, at:at + T],
                                           gs_k[32 * r:32 * r + DK, c, tok], gs_q[32 * r:32 * r + DK, c, tok],
                                           start=True, stop=True)
                    if r != 3:
                        mm.then_inc(row_tile_done, 1)
                        tile_count["n"] += 1
                mm.then_inc(gs_at, 1)
                pe.matmul(PS[:, 0, 0:D], t12(p, DK), gs_w2[DK:2 * DK, 0:D], start=True, stop=True).then_inc(gs_gate, 1)

                def z(lv):
                    if lv >= 2:
                        pe.wait_ge(gs_e, LEVELS * p + lv - 1)
                    pe.matmul(PS[:, 4 + lv % 2, :], const("lsum")[:, lv * P:(lv + 1) * P], gs_lf[:, i4, :],
                              start=True, stop=True).then_inc(gs_z, 1)

                z(0)
                z(1)
                for c in range(4):
                    if c >= 2:
                        pe.wait_ge(gs_ef, 4 * p + c - 1)
                    pe.matmul(PS[:, 6 + c % 2, 0:LEVELS * 2 * T], gs_lf[:, i4, c * P:(c + 1) * P], const("lsumc"),
                              start=True, stop=True).then_inc(gs_zf, 1)
                pe.wait_ge(gs_s_ready, p + 1)
                pe.wait_ge(gs_ef, 4 * p + 4)
                for c in range(4):
                    mm = pe.transpose(PS[:, 7, c * P:(c + 1) * P], gs_s[:, i4, c * P:(c + 1) * P], ident)
                mm.then_inc(gs_st, 1)
                pe.wait_ge(gs_gt_ready, p + 1)
                for lv in range(LV):
                    pe.wait_ge(gs_a, LV * p + lv + 1)
                    if lv < LEVELS:
                        pe.wait_ge(gs_l, LEVELS * p + lv + 1)
                    if lv >= 2:
                        pe.wait_ge(gs_okm, LV * p + lv - 1)
                    right = gs_L[:, lv % 2, :] if lv < LEVELS else gs_s[:, i4, :]
                    for i in range(2):
                        rws = slice(i * SP, i * SP + T)
                        for h in range(H8):
                            mm = pe.matmul(PS[rws, lv % 2, h * M:(h + 1) * M], gs_A[rws, lv % 2, (h % 4) * 2 + h // 4, :],
                                           right[rws, h * M:(h + 1) * M], start=True, stop=True)
                    mm.then_inc(gs_p1, 1)
                    if lv + 2 < LEVELS:
                        z(lv + 2)
                pe.wait_ge(gs_qv_ready, p + 1)
                for c in range(4):
                    mm = pe.transpose(PS[:, 6, c * P:(c + 1) * P], gs_qv[:, c * P:(c + 1) * P], ident)
                mm.then_inc(gs_qt, 1)
                for lv in range(LV):
                    if lv < LEVELS:
                        pe.wait_ge(gs_lf2, LEVELS * p + lv + 1)
                        pe.wait_ge(gs_qr, LEVELS * p + lv + 1)
                        left, right = gs_Lf[:, lv % 2], gs_qR[:, lv % 2]
                    else:
                        left, right = gs_sT, gs_qT
                    if lv >= 2:
                        pe.wait_ge(gs_bm, LV * p + lv - 1)
                    for e in range(2):
                        for i in range(2):
                            for c in range(4):
                                mm = pe.matmul(PS[i * SP:i * SP + T, 2 + 2 * (lv % 2) + e, c * T:(c + 1) * T],
                                               left[e * M:(e + 1) * M, c, i * T:(i + 1) * T],
                                               right[e * M:(e + 1) * M, c, i * T:(i + 1) * T], start=True, stop=True)
                    mm.then_inc(gs_p2, 1)
                pe.wait_ge(gs_bacc, p + 1)
                for i in range(2):
                    rws = slice(i * SP, i * SP + T)
                    for h in range(H8):
                        mm = pe.matmul(PS[rws, 6, h * DK:(h + 1) * DK], gs_B[rws, (h % 2) * 4 + h // 2, :],
                                       gs_v[rws, p, h * DK:(h + 1) * DK], start=True, stop=True)
                mm.then_inc(gs_ov, 1)

            for p in range(NP):
                pair(p)
            for p in range(NP):
                pe.wait_ge(gs_og, p + 1)
                if p >= 6:
                    pe.wait_ge(gs_aT, p - 5)
                for c in range(KD):
                    mm = pe.transpose(PS[:, p % 6, c * P:(c + 1) * P], gs_v[:, p, c * P:(c + 1) * P], ident)
                mm.then_inc(gs_ogt, 1)
            project_pe(gs_wo, lambda e: e.wait_ge(gs_aT, NP))
            ln_pe(4)

        def block4_act():
            a = nc.scalar
            block_before(a, 4)
            a.wait_ge(gs_pad, 1)
            n = 0
            for g in range(NG):
                sl = slice(g * GN, (g + 1) * GN)
                for dst in (gs_q, gs_k):
                    for c in range(2):
                        a.wait_ge(gs_o, n + 1)
                        a.activation(dst[:, c, sl], PS[:, n % 4, 0:GN], ACT.Silu).then_inc(gs_o_evac, 1)
                        n += 1
                a.wait_ge(gs_o, n + 1)
                a.activation(gs_t12[:, g * GI:(g + 1) * GI, 0:T], compact(PS[0:M, n % 4, 0:GN]),
                             ACT.Copy).then_inc(gs_o_evac, 1)
                n += 1
            for p in range(NP):
                i4 = p % 4
                if i4 == 0:
                    for x in range(4):
                        a.wait_ge(gs_f, p + x + 1)
                        ins = a.activation(gs_lf[:, x, :], PS[:, x, :], ACT.Abs)
                    act_then(ins)
                    act_then(a.activation(gs_lf[:, :, :], gs_lf[:, :, :], ACT.Exp, scale=-1.0))
                    a.activation(gs_lf[:, :, :], gs_lf[:, :, :], ACT.Ln, bias=1.0).then_inc(gs_ln, 1)
                    for x in range(4):
                        a.wait_ge(gs_lf_ready, p + x + 1)
                        a.activation(gs_s[:, x, :], gs_lf[:, x, :], ACT.Exp).then_inc(gs_se, 1)
                if p:
                    a.wait_ge(gs_ov_read, p)
                    a.wait_ge(gs_p2, LV * p)
                a.wait_ge(gs_gate, p + 1)
                a.activation(gs_gt, PS[:, 0, 0:D], ACT.Tanh, scale=0.5).then_inc(gs_gt_ready, 1)

                def decay(lv):
                    a.wait_ge(gs_z, LEVELS * p + lv + 1)
                    if lv >= 2:
                        a.wait_ge(gs_okm, LV * p + lv - 1)
                    a.activation(gs_E[:, lv % 2, :], PS[:, 4 + lv % 2, :], ACT.Exp).then_inc(gs_e, 1)

                decay(0)
                decay(1)
                for c in range(4):
                    a.wait_ge(gs_zf, 4 * p + c + 1)
                    a.activation(gs_Ef[:, c], PS[:, 6 + c % 2, 0:LEVELS * 2 * T].rearrange(
                        "q (l n) -> q l n", l=LEVELS), ACT.Exp).then_inc(gs_ef, 1)
                a.wait_ge(gs_st, p + 1)
                a.activation(gs_sT.rearrange("q c (i t) -> q c i t", i=2),
                             PS[:, 7, :].rearrange("q (c i t) -> q c i t", c=4, i=2)[:, :, :, 0:T],
                             ACT.Copy).then_inc(gs_st_evac, 1)
                for lv in range(2, LEVELS):
                    decay(lv)
                a.wait_ge(gs_sub, p + 1)
                a.activation(gs_qv, gs_qv, ACT.Exp).then_inc(gs_sexp, 1)
                a.wait_ge(gs_qt, p + 1)
                a.activation(gs_qT.rearrange("q c (i t) -> q c i t", i=2),
                             PS[:, 6, :].rearrange("q (c i t) -> q c i t", c=4, i=2)[:, :, :, 0:T],
                             ACT.Copy).then_inc(gs_qt_evac, 1)
            a.wait_ge(gs_ms, 1)
            act_then(a.activation(gs_t[:, 0:P], gs_t[:, 0:P], ACT.Ln, scale=1.0 / DK, bias=epscol[:, 0:1]))
            a.activation(gs_t[:, 0:P], gs_t[:, 0:P], ACT.Exp, scale=-0.5).then_inc(gs_rms, 1)
            for p in range(NP):
                a.wait_ge(gs_ogt, p + 1)
                src = PS[:, p % 6, 0:D].rearrange("q (c i t) -> q c i t", c=2, i=2)
                for c in range(KD):
                    ins = a.activation(aT[:, c, 2 * p:2 * p + 2, 1:T + 1], src[:, c, :, 0:T], ACT.Copy)
                ins.then_inc(gs_aT, 1)
            ln_act(4)

        def block4_pool():
            po = nc.gpsimd
            for p in range(NP):
                i4 = p % 4
                for lv in range(LEVELS):
                    po.wait_ge(gs_e, LEVELS * p + lv + 1)
                    po.wait_ge(gs_s_ready, p + 1)
                    if lv >= 2:
                        po.wait_ge(gs_p1, LV * p + lv - 1)
                    elif p:
                        po.wait_ge(gs_p1, LV * p)
                    po.tensor_tensor(gs_L[:, lv % 2, :], gs_s[:, i4, :], gs_E[:, lv % 2, :], ALU.mult).then_inc(gs_l, 1)
                for lv in range(LEVELS):
                    po.wait_ge(gs_st_evac, p + 1)
                    po.wait_ge(gs_ef, 4 * p + 4)
                    if lv >= 2:
                        po.wait_ge(gs_p2, LV * p + lv - 1)
                    elif p:
                        po.wait_ge(gs_p2, LV * p)
                    po.tensor_tensor(gs_Lf[:, lv % 2], gs_sT, gs_Ef[:, :, lv, :], ALU.mult).then_inc(gs_lf2, 1)

        def block4_dve():
            v = nc.vector
            block_before(v, 4)
            v.memset(xc[0:M, :, :], 0.0).then_inc(gs_pad, 1)
            for p in range(NP):
                v.wait_ge(gs_vr, p + 1)
                v.tensor_copy(gs_v[:, p, :], PS[:, 4 + p % 4, 0:D]).then_inc(gs_v_evac, 1)
            v.wait_ge(gs_o_evac, 5 * NG)
            v.memset(PS[:, 2:4, :], 0.0).then_inc(gs_pad, 1)
            for p in range(NP):
                i4 = p % 4
                if i4 == 0:
                    v.wait_ge(gs_ln, p // 4 + 1)
                    for x in range(4):
                        v.scalar_tensor_tensor(out=gs_lf[:, x, :], in0=PS[:, x, :], scalar=0.0, in1=gs_lf[:, x, :],
                                               op0=ALU.min, op1=ALU.subtract).then_inc(gs_lf_ready, 1)
                    for x in range(4):
                        v.wait_ge(gs_se, p + x + 1)
                        v.tensor_scalar(gs_s[:, x, :], gs_s[:, x, :], -1.0, 1.0, ALU.mult,
                                        ALU.add).then_inc(gs_s_ready, 1)

                def masked(lv):
                    v.wait_ge(gs_at, p + 1)
                    if lv >= 2:
                        v.wait_ge(gs_p1, LV * p + lv - 1)
                    elif p:
                        v.wait_ge(gs_p1, LV * p)
                    src = PS[:, 2:4, 0:4 * T].rearrange("q b (h t) -> q b h t", h=4)
                    m = const("lmask")[:, lv * T:(lv + 1) * T]
                    v.tensor_tensor(gs_A[:, lv % 2].rearrange("q (b h) t -> q b h t", b=2), src,
                                    bcast(bcast(m, 0, 4), 0, 2), ALU.mult).then_inc(gs_a, 1)

                masked(0)
                masked(1)
                for lv in range(LV):
                    v.wait_ge(gs_p1, LV * p + lv + 1)
                    src = PS[:, lv % 2, :]
                    if lv == 0:
                        v.tensor_tensor(gs_ok, src, gs_E[:, 0, :], ALU.mult).then_inc(gs_okm, 1)
                    elif lv < LEVELS:
                        v.tensor_tensor(gs_t, src, gs_E[:, lv % 2, :], ALU.mult).then_inc(gs_okm, 1)
                        v.wait_ge(gs_okm, LV * p + lv + 1)
                        dve_then(v.tensor_tensor(gs_ok, gs_ok, gs_t, ALU.add))
                    else:
                        v.tensor_tensor(gs_ok, gs_ok, src, ALU.add).then_inc(gs_okm, 1)
                    v.wait_ge(gs_okm, LV * p + lv + 1)
                    if lv + 2 < LV:
                        masked(lv + 2)
                ok = gs_ok.rearrange("q (h m) -> q h m", h=H8)
                qv = gs_qv.rearrange("q (h m) -> q h m", h=H8)
                dve_then(v.tensor_reduce(gs_col[:, 0:8], ok, AX, ALU.max))
                if p:
                    v.wait_ge(gs_qt, p)
                v.tensor_tensor(qv, ok, per(gs_col[:, 0:8], M), ALU.subtract).then_inc(gs_sub, 1)
                v.wait_ge(gs_sexp, p + 1)
                dve_then(v.tensor_reduce(gs_col[:, 8:16], qv, AX, ALU.add))
                dve_then(v.reciprocal(gs_col[:, 16:24], gs_col[:, 8:16]))
                v.tensor_tensor(qv, qv, per(gs_col[:, 16:24], M), ALU.mult).then_inc(gs_qv_ready, 1)
                v.wait_ge(gs_qt_evac, p + 1)

                def query(lv):
                    if lv >= 2:
                        v.wait_ge(gs_p2, LV * p + lv - 1)
                    v.tensor_tensor(gs_qR[:, lv % 2], gs_qT, gs_Ef[:, :, lv, :], ALU.mult).then_inc(gs_qr, 1)

                query(0)
                query(1)
                for lv in range(LV):
                    v.wait_ge(gs_p2, LV * p + lv + 1)
                    b = 2 + 2 * (lv % 2)
                    src = PS[:, b:b + 2, 0:4 * T].rearrange("q b (h t) -> q b h t", h=4)
                    m = bcast(bcast(const("lmask")[:, lv * T:(lv + 1) * T], 0, 4), 0, 2)
                    dst = gs_tB if lv else gs_B
                    v.tensor_tensor(dst.rearrange("q (b h) t -> q b h t", b=2), src, m, ALU.mult).then_inc(gs_bm, 1)
                    v.wait_ge(gs_bm, LV * p + lv + 1)
                    if lv == LV - 1:
                        v.tensor_tensor(gs_B, gs_B, gs_tB, ALU.add).then_inc(gs_bacc, 1)
                    elif lv:
                        dve_then(v.tensor_tensor(gs_B, gs_B, gs_tB, ALU.add))
                    if lv + 2 < LEVELS:
                        query(lv + 2)
                dve_then(v.tensor_scalar(gs_gt, gs_gt, 0.5, 0.5, ALU.mult, ALU.add))
                v.wait_ge(gs_ov, p + 1)
                v.tensor_tensor(gs_v[:, p, :], PS[:, 6, 0:D], gs_gt, ALU.mult).then_inc(gs_ov_read, 1)
                v.wait_ge(gs_ov_read, p + 1)
            for p in range(NP):
                sq = gs_E[:, p % 2, 0:D]
                dve_then(v.tensor_tensor(sq, gs_v[:, p, :], gs_v[:, p, :], ALU.mult))
                ins = v.tensor_reduce(gs_t[:, p * 8:(p + 1) * 8], sq.rearrange("q (h d) -> q h d", h=8), AX, ALU.add)
                dve_then(ins)
            v.tensor_copy(gs_col[:, 0:1], gs_col[:, 1:2]).then_inc(gs_ms, 1)
            v.wait_ge(gs_rms, 1)
            for p in range(NP):
                og = gs_v[:, p, :].rearrange("q (h d) -> q h d", h=8)
                dve_then(v.tensor_tensor(og, og, per(gs_t[:, p * 8:(p + 1) * 8], DK), ALU.mult))
                v.tensor_tensor(gs_v[:, p, :], gs_v[:, p, :], gs_nw, ALU.mult).then_inc(gs_og, 1)
            project_dve([zcol[:, 0:1]] * 2)
            ln_dve(4)

        int_loaded = sem("int_loaded")
        dequantized = sem("dequantized")
        QW = 3 * UNIT

        def block5_sync():
            nc.sync.wait_ge(ffn_down, FFN_STEP[5])
            for x in range(2):
                nc.sync.dma_start(ring[:, x, 0:QW].bitcast(I32), inp["ffn2"][:, x * QW:(x + 1) * QW]).then_inc(int_loaded, 16)

        def block5_pool():
            nc.gpsimd.wait_ge(int_loaded, 32)
            for x in range(2):
                nc.gpsimd.tensor_scalar(ring[:, x, 0:QW], ring[:, x, 0:QW].bitcast(I32), float(np.float32(1.0 / 127.0)),
                                        None, ALU.mult).then_inc(dequantized, 1)

        def block5_pe():
            block_before(nc.tensor, 5)
            ffn_pe(5, lambda pe: pe.wait_ge(dequantized, 2))
            ln_pe(5)

        def block5_act():
            block_before(nc.scalar, 5)
            ffn_act(5)
            ln_act(5)

        def block5_dve():
            block_before(nc.vector, 5)
            ffn_begin_dve()
            ffn_dve(5)
            ln_dve(5)

        w6 = carve(wA, 6656)
        a6_wq, a6_wk = [w6(1024).rearrange("q (k n) -> q k n", k=2) for _ in range(2)]
        a6_wv, a6_wo = [w6(512).rearrange("q (k n) -> q k n", k=2) for _ in range(2)]
        a6_cw = w6(3072).rearrange("q (s k n) -> q s k n", s=3, k=2)
        a6_b = w6(14)
        a6_vb = w6(D)
        bias_scaled = sem("bias_scaled")

        def block6_sync():
            nc.sync.wait_ge(h_ready, NG * 6)
            nc.sync.dma_start(wA[:, 0:w6.at - D], inp["attn3"]).then_inc(wA_loaded, 16)
            nc.sync.dma_start(a6_vb, inp["v_bias"].broadcast_to([P, D])).then_inc(wA_loaded, 16)

        def block6_pe():
            pe = nc.tensor
            block_before(pe, 6)
            pe.wait_ge(wA_loaded, 112 + 32)
            heads_pe(1, a6_wq, a6_wk, a6_wv)
            attend_pe(1, 1)
            pe.wait_ge(aT_ready, 2 * NP)
            n = 0
            for g in range(NG):
                for c in range(4):
                    if n >= 4:
                        pe.wait_ge(qk_evac, 2 * NQK + n - 3)
                    for tap in range(3):
                        for k in range(KD):
                            mm = pe.matmul(PS[:, n % 4, 0:GN], a6_cw[:, tap, k, c * P:(c + 1) * P],
                                           aT[:, k, g * GI:(g + 1) * GI, tap:tap + T],
                                           start=(tap + k == 0), stop=(tap + k == 3))
                    mm.then_inc(qk_ready, 1)
                    n += 1
            attend_pe(2, 1)
            project_pe(a6_wo, lambda e: e.wait_ge(aT_ready, 3 * NP))
            ln_pe(6)

        def block6_act():
            a = nc.scalar
            block_before(a, 6)
            a.wait_ge(bias_scaled, 1)
            cols = [[a6_b[:, 4 * x + c:4 * x + c + 1] for c in range(4)] for x in range(3)]
            heads_act(1, cols[0], cols[1])
            attend_act(1)
            for n in range(16):
                g, c = n // 4, n % 4
                a.wait_ge(qk_ready, 2 * NQK + n + 1)
                a.activation(q_s[:, c, g * GN:(g + 1) * GN], PS[:, n % 4, 0:GN], ACT.Identity, bias=cols[2][c],
                             scale=0.25).then_inc(qk_evac, 1)
            attend_act(2)
            ln_act(6)

        def block6_dve():
            v = nc.vector
            block_before(v, 6)
            v.wait_ge(wA_loaded, 112 + 32)
            dve_then(v.tensor_scalar(a6_b[:, 0:4], a6_b[:, 0:4], 0.25, None, ALU.mult))
            v.tensor_scalar(a6_b[:, 8:12], a6_b[:, 8:12], 0.25, None, ALU.mult).then_inc(bias_scaled, 1)
            heads_dve(1, a6_vb)
            attend_dve(1, 1)
            attend_dve(2, 1)
            project_dve([a6_b[:, 12 + c:13 + c] for c in range(KD)])
            ln_dve(6)

        E7, CAP = 32, int(1.25 * NT / 32)
        CAP_ROUNDS, CAP_REST = (CAP - 1) // 8, CAP - (CAP - 1) // 8 * 8
        TILES = [(i, min(P, NT - i * P)) for i in range((NT + P - 1) // P)]
        NTL = len(TILES)
        LASTN = TILES[-1][1]
        w7 = carve(wA, 6656)
        r1 = w7(2 * P).rearrange("q (k n) -> q k n", k=2)
        r2 = w7(E7)
        r1b = w7(1)
        r1s = w7(P)
        e2 = w7(16 * P)
        r7 = carve(arena, AR)
        X = r7(NTL * D).rearrange("q (i n) -> q i n", i=NTL)
        slotT, keptW = r7(NT), r7(NT)
        slot = r7(NTL * E7).rearrange("q (i e) -> q i e", i=NTL)
        front = r7.at

        def overlay():
            c = carve(arena, AR)
            c(front)
            return c

        o1 = overlay()
        tmp7 = o1(NTL * D).rearrange("q (i n) -> q i n", i=NTL)
        statT, h1 = o1(NT), o1(NT)
        o2 = overlay()
        scoreT, weightT, wk0, wk1 = [o2(NT) for _ in range(4)]
        o2(o1.at - o2.at if o1.at > o2.at else 0)
        eqT, gtT, preT = [o2(NT) for _ in range(3)]
        small = [o2(NTL * E7).rearrange("q (i e) -> q i e", i=NTL) for _ in range(9)]
        m8_7 = o2(NTL * 8).rearrange("q (i e) -> q i e", i=NTL)
        stat = o2(NTL * 6).rearrange("q (i e) -> q i e", i=NTL)
        c7 = o2(32)
        m8T, roomT = o2(8), o2(1)
        o3 = overlay()
        G8 = 8 * CAP
        pick = o3(NTL * G8).rearrange("q (i n) -> q i n", i=NTL)
        xe = o3(2 * E7 * CAP).rearrange("q (k n) -> q k n", k=2)
        ye = o3(16 * D).rearrange("q (p n) -> q p n", p=16)
        ex_sg, ex_h = [o3(2 * 4 * CAP).rearrange("q (s n) -> q s n", s=2) for _ in range(2)]
        place, wbc = [o3(2 * GN).rearrange("q (s n) -> q s n", s=2) for _ in range(2)]
        gwT = rs[0:16, :]
        router_dve, router_pe, router_act = sem("router_dve"), sem("router_pe"), sem("router_act")
        ROUTER = {name: n + 1 for names in (
            ("compact", "last_tile_zeroed", "squares", "stats", "stats_copied", "psum_zeroed", "shifted", "scores",
             "kept", "slots_copied"),
            ("stats_turned", "logits", "scores_turned", "slots_turned"),
            ("roots", "exponentials")) for n, name in enumerate(names)}
        (r_x_ready, r_x_evac, r_h1p, r_h1, r_gw, r_gw_evac, gw_stored, pick_ready, xe_ready, xe_evac, ex_full0,
         ex_full1, ex_up, ex_sg_ready, ex_hid, ex_down, ex_out, pl_ready, wbc_ready, place_ready, sc_ready, sc_added,
         r_sl_used) = [sem("r_" + x) for x in (
             "x_ready", "x_evac", "hidden_ready", "gelu_ready", "group_ready", "group_evac", "group_stored",
             "pick_ready", "gathered", "gather_evac", "expert_loaded0", "expert_loaded1", "expert_up", "expert_gate",
             "expert_hidden", "expert_down", "expert_evac", "place_broadcast", "weight_evac", "place_ready",
             "scatter_ready", "scatter_added", "place_used")]
        ex_full = [ex_full0, ex_full1]

        def ex_loop(eng, body):
            body(0, True)
            with eng.Fori(1, E7 // 2) as i:
                body(i, False)

        def block7_sync():
            sp = nc.sync
            sp.wait_ge(h_ready, NG * 7)
            for x in range(2):
                if x == 0:
                    sp.wait_ge(ffn_down, FFN_STEP[7])
                sp.dma_start(ring[:, x, :], inp["experts"][x]).then_inc(ex_full[x], 16)
            sp.wait_ge(h_ready, NG * 8)
            sp.dma_start(wA[:, 0:2 * P + E7 + 1], inp["router"]).then_inc(wA_loaded, 16)
            sp.dma_start(r1s[0:6, :], inp["router_stats"]).then_inc(wA_loaded, 16)
            sp.dma_start(e2[0:E7, :], inp["pairs"]).then_inc(wA_loaded, 16)
            sp.wait_ge(r_gw_evac, 4)
            sp.dma_start(scratch[2, 0:16, :], gwT).then_inc(gw_stored, 16)
            with sp.Fori(1, E7 // 2) as i:
                for x in range(2):
                    sp.wait_ge(ex_down, 2 * i + x - 1)
                    sp.dma_start(ring[:, x, :], inp["experts"][bass.ds(2 * i + x, 1)].rearrange(
                        "a q n -> q (a n)")).then_inc(ex_full[x], 16)
            sp.wait_ge(ex_down, E7)

            def combined(sp):
                sp.wait_ge(gw_stored, 16)
                sp.wait_ge(sc_added, NG)
            ffn_sync(7, combined)

        def flat(banks, rows_, n):
            return [(b, min(512, n - 512 * j)) for j, b in enumerate(banks)]

        def block7_pe():
            pe = nc.tensor
            block_before(pe, 7)
            pe.wait_ge(router_dve, ROUTER["compact"])
            for i, n in TILES:
                if i >= 8:
                    pe.wait_ge(r_x_evac, i - 7)
                for k in range(KD):
                    mm = pe.transpose(PS[0:n, i % 8, k * P:(k + 1) * P], xc[:, k, i * P:i * P + n], ident)
                mm.then_inc(r_x_ready, 1)
            pe.wait_ge(router_dve, ROUTER["stats"])
            for i, n in TILES:
                mm = pe.transpose(PS[0:6, i // 4, (i % 4) * P:(i % 4) * P + n], stat[0:n, i, :], ident[0:n, 0:n])
            mm.then_inc(router_pe, 1)
            pe.wait_ge(router_dve, ROUTER["stats_copied"])
            pe.wait_ge(wA_loaded, 144 + 48)
            for g in range(NG):
                sl = slice(g * GN, (g + 1) * GN)
                for k in range(KD):
                    pe.matmul(PS[:, 4 + g, 0:GN], r1[:, k, :], xc[:, k, sl], start=(k == 0), stop=False)
                pe.matmul(PS[:, 4 + g, 0:GN], r1s[0:6, :], statT[0:6, sl], start=False, stop=True).then_inc(r_h1p, 1)
            pe.wait_ge(r_h1, NG)
            pe.wait_ge(router_dve, ROUTER["psum_zeroed"])
            for i, n in TILES:
                mm = pe.matmul(PS[0:n, 0, i * E7:(i + 1) * E7], h1[:, i * P:i * P + n], r2, start=True, stop=True)
            mm.then_inc(router_pe, 1)
            pe.wait_ge(router_dve, ROUTER["scores"])
            for j, src in enumerate((small[1], small[2])):
                for i, n in TILES:
                    mm = pe.transpose(PS[0:E7, 1 + 3 * j + i // 4, (i % 4) * P:(i % 4) * P + n], src[0:n, i, :],
                                      ident[0:n, 0:n])
            mm.then_inc(router_pe, 1)
            pe.wait_ge(router_dve, ROUTER["kept"])
            for g in range(NG):
                pe.matmul(PS[0:16, g, 0:GN], const("two")[0:E7, :], keptW[0:E7, g * GN:(g + 1) * GN], start=True,
                          stop=True).then_inc(r_gw, 1)
            for i, n in TILES:
                mm = pe.transpose(PS[0:n, 4, i * E7:(i + 1) * E7], slotT[0:E7, i * P:i * P + n], ident[0:E7, 0:E7])
            mm.then_inc(router_pe, 1)
            pe.wait_ge(r_gw_evac, NG)
            for q in range(4):
                for k in range(KD):
                    if k == 0:
                        pe.wait_ge(pick_ready, q + 1)
                        if q:
                            pe.wait_ge(xe_evac, q)
                    for i in range(NTL):
                        mm = pe.matmul(PS[:, 6 + k, 0:G8], X[:, i, k * P:(k + 1) * P], pick[:, i, :],
                                       start=(i == 0), stop=(i == NTL - 1))
                mm.then_inc(xe_ready, 1)
            pe.wait_ge(xe_evac, 4)

            def down(x, e):
                pe.wait_ge(ex_hid, e + 1)
                if not isinstance(e, int) or e >= 2:
                    pe.wait_ge(ex_out, e - 1)
                for j in range(4):
                    mm = pe.matmul(PS[x * SP:x * SP + CAP, 4, 0:D], ex_h[:, x, j * CAP:(j + 1) * CAP],
                                   ring[:, x, 2048 + j * D:2048 + (j + 1) * D], start=(j == 0), stop=(j == 3),
                                   skip_group_check=True)
                mm.then_inc(ex_down, 1)

            def body(i, first):
                for x in range(2):
                    e = 2 * i + x
                    pe.wait_ge(ex_full[x], 16 * i + 16)
                    if not first:
                        pe.wait_ge(ex_hid, e - 1)
                    for j in range(8):
                        for k in range(KD):
                            mm = pe.matmul(PS[:, 2 * x + j // 4, (j % 4) * CAP:(j % 4 + 1) * CAP],
                                           ring[:, x, k * 1024 + j * P:k * 1024 + (j + 1) * P],
                                           xe[:, k, bass.ds(e * CAP, CAP)], start=(k == 0), stop=(k == 1))
                    mm.then_inc(ex_up, 1)
                    if x or not first:
                        down(1 - x, e - 1)

            ex_loop(pe, body)
            down(1, E7 - 1)
            pe.wait_ge(ex_out, E7)
            for g in range(NG):
                sl = slice(g * GN, (g + 1) * GN)

                def spread(q):
                    n = g * 16 + q
                    if n >= 2:
                        pe.wait_ge(place_ready, n - 1)
                    w = e2[0:E7, q * P:(q + 1) * P]
                    pe.matmul(PS[:, 2 * (q % 2), 0:GN], w, slotT[0:E7, sl], start=True, stop=True)
                    pe.matmul(PS[:, 2 * (q % 2) + 1, 0:GN], w, keptW[0:E7, sl], start=True,
                              stop=True).then_inc(pl_ready, 1)

                spread(0)
                for q in range(16):
                    if q + 1 < 16:
                        spread(q + 1)
                    pe.wait_ge(place_ready, g * 16 + q + 1)
                    if q == 0 and g >= 2:
                        pe.wait_ge(sc_added, g - 1)
                    for c in range(KD):
                        mm = pe.matmul(PS[:, 4 + 2 * (g % 2) + c, 0:GN], ye[:, q, c * P:(c + 1) * P],
                                       place[:, q % 2, :], start=(q == 0), stop=(q == 15))
                    if q == 15:
                        mm.then_inc(sc_ready, 1)
                    else:
                        mm.then_inc(r_sl_used, 1)
            pe.wait_ge(sc_added, NG)
            ffn_pe(7)
            ln_pe(7)

        def block7_act():
            a = nc.scalar
            block_before(a, 7)
            for i, n in TILES:
                if i == NTL - 1:
                    a.wait_ge(router_dve, ROUTER["last_tile_zeroed"])
                a.wait_ge(r_x_ready, i + 1)
                a.activation(X[0:n, i, :], PS[0:n, i % 8, 0:D], ACT.Copy).then_inc(r_x_evac, 1)
            a.wait_ge(router_dve, ROUTER["squares"])
            a.activation(c7[:, 0:2 * NTL], c7[:, 0:2 * NTL], ACT.Sqrt).then_inc(router_act, 1)
            for g in range(NG):
                a.wait_ge(r_h1p, g + 1)
                a.activation(h1[:, g * GN:(g + 1) * GN], PS[:, 4 + g, 0:GN], ACT.Gelu, bias=r1b).then_inc(r_h1, 1)
            a.wait_ge(router_dve, ROUTER["shifted"])
            a.activation(small[0], small[0], ACT.Exp).then_inc(router_act, 1)
            for q in range(4):
                a.wait_ge(xe_ready, q + 1)
                a.activation(xe[:, :, q * G8:(q + 1) * G8], PS[:, 6:8, 0:G8], ACT.Copy).then_inc(xe_evac, 1)

            def body(i, first):
                for x in range(2):
                    e = 2 * i + x
                    a.wait_ge(ex_up, e + 1)
                    if not first:
                        a.wait_ge(ex_hid, e - 1)
                    a.activation(ex_sg[:, x, :], PS[:, 2 * x, 0:4 * CAP], ACT.Silu).then_inc(ex_sg_ready, 1)

            ex_loop(a, body)
            for n in range(NG * 16):
                a.wait_ge(pl_ready, n + 1)
                if n >= 2:
                    a.wait_ge(place_ready, n - 1)
                a.activation(wbc[:, n % 2, :], PS[:, 2 * (n % 2) + 1, 0:GN], ACT.Copy).then_inc(wbc_ready, 1)
            ffn_act(7)
            ln_act(7)

        def block7_dve():
            v = nc.vector
            block_before(v, 7)
            for k in range(KD):
                for g in range(NG):
                    ins = v.tensor_copy(compact(xc[:, k, g * GN:(g + 1) * GN]), hgroup(k, g))
            ins.then_inc(router_dve, 1)
            v.memset(X[:, NTL - 1, :], 0.0).then_inc(router_dve, 1)
            v.wait_ge(r_x_evac, NTL)
            dve_then(v.tensor_reduce(stat[:, :, 0], X, AX, ALU.add))
            dve_then(v.tensor_scalar(stat[:, :, 0], stat[:, :, 0], 1.0 / D, None, ALU.mult))
            v.tensor_reduce(stat[:, :, 2], X, AX, ALU.min)
            v.tensor_reduce(stat[:, :, 3], X, AX, ALU.max)
            dve_then(v.tensor_tensor(tmp7, X, X, ALU.mult))
            dve_then(v.tensor_reduce(c7[:, 0:NTL], tmp7, AX, ALU.add))
            dve_then(v.tensor_tensor(tmp7, X, per(stat[:, :, 0], D), ALU.subtract))
            dve_then(v.tensor_tensor(tmp7, tmp7, tmp7, ALU.mult))
            dve_then(v.tensor_reduce(c7[:, NTL:2 * NTL], tmp7, AX, ALU.add))
            dve_then(v.tensor_scalar(c7[:, NTL:2 * NTL], c7[:, NTL:2 * NTL], 1.0 / (D - 1), None, ALU.mult))
            dve_then(v.tensor_scalar(tmp7, X, -1e-6, None, ALU.is_gt))
            v.scalar_tensor_tensor(out=tmp7, in0=X, scalar=1e-6, in1=tmp7, op0=ALU.is_lt,
                                   op1=ALU.mult).then_inc(router_dve, 1)
            v.wait_ge(router_dve, ROUTER["squares"])
            dve_then(v.tensor_reduce(stat[:, :, 5], tmp7, AX, ALU.add))
            dve_then(v.tensor_scalar(stat[:, :, 5], stat[:, :, 5], 1.0 / D, None, ALU.mult))
            v.wait_ge(router_act, ROUTER["roots"])
            dve_then(v.tensor_copy(stat[:, :, 4], c7[:, 0:NTL]))
            v.tensor_copy(stat[:, :, 1], c7[:, NTL:2 * NTL]).then_inc(router_dve, 1)
            v.wait_ge(router_pe, ROUTER["stats_turned"])
            for b, n in flat(range(3), 6, NT):
                ins = v.tensor_copy(statT[0:6, 512 * b:512 * b + n], PS[0:6, b, 0:n])
            ins.then_inc(router_dve, 1)
            v.wait_ge(router_dve, ROUTER["stats_copied"])
            v.memset(PS[:, 0, :], 0.0).then_inc(router_dve, 1)
            v.wait_ge(router_pe, ROUTER["logits"])
            lg = PS[:, 0, 0:NTL * E7].rearrange("q (i e) -> q i e", i=NTL)
            pr, score, weight, sel, gt, eq, pre, rst, t8 = small
            dve_then(v.tensor_reduce(c7[:, 0:NTL], lg, AX, ALU.max))
            v.tensor_tensor(pr, lg, per(c7[:, 0:NTL], E7), ALU.subtract).then_inc(router_dve, 1)
            v.wait_ge(router_act, ROUTER["exponentials"])
            dve_then(v.tensor_reduce(c7[:, 0:NTL], pr, AX, ALU.add))
            dve_then(v.reciprocal(c7[:, NTL:2 * NTL], c7[:, 0:NTL]))
            dve_then(v.tensor_tensor(pr, pr, per(c7[:, NTL:2 * NTL], E7), ALU.mult))
            choose_dve(pr, NTL, E7, 2, sel, (m8_7, gt, eq, pre, c7[:, 2 * NTL:3 * NTL]), rst)
            dve_then(v.tensor_tensor(t8, pr, sel, ALU.mult))
            dve_then(v.tensor_reduce(c7[:, 0:NTL], t8, AX, ALU.add))
            dve_then(v.reciprocal(c7[:, NTL:2 * NTL], c7[:, 0:NTL]))
            dve_then(v.tensor_tensor(weight, t8, per(c7[:, NTL:2 * NTL], E7), ALU.mult))
            dve_then(v.tensor_scalar(gt, sel, 1.0, None, ALU.subtract))
            v.tensor_tensor(score, t8, gt, ALU.add).then_inc(router_dve, 1)
            v.wait_ge(router_pe, ROUTER["scores_turned"])
            for j, dst in enumerate((scoreT, weightT)):
                for b, n in flat(range(3), E7, NT):
                    ins = v.tensor_copy(dst[0:E7, 512 * b:512 * b + n], PS[0:E7, 1 + 3 * j + b, 0:n])
            dve_then(ins)
            S = lambda x: x[0:E7]
            cur, nxt = scoreT, wk0
            for _ in range(CAP_ROUNDS):
                dve_then(v.max(S(m8T), S(cur)))
                dve_then(v.match_replace(S(nxt), S(m8T), S(cur), -2.0))
                cur, nxt = nxt, (wk1 if nxt is wk0 else wk0)
            dve_then(v.max(S(m8T), S(cur)))
            thr = m8T[0:E7, CAP_REST - 1:CAP_REST]
            v.memset(S(nxt), 1.0)
            v.tensor_scalar(S(gtT), S(cur), thr, None, ALU.is_gt)
            dve_then(v.tensor_scalar(S(eqT), S(cur), thr, None, ALU.is_equal))
            v.tensor_tensor_scan(S(preT), S(nxt), S(eqT), 0.0, ALU.mult, ALU.add)
            dve_then(v.tensor_reduce(S(roomT), S(gtT), AX, ALU.add))
            dve_then(v.tensor_scalar(S(roomT), S(roomT), -1.0, float(CAP_REST), ALU.mult, ALU.add))
            dve_then(v.tensor_scalar(S(preT), S(preT), roomT[0:E7, 0:1], None, ALU.is_le))
            dve_then(v.tensor_tensor(S(eqT), S(eqT), S(preT), ALU.mult))
            dve_then(v.tensor_tensor(S(gtT), S(gtT), S(eqT), ALU.add))
            dve_then(v.tensor_tensor(S(eqT), S(cur), S(scoreT), ALU.not_equal))
            dve_then(v.tensor_tensor(S(gtT), S(gtT), S(eqT), ALU.add))
            dve_then(v.tensor_scalar(S(eqT), S(scoreT), -0.5, None, ALU.is_gt))
            dve_then(v.tensor_tensor(S(gtT), S(gtT), S(eqT), ALU.mult))
            dve_then(v.tensor_tensor_scan(S(preT), S(nxt), S(gtT), 0.0, ALU.mult, ALU.add))
            dve_then(v.tensor_tensor(S(preT), S(preT), S(gtT), ALU.mult))
            dve_then(v.tensor_scalar(S(slotT), S(preT), 1.0, None, ALU.subtract))
            v.tensor_tensor(S(keptW), S(weightT), S(gtT), ALU.mult).then_inc(router_dve, 1)
            for g in range(NG):
                v.wait_ge(r_gw, g + 1)
                v.tensor_scalar(gwT[:, g * GN:(g + 1) * GN], PS[0:16, g, 0:GN], 0.05, None,
                                ALU.mult).then_inc(r_gw_evac, 1)
            dve_then(v.memset(slot[:, NTL - 1, :], -1.0))
            v.wait_ge(router_pe, ROUTER["slots_turned"])
            v.tensor_copy(slot[:, 0:NTL - 1, :], PS[:, 4, 0:(NTL - 1) * E7].rearrange("q (i e) -> q i e", e=E7))
            dve_then(v.tensor_copy(slot[0:LASTN, NTL - 1, :], PS[0:LASTN, 4, (NTL - 1) * E7:NTL * E7]))
            v.memset(PS[:, 4, :], 0.0).then_inc(router_dve, 1)
            for q in range(4):
                if q:
                    v.wait_ge(xe_ready, q)
                for i in range(NTL):
                    ins = v.tensor_tensor(pick[:, i, :].rearrange("q (e c) -> q e c", c=CAP), bcast(const("iota"), 0, 8),
                                          per(slot[:, i, q * 8:(q + 1) * 8], CAP), ALU.is_equal)
                ins.then_inc(pick_ready, 1)
            v.wait_ge(router_dve, ROUTER["slots_copied"])
            ffn_begin_dve()

            def evacuate(x, e):
                v.wait_ge(ex_down, e + 1)
                rws = slice(x * SP, (x + 1) * SP)
                q = e // 2 if isinstance(e, int) else None
                v.tensor_copy(ye_row(rws, e, x), PS[rws, 4, 0:D]).then_inc(ex_out, 1)

            def ye_row(rws, e, x):
                if isinstance(e, int):
                    return ye[rws, e // 2, :]
                at = (e - x) * (D // 2)
                return ye_flat[rws, bass.ds(at, D)]

            ye_flat = ye.rearrange("q p n -> q (p n)")

            def body(i, first):
                for x in range(2):
                    e = 2 * i + x
                    v.wait_ge(ex_sg_ready, e + 1)
                    if not first:
                        v.wait_ge(ex_down, e - 1)
                    v.tensor_tensor(ex_h[:, x, :], ex_sg[:, x, :], PS[:, 2 * x + 1, 0:4 * CAP],
                                    ALU.mult).then_inc(ex_hid, 1)
                    if x:
                        evacuate(0, e - 1)
                    elif not first:
                        evacuate(1, e - 1)

            ex_loop(v, body)
            evacuate(1, E7 - 1)
            v.wait_ge(acc_begun, 4)
            for g in range(NG):
                for q in range(16):
                    n = g * 16 + q
                    v.wait_ge(wbc_ready, n + 1)
                    if n >= 2:
                        last = (n - 2) // 16
                        if (n - 2) % 16 == 15:
                            v.wait_ge(sc_ready, last + 1)
                        else:
                            v.wait_ge(r_sl_used, n - 1 - last)
                    v.scalar_tensor_tensor(out=place[:, q % 2, :], in0=PS[:, 2 * (q % 2), 0:GN],
                                           scalar=const("slotno"), in1=wbc[:, q % 2, :], op0=ALU.is_equal,
                                           op1=ALU.mult).then_inc(place_ready, 1)
                v.wait_ge(sc_ready, g + 1)
                sl = slice(g * GN, (g + 1) * GN)
                v.tensor_tensor(acc[:, :, sl], acc[:, :, sl], PS[:, 4 + 2 * (g % 2):6 + 2 * (g % 2), 0:GN],
                                ALU.add).then_inc(sc_added, 1)
            v.wait_ge(sc_added, NG)
            ffn_dve(7)
            ln_dve(7)


        yout = arena[:, 0:2560].rearrange("q (i n) -> q i n", i=10)
        turned = sem("turned")
        y_ready = sem("y_ready")
        out_rows = out.rearrange("a t d -> (a t) d")

        def finish_dve():
            v = nc.vector
            block_before(v, LAYERS)
            for k in range(KD):
                for g in range(NG):
                    ins = v.tensor_copy(compact(xc[:, k, g * GN:(g + 1) * GN]), hgroup(k, g))
            ins.then_inc(turned, 1)

        def finish_pe():
            pe = nc.tensor
            pe.wait_ge(turned, 1)
            for i, n in TILES:
                if i >= 8:
                    pe.wait_ge(y_ready, i - 7)
                for k in range(KD):
                    mm = pe.transpose(PS[0:n, i % 8, k * P:(k + 1) * P], xc[:, k, i * P:i * P + n], ident)
                mm.then_inc(turned, 1)

        def finish_act():
            for i, n in TILES:
                nc.scalar.wait_ge(turned, i + 2)
                nc.scalar.activation(yout[0:n, i, :], PS[0:n, i % 8, 0:D], ACT.Copy).then_inc(y_ready, 1)

        def finish_sync():
            for i, n in TILES:
                nc.sync.wait_ge(y_ready, i + 1)
                nc.sync.dma_start(out_rows[i * P:i * P + n, :], yout[0:n, i, :]).then_inc(all_stored, 16)
            nc.sync.wait_ge(all_stored, 16 * len(TILES))

        @block.sync
        def _(sp):
            start_sync()
            tok_sync()
            block0_loads()
            if LAYERS > 1: block1_sync()
            if LAYERS > 2: block2_sync()
            if LAYERS > 3: block3_sync()
            if LAYERS > 4: block4_sync()
            if LAYERS > 5: block5_sync()
            if LAYERS > 6: block6_sync()
            if LAYERS > 7: block7_sync()
            finish_sync()

        @block.gpsimd
        def _(pool):
            start_pool()
            if LAYERS > 3: block3_pool()
            if LAYERS > 5: block5_pool()
            if LAYERS > 4: block4_pool()

        @block.tensor
        def _(pe):
            start_engine(pe)
            tok_pe()
            block0_pe()
            if LAYERS > 1: block1_pe()
            if LAYERS > 2: block2_pe()
            if LAYERS > 3: block3_pe()
            if LAYERS > 4: block4_pe()
            if LAYERS > 5: block5_pe()
            if LAYERS > 6: block6_pe()
            if LAYERS > 7: block7_pe()
            finish_pe()

        @block.scalar
        def _(act):
            start_engine(act)
            block0_act()
            if LAYERS > 1: block1_act()
            if LAYERS > 2: block2_act()
            if LAYERS > 3: block3_act()
            if LAYERS > 4: block4_act()
            if LAYERS > 5: block5_act()
            if LAYERS > 6: block6_act()
            if LAYERS > 7: block7_act()
            finish_act()

        @block.vector
        def _(dve):
            start_engine(dve)
            tok_dve()
            block0_dve()
            if LAYERS > 1: block1_dve()
            if LAYERS > 2: block2_dve()
            if LAYERS > 3: block3_dve()
            if LAYERS > 4: block4_dve()
            if LAYERS > 5: block5_dve()
            if LAYERS > 6: block6_dve()
            if LAYERS > 7: block7_dve()
            finish_dve()


def rows(w):
    k = w.shape[0] // P
    return w.reshape(k, P, w.shape[1]).transpose(1, 0, 2).reshape(P, -1)


def wide_heads(w):
    return np.pad(w.reshape(w.shape[0], HEADS, HD), ((0, 0), (0, 0), (0, HD))).reshape(w.shape[0], 2 * D)


def columns(b):
    return b.reshape(-1, P).T


def units(wg, wu, wd):
    e, _, f = wg.shape
    u = f // P
    g = wg.reshape(e, KD, P, u, P).transpose(0, 2, 3, 1, 4).reshape(e, P, u, KD * P)
    p = wu.reshape(e, KD, P, u, P).transpose(0, 2, 3, 1, 4).reshape(e, P, u, KD * P)
    d = wd.reshape(e, u, P, D).transpose(0, 2, 1, 3)
    return np.concatenate([g, p, d], 3).reshape(e, P, u * UNIT)


def lay_out(i):
    t = lambda w: np.swapaxes(w, -1, -2)
    a = {"consts": CONSTS}
    x = i["x"].reshape(NG, GI, 3, 6, 16, 6, 16).transpose(0, 2, 4, 6, 1, 3, 5).reshape(NG, 6, P, -1)
    a["patches"] = x.transpose(0, 2, 1, 3).reshape(NG, P, -1)
    side = np.concatenate([i["L0_tok_pos_embedding"][0], i["L0_tok_b"][None], i["L0_tok_cls_token"][0]])
    a["tok_w"] = np.concatenate([rows(t(i["L0_tok_W"])), rows(t(side))], 1)
    a["attn0"] = np.concatenate([rows(wide_heads(t(i["L0_attn_Wq"]))), rows(wide_heads(t(i["L0_attn_Wk"]))),
                                 rows(t(i["L0_attn_Wv"])), rows(t(i["L0_attn_Wout"])), columns(i["L0_attn_bout"])], 1)
    a["gates"] = np.concatenate([rows(i["L0_ffn_Wr"]), rows(t(i["L1_ffn_w_gate"]))], 1)
    a["ffn0"] = units(i["L0_ffn_Wg"], i["L0_ffn_Wu"], i["L0_ffn_Wd"])
    a["splat"] = np.concatenate([rows(t(i["L1_attn_splat_positions"])), rows(i["L1_attn_Wv"]), rows(i["L1_attn_Wo"])], 1)
    a["splat_side"] = np.concatenate([i["L1_attn_splat_positions"], i["L1_attn_splat_log_scales"][:, None],
                                      i["L1_attn_splat_amplitudes"][:, None]], 1)
    half = lambda w: t(w).reshape(D, 2, P).transpose(1, 0, 2)
    a["ffn1"] = units(np.concatenate([t(i["L1_ffn_w1_e"]), half(i["L1_ffn_w1_s"])]),
                      np.concatenate([t(i["L1_ffn_w3_e"]), half(i["L1_ffn_w3_s"])]),
                      np.concatenate([t(i["L1_ffn_w2_e"]), t(i["L1_ffn_w2_s"]).reshape(2, P, D)]))
    a["slots"] = np.concatenate([rows(i["L2_attn_Wq"]), rows(i["L2_attn_Wk"]), rows(i["L2_attn_Wv"]), rows(i["L2_attn_Wo"]),
                                 rows(np.concatenate([i["L2_attn_Wf1"], i["L2_attn_Wg1"]], 1))], 1)
    a["slots_2"] = np.concatenate([i["L2_attn_Wf2"], np.pad(i["L2_attn_Wg2"], ((0, 0), (0, D)))], 0)
    a["norm_w"] = i["L2_attn_norm_w"][None]
    a["ffn2"] = units(t(i["L2_ffn_w_gate"])[None], t(i["L2_ffn_w_up"])[None], t(i["L2_ffn_w_down"])[None])[0]
    w, b = i["L3_attn_Wqkv_w"], i["L3_attn_Wqkv_b"]
    conv = i["L3_attn_conv_w"]
    wide = lambda v: columns(wide_heads(v[None])[0])
    a["attn3"] = np.concatenate(
        [rows(wide_heads(t(w[0:D]))), rows(wide_heads(t(w[D:2 * D]))), rows(t(w[2 * D:])), rows(t(i["L3_attn_out_w"]))]
        + [rows(wide_heads(t(conv[:, :, tap]))) for tap in range(3)]
        + [wide(b[0:D]), wide(b[D:2 * D]), wide(i["L3_attn_conv_b"]), columns(i["L3_attn_out_b"])], 1)
    a["v_bias"] = b[None, 2 * D:]
    up = t(i["L3_ffn_w_up"]).reshape(32, KD, P, 1024).transpose(0, 2, 1, 3).reshape(32, P, -1)
    down = t(i["L3_ffn_w_down"]).reshape(32, 4, P, D).transpose(0, 2, 1, 3).reshape(32, P, -1)
    a["experts"] = np.concatenate([up, down], 2)
    r1 = t(i["L3_ffn_r1_w"])
    a["router"] = np.concatenate([rows(r1[0:D]), t(i["L3_ffn_r2_w"]), i["L3_ffn_r1_b"][:, None]], 1)
    a["router_stats"] = r1[D:]
    a["pairs"] = PAIRS
    gate, upper = np.split(t(i["L3_ffn_a_up"]), 2, axis=-1)
    a["ffn3"] = units(gate, upper, t(i["L3_ffn_a_down"]))
    return {k: np.ascontiguousarray(v) for k, v in a.items()}


def kernel(**inputs):
    import concourse.bacc as bacc
    from concourse.bass_utils import run_bass_kernel_spmd

    arrays = {f"in_{k}": v for k, v in lay_out({k: np.asarray(v) for k, v in inputs.items()}).items()}
    nc = bacc.Bacc("TRN2", target_bir_lowering=False, num_devices=1)
    inp = {k[3:]: nc.dram_tensor(k, v.shape, mybir.dt.from_np(v.dtype), kind="ExternalInput").ap()
           for k, v in arrays.items()}
    out = nc.dram_tensor("out", (B, T, D), F32, kind="ExternalOutput").ap()
    scratch = nc.dram_tensor("scratch", (3, 32, NT), F32, kind="Internal").ap()
    tower(nc, inp, out, scratch)
    r = run_bass_kernel_spmd(nc, [arrays], core_ids=[0])
    return r.results[0]["out"]
```

```python
from contextlib import ExitStack

import numpy as np

import concourse.bass as bass
from concourse import mybir

F32 = mybir.dt.float32
I32 = mybir.dt.int32
U32 = mybir.dt.uint32
ALU = mybir.AluOpType
ACT = mybir.ActivationFunctionType
AX = mybir.AxisListType.X

P = 128
B = 32
T = 37
SP = 64
D = 256
KD = D // P
NG = 4
GI = B // NG
GN = GI * T
NT = B * T
NP = B // 2
HEADS = 16
HD = 16
CP = T + 2
UNIT = 6 * P
RING = 4 * UNIT
AR = 19600
LEVELS = 6
BLOCKS = [(LEVELS - 1 - e, 2 ** e, (T - 1 + 2 ** e) // 2 ** (e + 1), T // 2 ** (e + 1)) for e in range(LEVELS - 1, -1, -1)]
NJ = sum(b * n for _, b, n, _ in BLOCKS) + T % 2
NR = sum(max(0, min(b, T - c)) for _, b, _, _ in BLOCKS for c in range(b, T, 2 * b)) + T
LN_EPS = 1e-5

FFNS = {"L0": (8, 4), "L1": (18, 1), "L3": (16, 1)}

CONST = {}


def build_constants():
    parts = {}
    r = np.arange(P)
    t = r % SP
    img = r // SP
    valid = t < T
    parts["ident"] = np.eye(P)
    parts["ones"] = np.ones((P, P))
    parts["mean"] = np.full((P, P), 1.0 / D)
    parts["negi"] = np.where(np.arange(T)[None, :] <= t[:, None], 0.0, -1e30)
    lefts = [(lv, j, c) for lv, b_, _, _ in BLOCKS for c in range(b_, T + b_, 2 * b_) for j in range(c - b_, c)
             if c < T or (b_ == 1 and j < T)]
    rights = [(lv, t_, c) for lv, b_, _, _ in BLOCKS for c in range(b_, T, 2 * b_) for t_ in range(c, min(c + b_, T))]
    rights += [(LEVELS, t_, t_ + 1) for t_ in range(T)]
    assert len(lefts) == NJ and len(rights) == NR
    mask = np.zeros((P, NR))
    for x, (lv, j, c) in enumerate(lefts):
        for y, (lw, t_, d) in enumerate(rights):
            mask[x, y] = (lv == lw and c == d) if lw < LEVELS else (j == t_ and c == j + 1)
    assert (mask.sum(0)[-T:] == 1).all() and (mask.sum() == T * (T + 1) // 2)
    total = np.zeros((P, SP))
    for y, (lw, t_, d) in enumerate(rights):
        total[y, t_] = 1.0
    for i in range(2):
        mine = (img == i) & valid
        left = [mine & (t > j) & (t < c) for lv, j, c in lefts]
        right = [mine & (t >= c) & (t <= t_) for lv, t_, c in rights]
        parts["left%d" % i] = np.stack(left, 1)
        parts["right%d" % i] = np.stack(right, 1)
        parts["pick_left%d" % i] = np.stack([(img == i) & (t == j) for lv, j, c in lefts], 1)
        parts["pick_right%d" % i] = np.stack([(img == i) & (t == t_) for lv, t_, c in rights], 1)
    parts["pair_mask"] = mask
    parts["total"] = total
    parts["iota"] = np.broadcast_to(np.arange(46), (P, 46))
    parts["slotno"] = (r % SP)[:, None]
    two = np.zeros((P, 16))
    two[np.arange(32), np.arange(32) // 2] = 1.0
    parts["two"] = two
    parts["tril4"] = np.broadcast_to((np.arange(4)[None, :] < np.arange(4)[:, None]).reshape(1, 16), (P, 16))
    at = 0
    out = []
    for name, a in parts.items():
        a = np.asarray(a, np.float32)
        CONST[name] = (at, a.shape[1])
        at += a.shape[1]
        out.append(a)
    return np.ascontiguousarray(np.concatenate(out, 1))


CONSTS = build_constants()


def bcast(ap, at, n):
    dims = list(ap.ap)
    return bass.AP(ap.tensor, ap.offset, dims[:at + 1] + [[0, n]] + dims[at + 1:])


def tower(nc, inp, out, scratch):
    ctx = ExitStack()
    with ctx:
        def sb(name, shape, dt=F32):
            return ctx.enter_context(nc.sbuf_tensor(name, shape, dt))

        def sem(name):
            return ctx.enter_context(nc.semaphore(name))

        hP = sb("hP", [P, KD, B, SP])
        acc = sb("acc", [P, KD, NT])
        xc = sb("xc", [P, KD, NT])
        rs = sb("rs", [P, NT])
        aT = sb("aT", [P, KD, B, CP])
        ring = sb("ring", [P, 2, RING])
        cst = sb("cst", [P, CONSTS.shape[1]])
        wA = sb("wA", [P, 6656])
        arena = sb("arena", [P, AR])
        zcol = sb("zcol", [P, 1])
        epscol = sb("epscol", [P, 1])
        PS = ctx.enter_context(nc.psum_tensor("PS", [P, 8, 512], F32))

        def const(name):
            at, n = CONST[name]
            return cst[:, at:at + n]

        ident = const("ident")

        class carve:
            def __init__(self, tile, size):
                self.tile, self.size, self.at = tile, size, 0

            def __call__(self, n):
                self.at += n
                assert self.at <= self.size, (self.at, self.size)
                return self.tile[:, self.at - n:self.at]

        def hgroup(k, g):
            return hP[:, k, g * GI:(g + 1) * GI, 0:T]

        def hpair(k, p):
            return hP[:, k, 2 * p:2 * p + 2, :].rearrange("q a t -> q (a t)")

        def agroup(k, g):
            return aT[:, k, g * GI:(g + 1) * GI, 1:T + 1]

        def compact(ap):
            return ap.rearrange("q (a t) -> q a t", t=T)

        cst_loaded = sem("cst_loaded")
        wA_loaded = sem("wA_loaded")
        pads_zeroed = sem("pads_zeroed")
        dve_step = sem("dve_step")
        act_step = sem("act_step")
        res_ready = sem("res_ready")
        mean_ready = sem("mean_ready")
        xc_ready = sem("xc_ready")
        sq_ready = sem("sq_ready")
        var_ready = sem("var_ready")
        rstd_ready = sem("rstd_ready")
        h_ready = sem("h_ready")
        all_stored = sem("all_stored")

        block = ctx.enter_context(nc.Block())
        steps = {"dve": 0, "act": 0}

        def dve_then(ins):
            steps["dve"] += 1
            ins.then_inc(dve_step, 1)
            nc.vector.wait_ge(dve_step, steps["dve"])

        def act_then(ins):
            steps["act"] += 1
            ins.then_inc(act_step, 1)
            nc.scalar.wait_ge(act_step, steps["act"])

        def block_before(eng, n):
            eng.wait_ge(h_ready, NG * (n + 1))

        def ln_pe(layer):
            pe = nc.tensor
            if layer % 2:
                pe.wait_ge(ffn_acc, FFN_END[layer])
            else:
                pe.wait_ge(res_ready, NG * (layer // 2 + 1))
            for g in range(NG):
                for k in range(KD):
                    mm = pe.matmul(PS[:, g, 0:GN], const("mean"), acc[:, k, g * GN:(g + 1) * GN],
                                   start=(k == 0), stop=(k == KD - 1))
                mm.then_inc(mean_ready, 1)
            for g in range(NG):
                pe.wait_ge(sq_ready, NG * layer + g + 1)
                for k in range(KD):
                    mm = pe.matmul(PS[:, NG + g, 0:GN], const("mean"), acc[:, k, g * GN:(g + 1) * GN],
                                   start=(k == 0), stop=(k == KD - 1))
                mm.then_inc(var_ready, 1)

        def ln_dve(layer):
            v = nc.vector
            for g in range(NG):
                n = NG * layer + g + 1
                sl = slice(g * GN, (g + 1) * GN)
                v.wait_ge(mean_ready, n)
                v.tensor_tensor(xc[:, :, sl], acc[:, :, sl], bcast(PS[:, g, 0:GN], 0, KD),
                                ALU.subtract).then_inc(xc_ready, 1)
            for g in range(NG):
                n = NG * layer + g + 1
                sl = slice(g * GN, (g + 1) * GN)
                v.wait_ge(xc_ready, n)
                v.wait_ge(rstd_ready, n)
                for k in range(KD):
                    ins = v.tensor_tensor(hgroup(k, g), compact(xc[:, k, sl]), compact(rs[:, sl]), ALU.mult)
                ins.then_inc(h_ready, 1)

        def ln_act(layer):
            a = nc.scalar
            for g in range(NG):
                n = NG * layer + g + 1
                sl = slice(g * GN, (g + 1) * GN)
                a.wait_ge(xc_ready, n)
                a.activation(acc[:, :, sl], xc[:, :, sl], ACT.Square).then_inc(sq_ready, 1)
            for g in range(NG):
                n = NG * layer + g + 1
                sl = slice(g * GN, (g + 1) * GN)
                a.wait_ge(var_ready, n)
                ins = a.activation(rs[:, sl], PS[:, NG + g, 0:GN], ACT.Ln, bias=epscol[:, 0:1])
            act_then(ins)
            for g in range(NG):
                sl = slice(g * GN, (g + 1) * GN)
                a.activation(rs[:, sl], rs[:, sl], ACT.Exp, scale=-0.5).then_inc(rstd_ready, 1)

        def per(ap, n):
            return bass.AP(ap.tensor, ap.offset, list(ap.ap) + [[0, n]])

        def start_sync():
            nc.sync.dma_start(cst[:, :], inp["consts"]).then_inc(cst_loaded, 16)

        def start_pool():
            pool = nc.gpsimd
            pool.memset(hP[:, :, :, :], 0.0).then_inc(pads_zeroed, 1)
            pool.memset(aT[:, :, :, :], 0.0).then_inc(pads_zeroed, 1)
            pool.memset(zcol[:, :], 0.0).then_inc(pads_zeroed, 1)
            pool.memset(epscol[:, :], LN_EPS).then_inc(pads_zeroed, 1)

        def start_engine(eng):
            eng.wait_ge(cst_loaded, 16)
            eng.wait_ge(pads_zeroed, 4)

        GT = GI * (T - 1)
        tw = carve(wA, 6656)
        tok_w = tw(6 * D).rearrange("q (k n) -> q k n", k=6)
        tok_side = tw(2 * (T + 2)).rearrange("q (k n) -> q k n", k=2)
        tok_pos = arena[:, 4 * 6 * GT:4 * 6 * GT + 2 * T].rearrange("q (k n) -> q k n", k=2)
        tok_x = arena[:, 0:4 * 6 * GT].rearrange("q (g k n) -> q g k n", g=4, k=6)
        x_loaded = [sem(f"x_loaded{g}") for g in range(NG)]
        tok_ready = sem("tok_ready")

        def tok_sync():
            sp = nc.sync
            sp.dma_start(wA[:, 0:6 * D + 2 * (T + 2)], inp["tok_w"]).then_inc(wA_loaded, 16)
            for g in range(NG):
                sp.dma_start(tok_x[:, g].rearrange("q k n -> q (k n)"), inp["patches"][g]).then_inc(x_loaded[g], 16)

        def tok_pe():
            pe = nc.tensor
            pe.wait_ge(wA_loaded, 16)
            for g in range(NG):
                pe.wait_ge(x_loaded[g], 16)
                for c in range(KD):
                    for k in range(6):
                        mm = pe.matmul(PS[:, 2 * g + c, 0:GT], tok_w[:, k, c * P:(c + 1) * P], tok_x[:, g, k, :],
                                       start=(k == 0), stop=(k == 5))
                mm.then_inc(tok_ready, 1)

        def tok_dve():
            v = nc.vector
            v.wait_ge(wA_loaded, 16)
            for c in range(KD):
                v.tensor_scalar(tok_pos[:, c, 1:T], tok_side[:, c, 1:T], tok_side[:, c, T:T + 1], None, ALU.add)
                dve_then(v.tensor_scalar(tok_pos[:, c, 0:1], tok_side[:, c, 0:1], tok_side[:, c, T + 1:T + 2], None,
                                         ALU.add))
            for g in range(NG):
                v.wait_ge(tok_ready, g + 1)
                for c in range(KD):
                    hg = hP[:, c, g * GI:(g + 1) * GI, :]
                    v.tensor_copy(hg[:, :, 0:1], bcast(tok_pos[:, c, 0:1], 0, GI))
                    ins = v.tensor_tensor(hg[:, :, 1:T], PS[:, 2 * g + c, 0:GT].rearrange("q (a t) -> q a t", a=GI),
                                          bcast(tok_pos[:, c, 1:T], 0, GI), ALU.add)
                ins.then_inc(h_ready, 1)

        proj_ready = sem("proj_ready")
        proj_count = {"n": 0}

        def project_pe(w, ready):
            pe = nc.tensor
            ready(pe)
            for g in range(NG):
                for c in range(KD):
                    for k in range(KD):
                        mm = pe.matmul(PS[:, 2 * g + c, 0:GN], w[:, k, c * P:(c + 1) * P], agroup(k, g),
                                       start=(k == 0), stop=(k == KD - 1))
                mm.then_inc(proj_ready, 1)

        def project_dve(bias):
            v = nc.vector
            for g in range(NG):
                proj_count["n"] += 1
                v.wait_ge(proj_ready, proj_count["n"])
                for c in range(KD):
                    ins = v.scalar_tensor_tensor(out=compact(acc[:, c, g * GN:(g + 1) * GN]),
                                                 in0=compact(PS[:, 2 * g + c, 0:GN]), scalar=bias[c],
                                                 in1=hgroup(c, g), op0=ALU.add, op1=ALU.add)
                ins.then_inc(res_ready, 1)

        ma = carve(arena, AR)
        q_s = ma(4 * NT).rearrange("q (c n) -> q c n", c=4)
        k_s = ma(4 * NT).rearrange("q (c n) -> q c n", c=4)
        v_s = ma((B + 1) * 8 * 17).rearrange("q (s h d) -> q s h d", s=B + 1, h=8)
        p_s = ma(2 * HEADS * SP).rearrange("q (s h j) -> q s h j", s=2, h=HEADS)
        pt_s = ma(2 * 8 * 2 * T).rearrange("q (s m i t) -> q s m i t", s=2, m=8, i=2)
        o_s = ma(2 * D).rearrange("q (s n) -> q s n", s=2)
        mx2_s = ma(2 * HEADS).rearrange("q (s h) -> q s h", s=2)
        rec_s = ma(HEADS)
        qk_evac = sem("qk_evac")
        qk_ready = sem("qk_ready")
        v_ready = sem("v_ready")
        v_evac = sem("v_evac")
        pads_set = sem("pads_set")
        s_ready = sem("s_ready")
        shifted = sem("shifted")
        p_ready = sem("p_ready")
        turned_ready = sem("turned_ready")
        pt_ready = sem("pt_ready")
        o_ready = sem("o_ready")
        on_ready = sem("on_ready")
        ot_ready = sem("ot_ready")
        aT_ready = sem("aT_ready")
        row_tile_done = sem("row_tile_done")
        tile_count = {"n": 0}
        NQK = 8 * NG
        NV = B + 1

        def heads_pe(m, wq, wk, wv):
            pe = nc.tensor
            n, nv = 0, 0
            for g in range(NG):
                for w in (wq, wk):
                    for c in range(4):
                        if n >= 4:
                            pe.wait_ge(qk_evac, m * NQK + n - 3)
                        for k in range(KD):
                            mm = pe.matmul(PS[:, n % 4, 0:GN], w[:, k, c * P:(c + 1) * P], hgroup(k, g),
                                           start=(k == 0), stop=(k == KD - 1))
                        mm.then_inc(qk_ready, 1)
                        n += 1
                for _ in range(GI if g < NG - 1 else GI + 1):
                    if nv >= 4:
                        pe.wait_ge(v_evac, m * NV + nv - 3)
                    for k in range(KD):
                        if nv == 0:
                            left, rws = hP[:, k, 0, :], slice(SP, P)
                        elif nv == B:
                            left, rws = hP[:, k, B - 1, :], slice(0, SP)
                        else:
                            left, rws = hP[:, k, nv - 1:nv + 1, :].rearrange("q a t -> q (a t)"), slice(0, P)
                        mm = pe.matmul(PS[rws, 4 + nv % 4, 0:D], left, wv[:, k, :], start=(k == 0),
                                       stop=(k == KD - 1))
                    mm.then_inc(v_ready, 1)
                    nv += 1

        def heads_act(m, qbias, kbias):
            a = nc.scalar
            n = 0
            for g in range(NG):
                for dst, bias, scale in ((q_s, qbias, 0.25), (k_s, kbias, 1.0)):
                    for c in range(4):
                        a.wait_ge(qk_ready, m * NQK + n + 1)
                        a.activation(dst[:, c, g * GN:(g + 1) * GN], PS[:, n % 4, 0:GN], ACT.Identity,
                                     bias=bias[c], scale=scale).then_inc(qk_evac, 1)
                        n += 1

        def heads_dve(m, vbias):
            v = nc.vector
            v.memset(v_s[:, :, :, 16:17], 1.0)
            v.memset(p_s[:, :, :, T:SP], 0.0).then_inc(pads_set, 1)
            for nv in range(NV):
                v.wait_ge(v_ready, m * NV + nv + 1)
                for e in range(2):
                    if (nv, e) in ((0, 0), (B, 1)):
                        continue
                    rws = slice(e * SP, (e + 1) * SP)
                    mine = lambda x: x[rws].rearrange("q (c e r d) -> q c e r d", c=2, e=2, r=4)[:, :, e]
                    src, dst = mine(PS[:, 4 + nv % 4, 0:D]), v_s[rws, nv, :, 0:16].rearrange("q (c r) d -> q c r d", c=2)
                    if vbias is None:
                        ins = v.tensor_copy(dst, src)
                    else:
                        ins = v.tensor_tensor(dst, src, mine(vbias), ALU.add)
                ins.then_inc(v_evac, 1)

        def head(ap, h, img):
            return ap[32 * (h % 4):32 * (h % 4) + HD, h // 4, img * T:(img + 1) * T]

        def attend_pe(a, m):
            pe = nc.tensor
            pe.wait_ge(qk_evac, NQK * (m + 1) + (16 if a == 2 else 0))
            pe.wait_ge(v_evac, NV * (m + 1))
            pe.wait_ge(pads_set, m + 1 + a + 1)

            def scores(p, between=None):
                n = a * NP + p
                if p >= 2:
                    pe.wait_ge(shifted, n - 1)
                for r in (0, 2, 1, 3):
                    if r % 2:
                        pe.wait_ge(row_tile_done, tile_count["n"] - 1)
                    for i in range(2):
                        for c in range(4):
                            at = ((r % 2) * 4 + c) * T
                            mm = pe.matmul(PS[i * SP:i * SP + T, 2 * (p % 2) + r // 2, at:at + T],
                                           head(q_s, 4 * c + r, 2 * p + i), head(k_s, 4 * c + r, 2 * p + i),
                                           start=True, stop=True)
                    if r != 3:
                        mm.then_inc(row_tile_done, 1)
                        tile_count["n"] += 1
                    if r == 2 and between:
                        between()
                mm.then_inc(s_ready, 1)

            def turn_scores(p):
                n = a * NP + p
                pe.wait_ge(p_ready, n + 1)
                if p:
                    pe.wait_ge(pt_ready, n)
                for x in range(8):
                    mm = pe.transpose(PS[:, 4 + x // 4, (x % 4) * P:(x % 4 + 1) * P],
                                      p_s[:, p % 2, 2 * x:2 * x + 2, :].rearrange("q h j -> q (h j)"), ident)
                mm.then_inc(turned_ready, 1)

            def values(p):
                n = a * NP + p
                pe.wait_ge(pt_ready, n + 1)
                if p:
                    pe.wait_ge(on_ready, n)
                    pe.wait_ge(aT_ready, n)
                for e in range(2):
                    rows = slice(e * SP, e * SP + T)
                    for i in range(2):
                        for c2 in range(2):
                            for r in range(4):
                                at = (c2 * 4 + r) * 17
                                mm = pe.matmul(PS[i * SP:i * SP + T, 6 + e, at:at + 17],
                                               pt_s[rows, p % 2, 2 * r + c2, i, :],
                                               v_s[rows, 2 * p + i - e + 1, c2 * 4 + r, :], start=True, stop=True)
                mm.then_inc(o_ready, 1)

            def turn(p):
                n = a * NP + p
                pe.wait_ge(on_ready, n + 1)
                for c in range(KD):
                    mm = pe.transpose(PS[:, 6, 256 + c * P:256 + (c + 1) * P], o_s[:, p % 2, c * P:(c + 1) * P],
                                      ident)
                mm.then_inc(ot_ready, 1)

            scores(0)
            scores(1)
            for p in range(NP):
                turn_scores(p)
                before = (lambda: turn(p - 1)) if p else None
                if p + 2 < NP:
                    scores(p + 2, before)
                elif before:
                    before()
                values(p)
            turn(NP - 1)

        def attend_dve(a, m):
            v = nc.vector
            v.wait_ge(qk_evac, NQK * (m + 1) + (16 if a == 2 else 0))
            v.wait_ge(v_evac, NV * (m + 1))
            v.memset(PS[:, 0:4, :], 1.0)
            v.memset(PS[:, 6:8, :], 1.0).then_inc(pads_set, 1)
            v.wait_ge(pads_set, m + 1 + a + 1)

            def shift(p):
                n = a * NP + p
                src = PS[:, 2 * (p % 2):2 * (p % 2) + 2, 0:8 * T].rearrange("q b (h j) -> q b h j", h=8)
                dst = p_s[:, p % 2, :, 0:T]
                mx = mx2_s[:, p % 2]
                v.wait_ge(s_ready, n + 1)
                if p >= 2:
                    v.wait_ge(shifted, n - 1)
                    v.wait_ge(turned_ready, n - 1)
                if a:
                    dve_then(v.tensor_tensor(dst.rearrange("q (b h) j -> q b h j", b=2), src,
                                             bcast(bcast(const("negi"), 0, 8), 0, 2), ALU.add))
                    dve_then(v.tensor_reduce(mx, dst, AX, ALU.max))
                    v.tensor_tensor(dst, dst, per(mx, T), ALU.subtract).then_inc(shifted, 1)
                else:
                    dve_then(v.tensor_reduce(mx.rearrange("q (b h) -> q b h", b=2), src, AX, ALU.max))
                    v.tensor_tensor(dst.rearrange("q (b h) j -> q b h j", b=2), src,
                                    per(mx.rearrange("q (b h) -> q b h", b=2), T),
                                    ALU.subtract).then_inc(shifted, 1)

            def normalize(p):
                n = a * NP + p
                v.wait_ge(o_ready, n + 1)
                if n:
                    v.wait_ge(on_ready, n)
                o = PS[:, 6:8, 0:8 * 17].rearrange("q e (h d) -> q e h d", h=8)
                rec = rec_s.rearrange("q (e h) -> q e h", e=2)
                dve_then(v.reciprocal(rec, o[:, :, :, 16]))
                if p >= 2:
                    v.wait_ge(ot_ready, n - 1)
                for e in range(2):
                    out = o_s[:, p % 2].rearrange("q (c e r d) -> q c e r d", c=2, e=2, r=4)[:, :, e]
                    ins = v.tensor_tensor(out, o[:, e, :, 0:16].rearrange("q (c r) d -> q c r d", c=2),
                                          per(rec[:, e].rearrange("q (c r) -> q c r", c=2), 16), ALU.mult)
                ins.then_inc(on_ready, 1)

            shift(0)
            shift(1)
            for p in range(NP):
                if p + 2 < NP:
                    shift(p + 2)
                normalize(p)

        def attend_act(a):
            s = nc.scalar

            def exponent(p):
                s.wait_ge(shifted, a * NP + p + 1)
                s.activation(p_s[:, p % 2, :, 0:T], p_s[:, p % 2, :, 0:T], ACT.Exp).then_inc(p_ready, 1)

            def evacuate(p):
                s.wait_ge(ot_ready, a * NP + p + 1)
                src = PS[:, 6, 256:512].rearrange("q (c i t) -> q c i t", c=2, i=2)
                for c in range(KD):
                    ins = s.activation(aT[:, c, 2 * p:2 * p + 2, 1:T + 1], src[:, c, :, 0:T], ACT.Copy)
                ins.then_inc(aT_ready, 1)

            exponent(0)
            for p in range(NP):
                n = a * NP + p
                s.wait_ge(turned_ready, n + 1)
                if p >= 2:
                    s.wait_ge(o_ready, n - 1)
                src = PS[:, 4:6, :].rearrange("q b (m i t) -> q (b m) i t", m=4, i=2)
                s.activation(pt_s[:, p % 2], src[:, :, :, 0:T], ACT.Copy).then_inc(pt_ready, 1)
                if p:
                    evacuate(p - 1)
                if p + 1 < NP:
                    exponent(p + 1)
            evacuate(NP - 1)

        w0 = carve(wA, 6656)
        a0_wq = w0(1024).rearrange("q (k n) -> q k n", k=2)
        a0_wk = w0(1024).rearrange("q (k n) -> q k n", k=2)
        a0_wv = w0(512).rearrange("q (k n) -> q k n", k=2)
        a0_wo = w0(512).rearrange("q (k n) -> q k n", k=2)
        a0_b = w0(2)

        def block0_loads():
            block_before(nc.sync, 0)
            nc.sync.dma_start(wA[:, 0:w0.at], inp["attn0"]).then_inc(wA_loaded, 16)

        def block0_pe():
            block_before(nc.tensor, 0)
            nc.tensor.wait_ge(wA_loaded, 32)
            heads_pe(0, a0_wq, a0_wk, a0_wv)
            attend_pe(0, 0)
            project_pe(a0_wo, lambda pe: pe.wait_ge(aT_ready, NP))
            ln_pe(0)

        def block0_act():
            block_before(nc.scalar, 0)
            heads_act(0, [zcol[:, 0:1]] * 4, [zcol[:, 0:1]] * 4)
            attend_act(0)
            ln_act(0)

        def block0_dve():
            block_before(nc.vector, 0)
            heads_dve(0, None)
            attend_dve(0, 0)
            project_dve([a0_b[:, c:c + 1] for c in range(KD)])
            ln_dve(0)

        fa = carve(arena, AR)
        hact = fa(2 * GN).rearrange("q (s n) -> q s n", s=2)
        sg = fa(2 * GN).rearrange("q (s n) -> q s n", s=2)
        tmp = fa(4 * GN).rearrange("q (s c n) -> q s c n", s=2, c=2)
        cb = fa(2 * NT).rearrange("q (s n) -> q s n", s=2)
        FA = fa.at
        ffn_up = sem("ffn_up")
        ffn_sg = sem("ffn_sg")
        ffn_hid = sem("ffn_hid")
        ffn_down = sem("ffn_down")
        ffn_out = sem("ffn_out")
        ffn_acc = sem("ffn_acc")
        ring_full = [sem(f"ring_full{i}") for i in range(2)]
        cb_full = [sem(f"cb_full{i}") for i in range(2)]
        acc_begun = sem("acc_begun")
        FFN = {1: (8, 4, "ffn0", 0), 3: (18, 1, "ffn1", 1), 5: (2, 3, None, None), 7: (16, 1, "ffn3", 2)}
        FFN_STEP, FFN_OG, FFN_RING, FFN_CB, FFN_END = {}, {}, {}, {}, {}
        count = [0, 0, 0, 0]
        for n, (e, u, w, r) in FFN.items():
            FFN_STEP[n], FFN_OG[n], FFN_RING[n], FFN_CB[n] = count
            count[0] += e * NG * u
            count[1] += e * NG
            count[2] += e // 2 if w else 0
            count[3] += e // 2 if w else 0
            FFN_END[n] = count[1]

        def ffn_order(n):
            return [(s, g, u) for s in range(2) for g in range(NG) for u in range(FFN[n][1])]

        def ffn_loop(eng, n, body):
            body(0, True)
            if FFN[n][0] > 2:
                with eng.Fori(1, FFN[n][0] // 2) as i:
                    body(i, False)

        def ffn_sync(n, wait_combine):
            sp = nc.sync
            E, U, w, r = FFN[n]
            S = 2 * NG * U

            def weights(i, s):
                if n > 1 or not isinstance(i, int):
                    before = FFN_STEP[n] if isinstance(i, int) else FFN_STEP[n] + i * S - S + (s + 1) * NG * U
                    sp.wait_ge(ffn_down, before)
                src = inp[w][bass.ds(2 * i + s, 1)].rearrange("a q n -> q (a n)")
                sp.dma_start(ring[:, s, 0:U * UNIT], src).then_inc(ring_full[s], 16)

            def combine(i, s):
                if not isinstance(i, int):
                    sp.wait_ge(ffn_out, FFN_OG[n] + i * 2 * NG - 2 * NG + (s + 1) * NG)
                row = scratch[r, bass.ds(2 * i + s, 1), :]
                sp.dma_start(cb[:, s, :], row.broadcast_to([P, NT])).then_inc(cb_full[s], 16)

            for s in range(2):
                weights(0, s)
            wait_combine(sp)
            for s in range(2):
                combine(0, s)
            with sp.Fori(1, E // 2) as i:
                for s in range(2):
                    weights(i, s)
                    combine(i, s)

        def ffn_pe(n, weights_ready=None):
            pe = nc.tensor
            U = FFN[n][1]
            order = ffn_order(n)
            S = len(order)

            def body(i, first):
                base = FFN_STEP[n] + i * S
                ogs = FFN_OG[n] + i * 2 * NG

                def out_product(x, step, ogs):
                    s, g, u = order[x]
                    pe.wait_ge(ffn_hid, step + 1)
                    if u == 0 and not (isinstance(ogs, int) and ogs + s * NG + g < 2):
                        pe.wait_ge(ffn_out, ogs + s * NG + g - 1)
                    for c in range(KD):
                        at = u * UNIT + 4 * P + c * P
                        mm = pe.matmul(PS[:, 4 + 2 * (g % 2) + c, 0:GN], ring[:, s, at:at + P], hact[:, x % 2, :],
                                       start=(u == 0), stop=(u == U - 1))
                    mm.then_inc(ffn_down, 1)

                for x, (s, g, u) in enumerate(order):
                    step = base + x
                    if g == 0 and u == 0:
                        if weights_ready:
                            weights_ready(pe)
                        else:
                            pe.wait_ge(ring_full[s], 16 * (FFN_RING[n] + i + 1))
                    if not (isinstance(step, int) and step < 2):
                        pe.wait_ge(ffn_hid, step - 1)
                    for b in range(2):
                        for k in range(KD):
                            at = u * UNIT + (2 * b + k) * P
                            mm = pe.matmul(PS[:, 2 * (x % 2) + b, 0:GN], ring[:, s, at:at + P], hgroup(k, g),
                                           start=(k == 0), stop=(k == KD - 1))
                    mm.then_inc(ffn_up, 1)
                    if x:
                        out_product(x - 1, step - 1, ogs)
                    elif not first:
                        out_product(S - 1, step - 1, ogs - 2 * NG)
                body.last = lambda: out_product(S - 1, FFN_STEP[n] + FFN[n][0] // 2 * S - 1,
                                                FFN_END[n] - 2 * NG)

            ffn_loop(pe, n, body)
            body.last()

        def ffn_act(n):
            a = nc.scalar
            order = ffn_order(n)

            def body(i, first):
                for x in range(len(order)):
                    step = FFN_STEP[n] + i * len(order) + x
                    a.wait_ge(ffn_up, step + 1)
                    if not (isinstance(step, int) and step < 2):
                        a.wait_ge(ffn_hid, step - 1)
                    a.activation(sg[:, x % 2, :], PS[:, 2 * (x % 2), 0:GN], ACT.Silu).then_inc(ffn_sg, 1)

            ffn_loop(a, n, body)

        def ffn_begin_dve():
            v = nc.vector
            for k in range(KD):
                ins = v.tensor_copy(acc[:, k, :].rearrange("q (a t) -> q a t", t=T), hP[:, k, :, 0:T])
            ins.then_inc(acc_begun, 1)

        def ffn_dve(n):
            v = nc.vector
            E, U, w, r = FFN[n]
            order = ffn_order(n)
            S = len(order)
            v.wait_ge(acc_begun, (n + 1) // 2)

            def body(i, first):
                def hidden(x):
                    step = FFN_STEP[n] + i * S + x
                    v.wait_ge(ffn_sg, step + 1)
                    if not (isinstance(step, int) and step < 2):
                        v.wait_ge(ffn_down, step - 1)
                    v.tensor_tensor(hact[:, x % 2, :], sg[:, x % 2, :], PS[:, 2 * (x % 2) + 1, 0:GN],
                                    ALU.mult).then_inc(ffn_hid, 1)

                def add_output(s, g, i, peeled):
                    og = FFN_OG[n] + i * 2 * NG + s * NG + g
                    sl = slice(g * GN, (g + 1) * GN)
                    v.wait_ge(ffn_down, FFN_STEP[n] + i * S + (s * NG + g + 1) * U)
                    if not (isinstance(og, int) and og < 2):
                        v.wait_ge(ffn_acc, og - 1)
                    src = PS[:, 4 + 2 * (g % 2):6 + 2 * (g % 2), 0:GN]
                    if r is None:
                        if s:
                            v.wait_ge(ffn_acc, og - 3)
                        v.tensor_tensor(tmp[:, g % 2], src, acc[:, :, sl], ALU.add).then_inc(ffn_out, 1)
                        v.wait_ge(ffn_out, og + 1)
                        v.tensor_copy(acc[:, :, sl], tmp[:, g % 2]).then_inc(ffn_acc, 1)
                        return
                    if g == 0:
                        v.wait_ge(cb_full[s], 16 * (FFN_CB[n] + i + 1))
                    v.tensor_tensor(tmp[:, g % 2], src, bcast(cb[:, s, sl], 0, KD), ALU.mult).then_inc(ffn_out, 1)
                    v.wait_ge(ffn_out, og + 1)
                    v.tensor_tensor(acc[:, :, sl], acc[:, :, sl], tmp[:, g % 2], ALU.add).then_inc(ffn_acc, 1)

                for x, (s, g, u) in enumerate(order):
                    hidden(x)
                    if u == 0:
                        if x:
                            add_output(*order[x - 1][:2], i, first)
                        elif not first:
                            add_output(1, NG - 1, i - 1, False)
                body.last = lambda: add_output(1, NG - 1, E // 2 - 1, False)

            ffn_loop(v, n, body)
            body.last()

        def choose_dve(vals, R, E, k, sel, work, reset, before=None):
            v = nc.vector
            m8, gt, eq, pre, room = work
            v.memset(reset, 1.0).then_inc(dve_step, 1)
            steps["dve"] += 1
            for i in range(R):
                ins = v.max(m8[:, i, :], vals[:, i, :])
            dve_then(ins)
            dve_then(v.memset(reset[:, :, 0:1], 0.0))
            thr = per(m8[:, :, k - 1], E)
            v.tensor_tensor(eq, vals, thr, ALU.is_equal)
            dve_then(v.tensor_tensor(gt, vals, thr, ALU.is_gt))
            v.tensor_tensor_scan(pre.rearrange("q a b -> q (a b)"), reset.rearrange("q a b -> q (a b)"),
                                 eq.rearrange("q a b -> q (a b)"), 0.0, ALU.mult, ALU.add)
            dve_then(v.tensor_reduce(room, gt, AX, ALU.add))
            dve_then(v.tensor_scalar(room, room, -1.0, float(k), ALU.mult, ALU.add))
            dve_then(v.tensor_tensor(pre, pre, per(room, E), ALU.is_le))
            dve_then(v.tensor_tensor(eq, eq, pre, ALU.mult))
            dve_then(v.tensor_tensor(sel, gt, eq, ALU.add))

        gate_w = sb("gate_w", [P, 48])
        gate_loaded = sem("gate_loaded")
        gate_ready = sem("gate_ready")
        gate_shifted = sem("gate_shifted")
        gate_exp = sem("gate_exp")
        comb_ready = sem("comb_ready")
        combT_ready = sem("combT_ready")
        combT_copied = sem("combT_copied")
        comb_stored = sem("comb_stored")
        ga = carve(arena, AR)
        ga(FA)
        g_lg, g_gt, g_eq, g_pre, g_sel, g_rst, g_e, g_c = [ga(256) for _ in range(8)]
        g_m8 = ga(128).rearrange("q (a b) -> q a b", b=8)
        g_room, g_sum, g_rec = ga(64), ga(64), ga(64)
        g_T = ga(NT)

        def tile3(ap, E):
            return ap[:, 0:16 * E].rearrange("q (a b) -> q a b", b=E)

        def logits_pe(w, E):
            pe = nc.tensor
            for p in range(NP):
                for k in range(KD):
                    mm = pe.matmul(PS[:, 0, p * E:(p + 1) * E], hpair(k, p), w[:, k, :], start=(k == 0),
                                   stop=(k == KD - 1))
            mm.then_inc(gate_ready, 1)

        def combine_pe(c, E):
            pe = nc.tensor
            pe.wait_ge(comb_ready, c + 1)
            for p in range(NP):
                mm = pe.transpose(PS[0:E, p // 4, (p % 4) * P:(p % 4 + 1) * P], tile3(g_c, E)[:, p, :], ident)
            mm.then_inc(combT_ready, 1)

        def combine_dve(c, E):
            v = nc.vector
            v.wait_ge(combT_ready, c + 1)
            src = PS[0:E, 0:4, :].rearrange("q b (a t) -> q (b a) t", t=SP)[:, :, 0:T]
            v.tensor_copy(g_T[0:E].rearrange("q (a t) -> q a t", t=T), src).then_inc(combT_copied, 1)

        def combine_sync(c, E):
            nc.sync.wait_ge(combT_copied, c + 1)
            nc.sync.dma_start(scratch[c, 0:E, :], g_T[0:E]).then_inc(comb_stored, 16)
            nc.sync.wait_ge(comb_stored, 16 * (c + 1))

        g0_w = gate_w[:, 0:16].rearrange("q (k e) -> q k e", k=2)
        g1_w = gate_w[:, 16:48].rearrange("q (k e) -> q k e", k=2)

        def block1_sync():
            nc.sync.dma_start(gate_w[:, :], inp["gates"]).then_inc(gate_loaded, 16)
            ffn_sync(1, lambda sp: combine_sync(0, 8))

        def block1_pe():
            block_before(nc.tensor, 1)
            nc.tensor.wait_ge(gate_loaded, 16)
            logits_pe(g0_w, 8)
            combine_pe(0, 8)
            nc.tensor.wait_ge(combT_copied, 1)
            ffn_pe(1)
            ln_pe(1)

        def block1_act():
            a = nc.scalar
            block_before(a, 1)
            a.wait_ge(gate_shifted, 1)
            a.activation(tile3(g_e, 8), tile3(g_e, 8), ACT.Exp).then_inc(gate_exp, 1)
            ffn_act(1)
            ln_act(1)

        def block1_dve():
            v = nc.vector
            block_before(v, 1)
            ffn_begin_dve()
            v.wait_ge(gate_ready, 1)
            lg, gt, eq, pre, sel, rst, e, c = [tile3(x, 8) for x in (g_lg, g_gt, g_eq, g_pre, g_sel, g_rst, g_e, g_c)]
            dve_then(v.tensor_copy(lg, PS[:, 0, 0:128].rearrange("q (a b) -> q a b", b=8)))
            choose_dve(lg, 16, 8, 2, sel, (g_m8, gt, eq, pre, g_room[:, 0:16]), rst)
            v.tensor_tensor(e, lg, per(g_m8[:, :, 0], 8), ALU.subtract).then_inc(gate_shifted, 1)
            v.wait_ge(gate_exp, 1)
            dve_then(v.tensor_tensor(c, e, sel, ALU.mult))
            dve_then(v.tensor_reduce(g_sum[:, 0:16], c, AX, ALU.add))
            dve_then(v.reciprocal(g_rec[:, 0:16], g_sum[:, 0:16]))
            v.tensor_tensor(c, c, per(g_rec[:, 0:16], 8), ALU.mult).then_inc(comb_ready, 1)
            combine_dve(0, 8)
            ffn_dve(1)
            ln_dve(1)

        S2 = 64
        w2 = carve(wA, 6656)
        sp_pT = w2(2 * S2).rearrange("q (k n) -> q k n", k=2)
        sp_wv = w2(2 * D).rearrange("q (k n) -> q k n", k=2)
        sp_wo = w2(2 * D).rearrange("q (k n) -> q k n", k=2)
        sp_p = w2(D + 2)
        s2 = carve(arena, AR)
        sp_pm2 = s2(2 * S2).rearrange("q (k n) -> q k n", k=2)
        sp_sq = s2(2 * NT).rearrange("q (k n) -> q k n", k=2)
        sp_raw = s2(NT)
        sp_g = s2(B * SP).rearrange("q (a t) -> q a t", t=SP)
        sp_v = s2(NP * D).rearrange("q (p n) -> q p n", p=NP)
        sp_gt = s2(2 * S2).rearrange("q (s n) -> q s n", s=2)
        sp_m = s2(2 * 2 * D).rearrange("q (s i n) -> q s i n", s=2, i=2)
        sp_cb = s2(2 * 2 * P).rearrange("q (s i n) -> q s i n", s=2, i=2)
        sp_den = s2(2 * 2 * T).rearrange("q (s n) -> q s n", s=2)
        sp_c, sp_tmp, sp_col = s2(B), s2(D), s2(8)
        sp_sq_ready = sem("sp_sq_ready")
        sp_par_ready = sem("sp_par_ready")
        sp_scale_ready = sem("sp_scale_ready")
        sp_d_ready = sem("sp_d_ready")
        sp_d2_ready = sem("sp_d2_ready")
        sp_exp_ready = sem("sp_exp_ready")
        sp_g_ready = sem("sp_g_ready")
        sp_v_ready = sem("sp_v_ready")
        sp_v_evac = sem("sp_v_evac")
        sp_c_ready = sem("sp_c_ready")
        sp_t_ready = sem("sp_t_ready")
        sp_gt_ready = sem("sp_gt_ready")
        sp_m_ready = sem("sp_m_ready")
        sp_m_evac = sem("sp_m_evac")
        sp_u_ready = sem("sp_u_ready")
        sp_out_ready = sem("sp_out_ready")

        def block2_sync():
            nc.sync.wait_ge(h_ready, NG * 2)
            nc.sync.dma_start(wA[:, 0:w2.at - D - 2], inp["splat"]).then_inc(wA_loaded, 16)
            nc.sync.dma_start(sp_p[0:S2, :], inp["splat_side"]).then_inc(wA_loaded, 16)

        def block2_pe():
            pe = nc.tensor
            block_before(pe, 2)
            pe.wait_ge(wA_loaded, 64)
            pe.wait_ge(sp_par_ready, 1)
            for g in range(NG):
                pe.wait_ge(sp_sq_ready, g + 1)
                for k in range(KD):
                    pe.matmul(PS[0:S2, g, 0:GN], sp_pm2[:, k, :], hgroup(k, g), start=(k == 0), stop=False)
                for k in range(KD):
                    mm = pe.matmul(PS[0:S2, g, 0:GN], const("ones")[:, 0:S2], sp_sq[:, k, g * GN:(g + 1) * GN],
                                   start=False, stop=(k == 1))
                mm.then_inc(sp_d_ready, 1)
            for p in range(NP):
                if p >= 4:
                    pe.wait_ge(sp_v_evac, p - 3)
                for k in range(KD):
                    mm = pe.matmul(PS[:, 4 + p % 4, 0:D], hpair(k, p), sp_wv[:, k, :], start=(k == 0), stop=(k == 1))
                mm.then_inc(sp_v_ready, 1)
            pe.wait_ge(sp_g_ready, NG)
            pe.wait_ge(sp_v_evac, NP)

            def turn(p):
                if p >= 2:
                    pe.wait_ge(sp_gt_ready, p - 1)
                pe.transpose(PS[:, p % 2, 0:S2], sp_g[0:S2, 2 * p:2 * p + 2, :].rearrange("q a t -> q (a t)"),
                             ident[0:S2, 0:S2]).then_inc(sp_t_ready, 1)

            def moments(p):
                pe.wait_ge(sp_gt_ready, p + 1)
                if p:
                    pe.wait_ge(sp_m_evac, p)
                for i in range(2):
                    rws = slice(i * SP, i * SP + T)
                    mm = pe.matmul(PS[0:S2, 2 + i, 0:D], sp_gt[rws, p % 2, :], sp_v[rws, p, :], start=True, stop=True)
                mm.then_inc(sp_m_ready, 1)

            def outputs(p):
                pe.wait_ge(sp_m_evac, p + 1)
                pe.wait_ge(sp_c_ready, p + 2)
                if p >= 2:
                    pe.wait_ge(sp_out_ready, p - 1)
                for i in range(2):
                    g = sp_g[0:S2, 2 * p + i, 0:T]
                    for c in range(KD):
                        at = (2 * c + i) * T
                        pe.matmul(PS[:, 4 + p % 2, at:at + T], sp_m[0:S2, p % 2, i, c * P:(c + 1) * P], g,
                                  start=True, stop=True)
                    at = (4 + i) * T
                    mm = pe.matmul(PS[:, 4 + p % 2, at:at + T], sp_cb[0:S2, p % 2, i, :], g, start=True, stop=True)
                mm.then_inc(sp_u_ready, 1)

            turn(0)
            for p in range(NP):
                moments(p)
                if p + 1 < NP:
                    turn(p + 1)
                if p:
                    outputs(p - 1)
            outputs(NP - 1)
            project_pe(sp_wo, lambda e: e.wait_ge(sp_out_ready, NP))
            ln_pe(2)

        def block2_act():
            a = nc.scalar
            block_before(a, 2)
            for g in range(NG):
                for k in range(KD):
                    ins = a.activation(compact(sp_sq[:, k, g * GN:(g + 1) * GN]), hgroup(k, g), ACT.Square)
                ins.then_inc(sp_sq_ready, 1)
            a.wait_ge(wA_loaded, 64)
            a.activation(sp_col[0:S2, 0:1], sp_p[0:S2, D:D + 1], ACT.Exp).then_inc(sp_scale_ready, 1)
            for g in range(NG):
                a.wait_ge(sp_d2_ready, g + 1)
                sl = slice(g * GN, (g + 1) * GN)
                a.activation(sp_raw[0:S2, sl], sp_raw[0:S2, sl], ACT.Exp, scale=sp_col[0:S2, 3:4]).then_inc(sp_exp_ready, 1)
            for p in range(NP):
                a.wait_ge(sp_m_ready, p + 1)
                if p >= 2:
                    a.wait_ge(sp_u_ready, p - 1)
                a.activation(sp_m[0:S2, p % 2], PS[0:S2, 2:4, 0:D], ACT.Copy).then_inc(sp_m_evac, 1)
            ln_act(2)

        def block2_dve():
            v = nc.vector
            block_before(v, 2)
            v.wait_ge(wA_loaded, 64)
            v.tensor_scalar(sp_pm2, sp_pT, -2.0, None, ALU.mult).then_inc(sp_par_ready, 1)
            dve_then(v.tensor_tensor(sp_tmp[0:S2], sp_p[0:S2, 0:D], sp_p[0:S2, 0:D], ALU.mult))
            v.tensor_reduce(sp_col[0:S2, 1:2], sp_tmp[0:S2], AX, ALU.add)
            v.wait_ge(sp_scale_ready, 1)
            dve_then(v.tensor_tensor(sp_col[0:S2, 2:3], sp_col[0:S2, 0:1], sp_col[0:S2, 0:1], ALU.mult))
            dve_then(v.reciprocal(sp_col[0:S2, 4:5], sp_col[0:S2, 2:3]))
            dve_then(v.tensor_scalar(sp_col[0:S2, 3:4], sp_col[0:S2, 4:5], -0.5, None, ALU.mult))
            dve_then(v.memset(sp_g[0:S2], 0.0))
            for g in range(NG):
                v.wait_ge(sp_d_ready, g + 1)
                v.tensor_scalar(sp_raw[0:S2, g * GN:(g + 1) * GN], PS[0:S2, g, 0:GN], sp_col[0:S2, 1:2], 0.0, ALU.add,
                                ALU.max).then_inc(sp_d2_ready, 1)
            for p in range(NP):
                v.wait_ge(sp_v_ready, p + 1)
                v.tensor_copy(sp_v[:, p, :], PS[:, 4 + p % 4, 0:D]).then_inc(sp_v_evac, 1)
            for g in range(NG):
                v.wait_ge(sp_exp_ready, g + 1)
                v.tensor_scalar(sp_g[0:S2, g * GI:(g + 1) * GI, 0:T], compact(sp_raw[0:S2, g * GN:(g + 1) * GN]),
                                sp_p[0:S2, D + 1:D + 2], None, ALU.mult).then_inc(sp_g_ready, 1)
            v.wait_ge(sp_g_ready, NG)
            v.tensor_reduce(sp_c[0:S2], sp_g[0:S2, :, 0:T], AX, ALU.add).then_inc(sp_c_ready, 1)
            v.wait_ge(sp_c_ready, 1)

            def out_rows_of(p):
                v.wait_ge(sp_u_ready, p + 1)
                dve_then(v.tensor_scalar(sp_den[:, 0, :], PS[:, 4 + p % 2, 4 * T:6 * T], 1e-8, None, ALU.add))
                dve_then(v.reciprocal(sp_den[:, 1, :], sp_den[:, 0, :]))
                for c in range(KD):
                    ins = v.tensor_tensor(aT[:, c, 2 * p:2 * p + 2, 1:T + 1],
                                          compact(PS[:, 4 + p % 2, 2 * c * T:(2 * c + 2) * T]),
                                          compact(sp_den[:, 1, :]), ALU.mult)
                ins.then_inc(sp_out_ready, 1)
                v.wait_ge(sp_out_ready, p + 1)

            for p in range(NP):
                v.wait_ge(sp_t_ready, p + 1)
                if p >= 2:
                    v.wait_ge(sp_m_ready, p - 1)
                v.tensor_copy(sp_gt[:, p % 2, :], PS[:, p % 2, 0:S2]).then_inc(sp_gt_ready, 1)
                if p >= 2:
                    v.wait_ge(sp_u_ready, p - 1)
                v.tensor_copy(sp_cb[0:S2, p % 2], per(sp_c[0:S2, 2 * p:2 * p + 2], P)).then_inc(sp_c_ready, 1)
                if p >= 2:
                    out_rows_of(p - 2)
            out_rows_of(NP - 2)
            out_rows_of(NP - 1)
            project_dve([zcol[:, 0:1]] * 2)
            ln_dve(2)

        one_rows = sb("one_rows", [2, NT])
        one_set = sem("one_set")
        one_stored = sem("one_stored")

        def block3_pool():
            nc.gpsimd.memset(one_rows[:, :], 1.0).then_inc(one_set, 1)
            nc.gpsimd.wait_ge(one_set, 1)
            nc.gpsimd.dma_start(scratch[1, 16:18, :], one_rows[:, :]).then_inc(one_stored, 16)

        def block3_sync():
            def combined(sp):
                combine_sync(1, 16)
                sp.wait_ge(one_stored, 16)
            ffn_sync(3, combined)

        def block3_pe():
            block_before(nc.tensor, 3)
            logits_pe(g1_w, 16)
            combine_pe(1, 16)
            nc.tensor.wait_ge(combT_copied, 2)
            ffn_pe(3)
            ln_pe(3)

        def block3_act():
            a = nc.scalar
            block_before(a, 3)
            a.wait_ge(gate_ready, 2)
            a.activation(g_e, PS[:, 0, 0:256], ACT.Sigmoid).then_inc(gate_exp, 1)
            ffn_act(3)
            ln_act(3)

        def block3_dve():
            v = nc.vector
            block_before(v, 3)
            ffn_begin_dve()
            v.wait_ge(gate_exp, 2)
            E = 16
            sc, gt, eq, pre, sel, rst, c, mk = [tile3(x, E) for x in (g_e, g_gt, g_eq, g_pre, g_sel, g_rst, g_c, g_lg)]
            s4 = g_e.rearrange("q (a b) -> q a b", b=4)
            t1, gs = g_gt[:, 0:64], g_room
            dve_then(v.tensor_tensor(gs, s4[:, :, 0], s4[:, :, 1], ALU.add))
            for x, y in ((0, 2), (0, 3), (1, 2), (1, 3), (2, 3)):
                dve_then(v.tensor_tensor(t1, s4[:, :, x], s4[:, :, y], ALU.add))
                dve_then(v.tensor_tensor(gs, gs, t1, ALU.max))
            g3 = gs.rearrange("q (p g) -> q p g", g=4)
            other = bass.AP(g3.tensor, g3.offset, [g3.ap[0], g3.ap[1], [0, 4], g3.ap[2]])
            own = per(g3, 4)
            cmp4 = lambda x: x[:, 0:256].rearrange("q (p g o) -> q p g o", g=4, o=4)
            v.tensor_tensor(cmp4(g_eq), other, own, ALU.is_equal)
            dve_then(v.tensor_tensor(cmp4(g_pre), other, own, ALU.is_gt))
            dve_then(v.tensor_tensor(tile3(g_eq, 16), tile3(g_eq, 16), bcast(const("tril4"), 0, 16), ALU.mult))
            dve_then(v.tensor_tensor(g_pre, g_pre, g_eq, ALU.add))
            dve_then(v.tensor_reduce(g_sum, g_pre.rearrange("q (a b) -> q a b", b=4), AX, ALU.add))
            dve_then(v.tensor_scalar(g_sum, g_sum, 2.0, None, ALU.is_lt))
            dve_then(v.tensor_scalar(g_rec, g_sum, 2.0, -2.0, ALU.mult, ALU.add))
            m4 = g_lg.rearrange("q (a b) -> q a b", b=4)
            dve_then(v.tensor_tensor(m4, s4, per(g_sum, 4), ALU.mult))
            dve_then(v.tensor_tensor(m4, m4, per(g_rec, 4), ALU.add))
            choose_dve(mk, 16, E, 4, sel, (g_m8, gt, eq, pre, g_room[:, 0:16]), rst)
            dve_then(v.tensor_tensor(c, sc, sel, ALU.mult))
            dve_then(v.tensor_reduce(g_sum[:, 0:16], c, AX, ALU.add))
            dve_then(v.tensor_scalar(g_sum[:, 0:16], g_sum[:, 0:16], 1e-6, None, ALU.add))
            dve_then(v.reciprocal(g_rec[:, 0:16], g_sum[:, 0:16]))
            v.tensor_tensor(c, c, per(g_rec[:, 0:16], E), ALU.mult).then_inc(comb_ready, 1)
            combine_dve(1, 16)
            ffn_dve(3)
            ln_dve(3)

        H8, M, DK = 8, 64, 32
        w4 = carve(wA, 6656)
        gs_wq, gs_wk, gs_wv, gs_wo = [w4(2 * D).rearrange("q (k n) -> q k n", k=2) for _ in range(4)]
        gs_w1 = w4(2 * M).rearrange("q (k n) -> q k n", k=2)
        gs_w2 = w4(H8 * M)
        gs_nw = w4(D)
        s4_ = carve(arena, AR)
        gs_q, gs_k = [s4_(2 * NT).rearrange("q (c n) -> q c n", c=2) for _ in range(2)]
        gs_v = s4_(NP * D).rearrange("q (p n) -> q p n", p=NP)
        gs_lf, gs_s = [s4_(4 * 512).rearrange("q (p n) -> q p n", p=4) for _ in range(2)]
        xw = carve(acc[:, :, :].rearrange("q k n -> q (k n)"), KD * NT)
        gs_L = s4_(4 * 512).rearrange("q (s i n) -> q s i n", s=2, i=2)
        gs_E = s4_(4 * 512).rearrange("q (s i n) -> q s i n", s=2, i=2)
        gs_A = xw(2 * 8 * NR).rearrange("q (i h t) -> q i h t", i=2, h=8)
        gs_R = s4_(2 * 512).rearrange("q (i n) -> q i n", i=2)
        gs_RT = w4(2 * 4 * NR).rearrange("q (i c n) -> q i c n", i=2, c=4)
        gs_LT = w4(2 * 4 * NJ).rearrange("q (i c n) -> q i c n", i=2, c=4)
        gs_vx = s4_(2 * D).rearrange("q (i n) -> q i n", i=2)
        gs_ox = s4_(2 * D).rearrange("q (i n) -> q i n", i=2)
        gs_qv = w4(512)
        gs_kx = w4(2 * 2 * 2 * NJ).rearrange("q (s c i n) -> q s c i n", s=2, c=2, i=2)
        gs_qx = carve(rs, NT)(2 * 2 * 2 * NR).rearrange("q (s c i n) -> q s c i n", s=2, c=2, i=2)
        gs_gt = xw(D)
        gs_col = s4_(32)
        gs_t = s4_(P)
        gs_sq = s4_(D)
        gs_t12 = xc[0:M, :, :].rearrange("q k n -> q (k n)")[:, 0:B * SP].rearrange("q (a t) -> q a t", t=SP)
        (gs_pad, gs_o, gs_o_evac, gs_vr, gs_v_evac, gs_f, gs_ln, gs_lf_ready, gs_se, gs_s_ready, gs_gathered,
         gs_zl, gs_zr, gs_sj, gs_at, gs_p1, gs_sum, gs_qs, gs_tq, gs_tl, gs_vs, gs_b, gs_o2, gs_fin, gs_gate,
         gs_el, gs_er, gs_qt, gs_lt, gs_vx_ready, gs_ox_ready, gs_sexp, gs_gt_ready,
         gs_l, gs_a, gs_r, gs_qr, gs_bm, gs_sub, gs_ov_read, gs_ms, gs_rms, gs_og, gs_ogt, gs_aT) = [
             sem("gs_" + x) for x in (
             "pad_zeroed", "proj_ready", "proj_evac", "v_ready", "v_evac", "f_ready", "ln_ready", "logf_ready",
             "exp_logf_ready", "s_ready", "rows_gathered",
             "zleft_ready", "zright_ready", "srows_ready", "scores_ready", "slots_ready", "slots_summed",
             "qrows_ready", "qT_ready", "leftT_ready", "vrows_ready", "pairs_ready", "outrows_ready", "out_ready",
             "gate_ready", "eleft_ready", "eright_ready", "qT_evac", "leftT_evac", "vrows_evac", "outrows_evac",
             "exp_ready", "tanh_ready", "left_ready", "masked_ready", "slots_decayed", "queries_decayed",
             "pairs_masked", "shifted", "out_read", "squares_ready", "rms_ready", "normed", "normT_ready",
             "aT_ready")]

        def block4_sync():
            nc.sync.wait_ge(h_ready, NG * 4)
            nc.sync.dma_start(wA[:, 0:4 * 2 * D + 2 * M], inp["slots"]).then_inc(wA_loaded, 16)
            nc.sync.dma_start(gs_w2[0:M, :], inp["slots_2"]).then_inc(wA_loaded, 16)
            nc.sync.dma_start(gs_nw, inp["norm_w"].broadcast_to([P, D])).then_inc(wA_loaded, 16)

        def block4_pe():
            pe = nc.tensor
            block_before(pe, 4)
            pe.wait_ge(wA_loaded, 64 + 48)
            n = 0
            for g in range(NG):
                outs = [(w[:, :, c * P:(c + 1) * P], P) for w in (gs_wq, gs_wk) for c in range(2)] + [(gs_w1, M)]
                for w, m in outs:
                    if n >= 4:
                        pe.wait_ge(gs_o_evac, n - 3)
                    for k in range(KD):
                        mm = pe.matmul(PS[0:m, n % 4, 0:GN], w[:, k, :], hgroup(k, g), start=(k == 0), stop=(k == 1))
                    mm.then_inc(gs_o, 1)
                    n += 1
                for p in range(4 * g, 4 * g + 4):
                    if p >= 4:
                        pe.wait_ge(gs_v_evac, p - 3)
                    for k in range(KD):
                        mm = pe.matmul(PS[:, 4 + p % 4, 0:D], hpair(k, p), gs_wv[:, k, :], start=(k == 0),
                                       stop=(k == 1))
                    mm.then_inc(gs_vr, 1)
            pe.wait_ge(gs_o_evac, 5 * NG)
            pe.wait_ge(gs_v_evac, NP)

            def t12(p, at):
                return gs_t12[at:at + DK, 2 * p:2 * p + 2, :].rearrange("q a t -> q (a t)")

            def log_forget(p):
                if p:
                    pe.wait_ge(gs_bm, 2 * (p - 1))
                    pe.wait_ge(gs_er, 2 * p)
                    pe.wait_ge(gs_a, 2 * p)
                for x in range(4):
                    pe.matmul(PS[:, 1 + x, :], t12(p + x, 0), gs_w2[0:DK, :], start=True, stop=True).then_inc(gs_f, 1)

            def front(p, i):
                u, i4 = 2 * p + i, p % 4
                if i == 0:
                    pe.wait_ge(gs_lf_ready, p - i4 + 4)
                if u:
                    pe.wait_ge(gs_el, u)
                if i == 0 and p and i4 == 0:
                    pe.wait_ge(gs_lt, 2 * p - 1)
                if i == 0 and p >= 2:
                    pe.wait_ge(gs_vx_ready, 2 * (p - 1))
                    pe.wait_ge(gs_gt_ready, p - 1)
                    pe.wait_ge(gs_bm, 2 * (p - 1))
                pe.matmul(PS[0:NJ, 0, :], const("left%d" % i), gs_lf[:, i4, :], start=True, stop=True).then_inc(gs_zl, 1)
                if u:
                    pe.wait_ge(gs_er, u)
                pe.matmul(PS[0:NR, 1, :], const("right%d" % i), gs_lf[:, i4, :], start=True, stop=True).then_inc(gs_zr, 1)
                pe.wait_ge(gs_s_ready, p + 1)
                if u:
                    pe.wait_ge(gs_l, u)
                pe.matmul(PS[0:NJ, 2, :], const("pick_left%d" % i), gs_s[:, i4, :], start=True,
                          stop=True).then_inc(gs_sj, 1)
                pe.wait_ge(gs_gathered, p + 1)
                if u:
                    pe.wait_ge(gs_a, u)
                for r in (0, 2, 1, 3):
                    if r % 2:
                        pe.wait_ge(row_tile_done, tile_count["n"] - 1)
                    for c in range(2):
                        at = ((r % 2) * 2 + c) * NR
                        mm = pe.matmul(PS[0:NJ, 3 + r // 2, at:at + NR], gs_kx[32 * r:32 * r + DK, p % 2, c, i, :],
                                       gs_qx[32 * r:32 * r + DK, p % 2, c, i, :], start=True, stop=True)
                    if r != 3:
                        mm.then_inc(row_tile_done, 1)
                        tile_count["n"] += 1
                mm.then_inc(gs_at, 1)

            def slots(p, i):
                pe.wait_ge(gs_l, 2 * p + i + 1)
                pe.wait_ge(gs_a, 2 * p + i + 1)
                if p:
                    pe.wait_ge(gs_qr, 2 * (p - 1) + i + 1)
                for h in range(H8):
                    mm = pe.matmul(PS[0:NR, 5 + i, h * M:(h + 1) * M], gs_A[0:NJ, i, (h % 4) * 2 + h // 4, :],
                                   gs_L[0:NJ, p % 2, i, h * M:(h + 1) * M], start=True, stop=True)
                mm.then_inc(gs_p1, 1)

            def add_levels(p):
                for i in range(2):
                    pe.wait_ge(gs_r, 2 * p + i + 1)
                    pe.matmul(PS[i * SP:(i + 1) * SP, 5, :], const("total")[0:NR, :], gs_R[0:NR, i, :], start=True,
                              stop=True).then_inc(gs_sum, 1)

            def query_rows(q):
                pe.wait_ge(gs_sexp, q + 1)
                if q:
                    pe.wait_ge(gs_ov_read, q)
                for i in range(2):
                    pe.matmul(PS[0:NR, 5 + i, :], const("pick_right%d" % i), gs_qv, start=True,
                              stop=True).then_inc(gs_qs, 1)

            def turn(q, i, last):
                pe.wait_ge(gs_qr, 2 * q + i + 1)
                if i == 0 and q:
                    pe.wait_ge(gs_ox_ready, 2 * q)
                if i == 1:
                    pe.wait_ge(gs_er, 2 * q + (2 if last else 4))
                    if q:
                        pe.wait_ge(gs_bm, 2 * q)
                for c in range(4):
                    mm = pe.transpose(PS[:, 1 if i else 7, c * P:c * P + NR], gs_R[0:NR, i, c * P:(c + 1) * P],
                                      ident[0:NR, 0:NR])
                mm.then_inc(gs_tq, 1)
                if i == 0:
                    pe.wait_ge(gs_el, 2 * q + (2 if last else 4))
                    if q:
                        pe.wait_ge(gs_vx_ready, 2 * q)
                        pe.wait_ge(gs_gt_ready, q)
                pe.wait_ge(gs_l, 2 * q + (2 if last or i == 0 else 4))
                for c in range(4):
                    mm = pe.transpose(PS[:, 2 if i else 0, c * P:c * P + NJ], gs_L[0:NJ, q % 2, i, c * P:(c + 1) * P],
                                      ident[0:NJ, 0:NJ])
                mm.then_inc(gs_tl, 1)

            def pairs(q, i, last):
                pe.wait_ge(gs_qt, 2 * q + i + 1)
                pe.wait_ge(gs_lt, 2 * q + i + 1)
                if i:
                    pe.matmul(PS[:, 0, D:2 * D], t12(q, DK), gs_w2[DK:2 * DK, 0:D], start=True,
                              stop=True).then_inc(gs_gate, 1)
                    pe.wait_ge(gs_gate, q + 1)
                pe.matmul(PS[0:NJ, 0 if i else 7, 0:D], const("pick_left%d" % i), gs_v[:, q, :], start=True,
                          stop=True).then_inc(gs_vs, 1)
                if i == 0 and not last:
                    pe.wait_ge(gs_a, 2 * q + 4)
                for e in range(2):
                    for c in range(4):
                        mm = pe.matmul(PS[0:NJ, (1 if i else 3) + e, c * NR:(c + 1) * NR],
                                       gs_LT[e * M:(e + 1) * M, i, c, :], gs_RT[e * M:(e + 1) * M, i, c, :],
                                       start=True, stop=True)
                mm.then_inc(gs_b, 1)

            def outputs(q, last):
                for i in range(2):
                    pe.wait_ge(gs_bm, 2 * q + i + 1)
                    pe.wait_ge(gs_vx_ready, 2 * q + i + 1)
                    if i == 0 and not last:
                        pe.wait_ge(gs_r, 2 * q + 4)
                    for h in range(H8):
                        mm = pe.matmul(PS[0:NR, 6 + i, h * DK:(h + 1) * DK], gs_A[0:NJ, i, (h % 2) * 4 + h // 2, :],
                                       gs_vx[0:NJ, i, h * DK:(h + 1) * DK], start=True, stop=True)
                    mm.then_inc(gs_o2, 1)
                for i in range(2):
                    pe.wait_ge(gs_ox_ready, 2 * q + i + 1)
                    pe.matmul(PS[i * SP:(i + 1) * SP, 6, 0:D], const("total")[0:NR, :], gs_ox[0:NR, i, :], start=True,
                              stop=True).then_inc(gs_fin, 1)

            for p in range(NP + 1):
                q, first, last = p - 1, p == 0, p == NP
                if p % 4 == 0 and not last:
                    log_forget(p)
                    if not first:
                        query_rows(q)
                        turn(q, 0, True)
                    front(p, 0)
                    front(p, 1)
                else:
                    if not last:
                        front(p, 0)
                    if not first:
                        query_rows(q)
                    if not last:
                        front(p, 1)
                    if not first:
                        turn(q, 0, last)
                if not last:
                    slots(p, 0)
                if not first:
                    turn(q, 1, last)
                if not last:
                    slots(p, 1)
                if not first:
                    pairs(q, 0, last)
                if not last:
                    add_levels(p)
                if not first:
                    pairs(q, 1, last)
                    outputs(q, last)
            for p in range(NP):
                pe.wait_ge(gs_og, p + 1)
                if p >= 6:
                    pe.wait_ge(gs_aT, p - 5)
                for c in range(KD):
                    mm = pe.transpose(PS[:, p % 6, c * P:(c + 1) * P], gs_v[:, p, c * P:(c + 1) * P], ident)
                mm.then_inc(gs_ogt, 1)
            project_pe(gs_wo, lambda e: e.wait_ge(gs_aT, NP))
            ln_pe(4)

        def block4_act():
            a = nc.scalar
            block_before(a, 4)
            a.wait_ge(gs_pad, 1)
            n = 0
            for g in range(NG):
                sl = slice(g * GN, (g + 1) * GN)
                for dst in (gs_q, gs_k):
                    for c in range(2):
                        a.wait_ge(gs_o, n + 1)
                        a.activation(dst[:, c, sl], PS[:, n % 4, 0:GN], ACT.Silu).then_inc(gs_o_evac, 1)
                        n += 1
                a.wait_ge(gs_o, n + 1)
                a.activation(gs_t12[:, g * GI:(g + 1) * GI, 0:T], compact(PS[0:M, n % 4, 0:GN]),
                             ACT.Copy).then_inc(gs_o_evac, 1)
                n += 1
            def log_forget(p):
                for x in range(4):
                    a.wait_ge(gs_f, p + x + 1)
                    ins = a.activation(gs_lf[:, x, :], PS[:, 1 + x, :], ACT.Abs)
                act_then(ins)
                act_then(a.activation(gs_lf[:, :, :], gs_lf[:, :, :], ACT.Exp, scale=-1.0))
                a.activation(gs_lf[:, :, :], gs_lf[:, :, :], ACT.Ln, bias=1.0).then_inc(gs_ln, 1)
                if p:
                    a.wait_ge(gs_sj, 2 * p)
                for x in range(4):
                    a.wait_ge(gs_lf_ready, p + x + 1)
                    a.activation(gs_s[:, x, :], gs_lf[:, x, :], ACT.Exp).then_inc(gs_se, 1)

            def decays(p, i):
                a.wait_ge(gs_zl, 2 * p + i + 1)
                if p >= 2:
                    a.wait_ge(gs_tl, 2 * (p - 2) + i + 1)
                a.activation(gs_L[0:NJ, p % 2, i, :], PS[0:NJ, 0, :], ACT.Exp).then_inc(gs_el, 1)
                a.wait_ge(gs_zr, 2 * p + i + 1)
                if p >= 2:
                    a.wait_ge(gs_qr, 2 * (p - 2) + i + 1)
                a.activation(gs_E[0:NR, p % 2, i, :], PS[0:NR, 1, :], ACT.Exp).then_inc(gs_er, 1)

            def evacuate_turned(q, i):
                w = 2 * q + i
                a.wait_ge(gs_tq, w + 1)
                if q:
                    a.wait_ge(gs_b, w - 1)
                a.activation(gs_RT[:, i], PS[:, 1 if i else 7, :].rearrange("q (c n) -> q c n", c=4)[:, :, 0:NR],
                             ACT.Copy).then_inc(gs_qt, 1)
                a.wait_ge(gs_tl, w + 1)
                a.activation(gs_LT[:, i], PS[:, 2 if i else 0, :].rearrange("q (c n) -> q c n", c=4)[:, :, 0:NJ],
                             ACT.Copy).then_inc(gs_lt, 1)

            def evacuate_v(q, i):
                a.wait_ge(gs_vs, 2 * q + i + 1)
                if q:
                    a.wait_ge(gs_o2, 2 * q + i - 1)
                a.activation(gs_vx[0:NJ, i, :], PS[0:NJ, 0 if i else 7, 0:D], ACT.Copy).then_inc(gs_vx_ready, 1)

            for p in range(NP + 1):
                q, first, last = p - 1, p == 0, p == NP
                if p % 4 == 0 and not last:
                    log_forget(p)
                if p % 4 == 0 and not first:
                    evacuate_turned(q, 0)
                if not last:
                    decays(p, 0)
                    decays(p, 1)
                if not first:
                    if p % 4:
                        evacuate_turned(q, 0)
                    evacuate_turned(q, 1)
                    evacuate_v(q, 0)
                    evacuate_v(q, 1)
                    if q:
                        a.wait_ge(gs_ov_read, q)
                    a.wait_ge(gs_gate, q + 1)
                    a.activation(gs_gt, PS[:, 0, D:2 * D], ACT.Tanh, scale=0.5).then_inc(gs_gt_ready, 1)
                    for i in range(2):
                        a.wait_ge(gs_o2, 2 * q + i + 1)
                        if q:
                            a.wait_ge(gs_fin, 2 * q + i - 1)
                        a.activation(gs_ox[0:NR, i, :], PS[0:NR, 6 + i, 0:D], ACT.Copy).then_inc(gs_ox_ready, 1)
                if not last:
                    a.wait_ge(gs_sub, p + 1)
                    a.activation(gs_qv, gs_qv, ACT.Exp).then_inc(gs_sexp, 1)
            a.wait_ge(gs_ms, 1)
            act_then(a.activation(gs_t[:, 0:P], gs_t[:, 0:P], ACT.Ln, scale=1.0 / DK, bias=epscol[:, 0:1]))
            a.activation(gs_t[:, 0:P], gs_t[:, 0:P], ACT.Exp, scale=-0.5).then_inc(gs_rms, 1)
            for p in range(NP):
                a.wait_ge(gs_ogt, p + 1)
                src = PS[:, p % 6, 0:D].rearrange("q (c i t) -> q c i t", c=2, i=2)
                for c in range(KD):
                    ins = a.activation(aT[:, c, 2 * p:2 * p + 2, 1:T + 1], src[:, c, :, 0:T], ACT.Copy)
                ins.then_inc(gs_aT, 1)
            ln_act(4)

        def block4_pool():
            po = nc.gpsimd
            po.wait_ge(gs_o_evac, 5 * NG)

            def blocks(ap, start, n, step, b):
                dims = [list(x) for x in ap.ap]
                return bass.AP(ap.tensor, ap[:, :, start:start + 1].offset, dims[:2] + [[step, n], [1, b]])

            for p in range(NP):
                if p >= 2:
                    po.wait_ge(gs_at, 2 * (p - 1))
                for c in range(2):
                    ks, qs = [compact(w[:, c, 2 * p * T:(2 * p + 2) * T]) for w in (gs_k, gs_q)]
                    at_k = at_q = 0

                    def gather(dst, at, src, start, n, step, b):
                        return po.tensor_copy(dst[:, p % 2, c, :, at:at + n * b].rearrange("q i (n b) -> q i n b", b=b),
                                              blocks(src, start, n, step, b))

                    for _, b, n, full in BLOCKS:
                        n += T % 2 if b == 1 else 0
                        gather(gs_kx, at_k, ks, 0, n, 2 * b, b)
                        at_k += n * b
                        if full:
                            gather(gs_qx, at_q, qs, b, full, 2 * b, b)
                            at_q += full * b
                        rest = T - (2 * b * full + b)
                        if rest > 0:
                            gather(gs_qx, at_q, qs, T - rest, 1, rest, rest)
                            at_q += rest
                    ins = gather(gs_qx, at_q, qs, 0, 1, T, T)
                ins.then_inc(gs_gathered, 1)

        def block4_dve():
            v = nc.vector
            block_before(v, 4)
            v.memset(xc[0:M, :, :], 0.0).then_inc(gs_pad, 1)
            for p in range(NP):
                v.wait_ge(gs_vr, p + 1)
                v.tensor_copy(gs_v[:, p, :], PS[:, 4 + p % 4, 0:D]).then_inc(gs_v_evac, 1)
            def log_forget(p):
                v.wait_ge(gs_ln, p // 4 + 1)
                for x in range(4):
                    v.scalar_tensor_tensor(out=gs_lf[:, x, :], in0=PS[:, 1 + x, :], scalar=0.0, in1=gs_lf[:, x, :],
                                           op0=ALU.min, op1=ALU.subtract).then_inc(gs_lf_ready, 1)
                for x in range(4):
                    v.wait_ge(gs_se, p + x + 1)
                    v.tensor_scalar(gs_s[:, x, :], gs_s[:, x, :], -1.0, 1.0, ALU.mult, ALU.add).then_inc(gs_s_ready, 1)

            def masked(banks, i, done):
                src = PS[0:NJ, banks:banks + 2, 0:4 * NR].rearrange("q b (h t) -> q b h t", h=4)
                v.tensor_tensor(gs_A[0:NJ, i].rearrange("q (b h) t -> q b h t", b=2), src,
                                bcast(bcast(const("pair_mask")[0:NJ, :], 0, 4), 0, 2), ALU.mult).then_inc(done, 1)

            def front(p, i):
                u = 2 * p + i
                v.wait_ge(gs_el, u + 1)
                v.wait_ge(gs_sj, u + 1)
                left = gs_L[0:NJ, p % 2, i, :]
                v.tensor_tensor(left, left, PS[0:NJ, 2, :], ALU.mult).then_inc(gs_l, 1)
                v.wait_ge(gs_at, u + 1)
                if p:
                    v.wait_ge(gs_p1, u - 1)
                if p >= 2:
                    v.wait_ge(gs_o2, u - 3)
                masked(3, i, gs_a)

            def queries(q, i):
                v.wait_ge(gs_qs, 2 * q + i + 1)
                v.wait_ge(gs_er, 2 * q + i + 1)
                v.wait_ge(gs_sum, 2 * q + i + 1)
                v.tensor_tensor(gs_R[0:NR, i, :], PS[0:NR, 5 + i, :], gs_E[0:NR, q % 2, i, :],
                                ALU.mult).then_inc(gs_qr, 1)

            def slots(p, i):
                v.wait_ge(gs_p1, 2 * p + i + 1)
                v.wait_ge(gs_er, 2 * p + i + 1)
                if p:
                    v.wait_ge(gs_tq, 2 * (p - 1) + i + 1)
                v.tensor_tensor(gs_R[0:NR, i, :], PS[0:NR, 5 + i, :], gs_E[0:NR, p % 2, i, :],
                                ALU.mult).then_inc(gs_r, 1)

            def output(q):
                v.wait_ge(gs_gt_ready, q + 1)
                dve_then(v.tensor_scalar(gs_gt, gs_gt, 0.5, 0.5, ALU.mult, ALU.add))
                gt = gs_gt.rearrange("q (h d) -> q h d", h=H8)
                dve_then(v.tensor_tensor(gt, gt, per(gs_col[:, 16 + 8 * (q % 2):24 + 8 * (q % 2)], DK), ALU.mult))
                v.wait_ge(gs_fin, 2 * q + 2)
                v.tensor_tensor(gs_v[:, q, :], PS[:, 6, 0:D], gs_gt, ALU.mult).then_inc(gs_ov_read, 1)

            def squares(q):
                v.wait_ge(gs_ov_read, q + 1)
                dve_then(v.tensor_tensor(gs_sq, gs_v[:, q, :], gs_v[:, q, :], ALU.mult))
                dve_then(v.tensor_reduce(gs_t[:, q * 8:(q + 1) * 8], gs_sq.rearrange("q (h d) -> q h d", h=8), AX,
                                         ALU.add))

            qv = gs_qv.rearrange("q (h m) -> q h m", h=H8)
            for p in range(NP + 1):
                q, first, last = p - 1, p == 0, p == NP
                if p % 4 == 0:
                    if not first:
                        queries(q, 0)
                        queries(q, 1)
                    if not last:
                        log_forget(p)
                if not last:
                    front(p, 0)
                if p % 4:
                    queries(q, 0)
                    queries(q, 1)
                if not last:
                    front(p, 1)
                    slots(p, 0)
                    slots(p, 1)
                if not first:
                    for i in range(2):
                        v.wait_ge(gs_b, 2 * q + i + 1)
                        if not last:
                            v.wait_ge(gs_p1, 2 * p + i + 1)
                        masked(1 if i else 3, i, gs_bm)
                if not last:
                    v.wait_ge(gs_sum, 2 * p + 2)
                    ok = PS[:, 5, :].rearrange("q (h m) -> q h m", h=H8)
                    dve_then(v.tensor_reduce(gs_col[:, 0:8], ok, AX, ALU.max))
                    if p:
                        v.wait_ge(gs_qs, 2 * p)
                    v.tensor_tensor(qv, ok, per(gs_col[:, 0:8], M), ALU.subtract).then_inc(gs_sub, 1)
                if not first:
                    output(q)
                    if last:
                        squares(q)
                if not last:
                    v.wait_ge(gs_sexp, p + 1)
                    dve_then(v.tensor_reduce(gs_col[:, 8:16], qv, AX, ALU.add))
                    dve_then(v.reciprocal(gs_col[:, 16 + 8 * (p % 2):24 + 8 * (p % 2)], gs_col[:, 8:16]))
                    if not first:
                        squares(q)
            v.tensor_copy(gs_col[:, 0:1], gs_col[:, 1:2]).then_inc(gs_ms, 1)
            v.wait_ge(gs_rms, 1)
            for p in range(NP):
                og = gs_v[:, p, :].rearrange("q (h d) -> q h d", h=8)
                dve_then(v.tensor_tensor(og, og, per(gs_t[:, p * 8:(p + 1) * 8], DK), ALU.mult))
                v.tensor_tensor(gs_v[:, p, :], gs_v[:, p, :], gs_nw, ALU.mult).then_inc(gs_og, 1)
            project_dve([zcol[:, 0:1]] * 2)
            ln_dve(4)

        int_loaded = sem("int_loaded")
        dequantized = sem("dequantized")
        QW = 3 * UNIT

        def block5_sync():
            nc.sync.wait_ge(ffn_down, FFN_STEP[5])
            for x in range(2):
                nc.sync.dma_start(ring[:, x, 0:QW].bitcast(I32), inp["ffn2"][:, x * QW:(x + 1) * QW]).then_inc(int_loaded, 16)

        def block5_pool():
            nc.gpsimd.wait_ge(int_loaded, 32)
            for x in range(2):
                nc.gpsimd.tensor_scalar(ring[:, x, 0:QW], ring[:, x, 0:QW].bitcast(I32), float(np.float32(1.0 / 127.0)),
                                        None, ALU.mult).then_inc(dequantized, 1)

        def block5_pe():
            block_before(nc.tensor, 5)
            ffn_pe(5, lambda pe: pe.wait_ge(dequantized, 2))
            ln_pe(5)

        def block5_act():
            block_before(nc.scalar, 5)
            ffn_act(5)
            ln_act(5)

        def block5_dve():
            block_before(nc.vector, 5)
            ffn_begin_dve()
            ffn_dve(5)
            ln_dve(5)

        w6 = carve(wA, 6656)
        a6_wq, a6_wk = [w6(1024).rearrange("q (k n) -> q k n", k=2) for _ in range(2)]
        a6_wv, a6_wo = [w6(512).rearrange("q (k n) -> q k n", k=2) for _ in range(2)]
        a6_cw = w6(3072).rearrange("q (s k n) -> q s k n", s=3, k=2)
        a6_b = w6(14)
        a6_vb = w6(D)
        bias_scaled = sem("bias_scaled")

        def block6_sync():
            nc.sync.wait_ge(h_ready, NG * 6)
            nc.sync.dma_start(wA[:, 0:w6.at - D], inp["attn3"]).then_inc(wA_loaded, 16)
            nc.sync.dma_start(a6_vb, inp["v_bias"].broadcast_to([P, D])).then_inc(wA_loaded, 16)

        def block6_pe():
            pe = nc.tensor
            block_before(pe, 6)
            pe.wait_ge(wA_loaded, 112 + 32)
            heads_pe(1, a6_wq, a6_wk, a6_wv)
            attend_pe(1, 1)
            pe.wait_ge(aT_ready, 2 * NP)
            n = 0
            for g in range(NG):
                for c in range(4):
                    if n >= 4:
                        pe.wait_ge(qk_evac, 2 * NQK + n - 3)
                    for tap in range(3):
                        for k in range(KD):
                            mm = pe.matmul(PS[:, n % 4, 0:GN], a6_cw[:, tap, k, c * P:(c + 1) * P],
                                           aT[:, k, g * GI:(g + 1) * GI, tap:tap + T],
                                           start=(tap + k == 0), stop=(tap + k == 3))
                    mm.then_inc(qk_ready, 1)
                    n += 1
            attend_pe(2, 1)
            project_pe(a6_wo, lambda e: e.wait_ge(aT_ready, 3 * NP))
            ln_pe(6)

        def block6_act():
            a = nc.scalar
            block_before(a, 6)
            a.wait_ge(bias_scaled, 1)
            cols = [[a6_b[:, 4 * x + c:4 * x + c + 1] for c in range(4)] for x in range(3)]
            heads_act(1, cols[0], cols[1])
            attend_act(1)
            for n in range(16):
                g, c = n // 4, n % 4
                a.wait_ge(qk_ready, 2 * NQK + n + 1)
                a.activation(q_s[:, c, g * GN:(g + 1) * GN], PS[:, n % 4, 0:GN], ACT.Identity, bias=cols[2][c],
                             scale=0.25).then_inc(qk_evac, 1)
            attend_act(2)
            ln_act(6)

        def block6_dve():
            v = nc.vector
            block_before(v, 6)
            v.wait_ge(wA_loaded, 112 + 32)
            dve_then(v.tensor_scalar(a6_b[:, 0:4], a6_b[:, 0:4], 0.25, None, ALU.mult))
            v.tensor_scalar(a6_b[:, 8:12], a6_b[:, 8:12], 0.25, None, ALU.mult).then_inc(bias_scaled, 1)
            heads_dve(1, a6_vb)
            attend_dve(1, 1)
            attend_dve(2, 1)
            project_dve([a6_b[:, 12 + c:13 + c] for c in range(KD)])
            ln_dve(6)

        E7, CAP = 32, int(1.25 * NT / 32)
        CAP_ROUNDS, CAP_REST = (CAP - 1) // 8, CAP - (CAP - 1) // 8 * 8
        TILES = [(i, min(P, NT - i * P)) for i in range((NT + P - 1) // P)]
        NTL = len(TILES)
        LASTN = TILES[-1][1]
        w7 = carve(wA, 6656)
        r1 = w7(2 * P).rearrange("q (k n) -> q k n", k=2)
        r2 = w7(E7)
        r1b = w7(1)
        r1s = w7(P)
        r7_tail = w7.at
        place_in0 = w7(2 * NT)
        r7 = carve(arena, AR)
        X = r7(NTL * D).rearrange("q (i n) -> q i n", i=NTL)
        slotT, keptW = r7(NT), r7(NT)
        slot = r7(NTL * E7).rearrange("q (i e) -> q i e", i=NTL)
        front = r7.at

        def overlay():
            c = carve(arena, AR)
            c(front)
            return c

        o1 = overlay()
        tmp7 = o1(NTL * D).rearrange("q (i n) -> q i n", i=NTL)
        statT, h1 = o1(NT), o1(NT)
        o2 = overlay()
        scoreT, weightT, wk0, wk1 = [o2(NT) for _ in range(4)]
        o2(o1.at - o2.at if o1.at > o2.at else 0)
        eqT, gtT, preT = [o2(NT) for _ in range(3)]
        small = [o2(NTL * E7).rearrange("q (i e) -> q i e", i=NTL) for _ in range(9)]
        m8_7 = o2(NTL * 8).rearrange("q (i e) -> q i e", i=NTL)
        stat = o2(NTL * 6).rearrange("q (i e) -> q i e", i=NTL)
        c7 = o2(32)
        m8T, roomT = o2(8), o2(1)
        o3 = overlay()
        G8 = 8 * CAP
        w9 = carve(wA, 6656)
        w9(r7_tail)
        sq7, nz7 = [w9(NTL * D).rearrange("q (i n) -> q i n", i=NTL) for _ in range(2)]
        w8 = carve(wA, 6656)
        w8(r7_tail)
        pick = [w(NTL * G8).rearrange("q (i n) -> q i n", i=NTL) for w in (o3, w8)]
        xe = o3(2 * E7 * CAP).rearrange("q (k n) -> q k n", k=2)
        ye = o3(16 * D).rearrange("q (p n) -> q p n", p=16)
        ex_x = o3(2 * 2 * 2 * SP).rearrange("q (s b k n) -> q s b k n", s=2, b=2, k=2)
        ex_sg, ex_h, ex_hT = [o3(2 * 512).rearrange("q (s n) -> q s n", s=2) for _ in range(3)]
        o5 = overlay()
        place_in = [w.rearrange("q (j n) -> q j n", j=2) for w in (place_in0, o5(2 * NT))]
        place = o5(2 * NT).rearrange("q (s n) -> q s n", s=2)
        assert o5.at <= front + NTL * G8 + 2 * E7 * CAP
        gwT = rs[0:16, :]
        router_dve, router_pe, router_act = sem("router_dve"), sem("router_pe"), sem("router_act")
        ROUTER = {name: n + 1 for names in (
            ("compact", "last_tile_zeroed", "deviations", "squares", "stats", "stats_copied", "psum_zeroed", "shifted", "scores",
             "kept", "slots_copied"),
            ("stats_turned", "logits", "scores_turned", "slots_turned"),
            ("squared", "deviations_squared", "roots", "exponentials")) for n, name in enumerate(names)}
        (r_x_ready, r_x_evac, r_h1p, r_h1, r_gw, r_gw_evac, gw_stored, pick_ready, xe_ready, xe_evac, ex_full0,
         ex_full1, ex_up, ex_sg_ready, ex_hid, ex_down, ex_out, place_in_full0, place_in_full1, place_ready, sc_used, sc_added) = [sem("r_" + x) for x in (
             "x_ready", "x_evac", "hidden_ready", "gelu_ready", "group_ready", "group_evac", "group_stored",
             "pick_ready", "gathered", "gather_evac", "expert_loaded0", "expert_loaded1", "expert_up", "expert_gate",
             "expert_hidden", "expert_down", "expert_evac", "place_loaded0", "place_loaded1", "place_ready",
             "place_used", "scatter_added")]
        place_in_full = [place_in_full0, place_in_full1]
        slots_stored = sem("slots_stored")
        ex_x_ready, ex_turned, ex_turned_evac = sem("r_expert_x"), sem("r_expert_turned"), sem("r_expert_turn_evac")
        ex_full = [ex_full0, ex_full1, sem("expert_loaded2"), sem("expert_loaded3")]
        ex_down_full = [sem("r_expert_down_loaded%d" % x) for x in range(4)]
        UPW = 2048
        o4 = overlay()
        ex_w = [ring[:, 0, :], ring[:, 1, :], w7(RING), o4(RING)]
        NX = 4

        def ex_loop(eng, body):
            body(0, True)
            with eng.Fori(1, E7 // NX) as i:
                body(i, False)

        def block7_sync():
            sp = nc.sync
            sp.wait_ge(h_ready, NG * 7)
            def expert_up(x, e):
                src = inp["experts"][bass.ds(e, 1)].rearrange("a q n -> q (a n)")
                sp.dma_start(ex_w[x][:, 0:UPW], src[:, 0:UPW]).then_inc(ex_full[x], 16)

            def expert_down(x, e):
                src = inp["experts"][bass.ds(e, 1)].rearrange("a q n -> q (a n)")
                sp.dma_start(ex_w[x][:, UPW:RING], src[:, UPW:RING]).then_inc(ex_down_full[x], 16)

            sp.wait_ge(ffn_down, FFN_STEP[7])
            for x in range(2):
                expert_up(x, x)
                expert_down(x, x)
            sp.wait_ge(h_ready, NG * 8)
            sp.dma_start(wA[:, 0:2 * P + E7 + 1], inp["router"]).then_inc(wA_loaded, 16)
            sp.dma_start(r1s[0:6, :], inp["router_stats"]).then_inc(wA_loaded, 16)

            def place_inputs(q):
                for e in range(2):
                    for j in range(2):
                        row = scratch[j, 2 * q + e:2 * q + e + 1, :]
                        sp.dma_start(place_in[q % 2][e * SP:(e + 1) * SP, j, :],
                                     row.broadcast_to([SP, NT])).then_inc(place_in_full[q % 2], 16)

            sp.wait_ge(router_dve, ROUTER["kept"])
            sp.dma_start(scratch[0, 0:E7, :], slotT[0:E7]).then_inc(slots_stored, 16)
            sp.dma_start(scratch[1, 0:E7, :], keptW[0:E7]).then_inc(slots_stored, 16)
            sp.wait_ge(r_gw_evac, 4)
            sp.dma_start(scratch[2, 0:16, :], gwT).then_inc(gw_stored, 16)
            sp.wait_ge(xe_ready, 4)
            for x in (2, 3):
                expert_up(x, x)
                expert_down(x, x)
            sp.wait_ge(slots_stored, 32)
            place_inputs(0)

            def pair_up(y, K):
                sp.wait_ge(ex_up, K - 1)
                for b in range(2):
                    expert_up(2 * y + b, 2 * K + b)

            def pair_down(y, K):
                sp.wait_ge(ex_down, 2 * K - 2)
                for b in range(2):
                    expert_down(2 * y + b, 2 * K + b)

            pair_up(0, 2)
            with sp.Fori(1, E7 // NX - 1) as i:
                for y in range(2):
                    pair_up(1 - y, 2 * i + y + 1)
                    pair_down(y, 2 * i + y)
            pair_up(1, E7 // 2 - 1)
            pair_down(0, E7 // 2 - 2)
            pair_down(1, E7 // 2 - 1)
            sp.wait_ge(ex_down, E7)
            for q in range(1, E7 // 2):
                if q >= 2:
                    sp.wait_ge(place_ready, q - 1)
                place_inputs(q)

            def combined(sp):
                sp.wait_ge(gw_stored, 16)
                sp.wait_ge(sc_added, NG)
            ffn_sync(7, combined)

        def flat(banks, n):
            return [(b, min(512, n - 512 * j)) for j, b in enumerate(banks)]

        def block7_pe():
            pe = nc.tensor
            block_before(pe, 7)
            pe.wait_ge(router_dve, ROUTER["compact"])
            for i, n in TILES:
                if i >= 8:
                    pe.wait_ge(r_x_evac, i - 7)
                for k in range(KD):
                    mm = pe.transpose(PS[0:n, i % 8, k * P:(k + 1) * P], xc[:, k, i * P:i * P + n], ident)
                mm.then_inc(r_x_ready, 1)
            pe.wait_ge(router_dve, ROUTER["stats"])
            for i, n in TILES:
                mm = pe.transpose(PS[0:6, i // 4, (i % 4) * P:(i % 4) * P + n], stat[0:n, i, :], ident[0:n, 0:n])
            mm.then_inc(router_pe, 1)
            pe.wait_ge(router_dve, ROUTER["stats_copied"])
            pe.wait_ge(wA_loaded, 144 + 32)
            for g in range(NG):
                sl = slice(g * GN, (g + 1) * GN)
                for k in range(KD):
                    pe.matmul(PS[:, 4 + g, 0:GN], r1[:, k, :], xc[:, k, sl], start=(k == 0), stop=False)
                pe.matmul(PS[:, 4 + g, 0:GN], r1s[0:6, :], statT[0:6, sl], start=False, stop=True).then_inc(r_h1p, 1)
            pe.wait_ge(r_h1, NG)
            pe.wait_ge(router_dve, ROUTER["psum_zeroed"])
            for i, n in TILES:
                mm = pe.matmul(PS[0:n, 0, i * E7:(i + 1) * E7], h1[:, i * P:i * P + n], r2, start=True, stop=True)
            mm.then_inc(router_pe, 1)
            pe.wait_ge(router_dve, ROUTER["scores"])
            for j, src in enumerate((small[1], small[2])):
                for i, n in TILES:
                    mm = pe.transpose(PS[0:E7, 1 + 3 * j + i // 4, (i % 4) * P:(i % 4) * P + n], src[0:n, i, :],
                                      ident[0:n, 0:n])
            mm.then_inc(router_pe, 1)
            pe.wait_ge(router_dve, ROUTER["kept"])
            for g in range(NG):
                pe.matmul(PS[0:16, g, 0:GN], const("two")[0:E7, :], keptW[0:E7, g * GN:(g + 1) * GN], start=True,
                          stop=True).then_inc(r_gw, 1)
            for i, n in TILES:
                mm = pe.transpose(PS[0:n, 4, i * E7:(i + 1) * E7], slotT[0:E7, i * P:i * P + n], ident[0:E7, 0:E7])
            mm.then_inc(router_pe, 1)
            pe.wait_ge(r_gw_evac, NG)
            for q in range(4):
                pe.wait_ge(pick_ready, q + 1)
                if q >= 2:
                    pe.wait_ge(xe_evac, q - 1)
                for k in range(KD):
                    for i in range(NTL):
                        mm = pe.matmul(PS[:, (2 if q % 2 else 6) + k, 0:G8], X[:, i, k * P:(k + 1) * P],
                                       pick[q % 2][:, i, :], start=(i == 0), stop=(i == NTL - 1))
                mm.then_inc(xe_ready, 1)
            pe.wait_ge(xe_evac, 4)

            def up(y, b, J, i):
                x = 2 * y + b
                pe.wait_ge(ex_full[x], 16 * i + 16)
                for half in range(2):
                    for k in range(KD):
                        mm = pe.matmul(PS[b * SP:(b + 1) * SP, 2 * y + half, :], ex_x[:, y, b, k, :],
                                       ex_w[x][:, k * 1024 + half * 512:k * 1024 + (half + 1) * 512],
                                       start=(k == 0), stop=(k == 1), skip_group_check=True)
                if b:
                    mm.then_inc(ex_up, 1)

            def turn_hidden(y, J):
                pe.wait_ge(ex_hid, J + 1)
                if not isinstance(J, int) or J >= 1:
                    pe.wait_ge(ex_turned_evac, J)
                for j in range(4):
                    mm = pe.transpose(PS[:, 4 + y, j * P:(j + 1) * P], ex_h[:, y, j * P:(j + 1) * P], ident)
                mm.then_inc(ex_turned, 1)

            def down(y, J, loads):
                for b in range(2):
                    pe.wait_ge(ex_down_full[2 * y + b], 16 * loads)
                pe.wait_ge(ex_turned_evac, J + 1)
                if not isinstance(J, int) or J >= 1:
                    pe.wait_ge(ex_out, J)
                for b in range(2):
                    for j in range(4):
                        mm = pe.matmul(PS[b * SP:(b + 1) * SP, 6 + y, 0:D],
                                       ex_hT[:, y, j * P + b * SP:j * P + (b + 1) * SP],
                                       ex_w[2 * y + b][:, 2048 + j * D:2048 + (j + 1) * D], start=(j == 0),
                                       stop=(j == 3), skip_group_check=True)
                    mm.then_inc(ex_down, 1)

            def body(i, first):
                for y in range(2):
                    J = 2 * i + y
                    pe.wait_ge(ex_x_ready, J + 2)
                    if not first:
                        pe.wait_ge(ex_hid, J - 1)
                    up(y, 0, J, i)
                    if y or not first:
                        turn_hidden(1 - y, J - 1)
                    up(y, 1, J, i)
                    if y or not first:
                        down(1 - y, J - 1, i + y)

            ex_loop(pe, body)
            turn_hidden(1, E7 // 2 - 1)
            down(1, E7 // 2 - 1, E7 // NX)
            pe.wait_ge(ex_out, E7 // 2)
            for q in range(E7 // 2):
                pe.wait_ge(place_ready, q + 1)
                for c in range(KD):
                    for g in range(NG):
                        mm = pe.matmul(PS[:, 2 * g + c, 0:GN], ye[:, q, c * P:(c + 1) * P],
                                       place[:, q % 2, g * GN:(g + 1) * GN], start=(q == 0), stop=(q == E7 // 2 - 1))
                mm.then_inc(sc_used, 1)
            pe.wait_ge(sc_added, NG)
            ffn_pe(7)
            ln_pe(7)

        def block7_act():
            a = nc.scalar
            block_before(a, 7)
            for i, n in TILES:
                if i == NTL - 1:
                    a.wait_ge(router_dve, ROUTER["last_tile_zeroed"])
                a.wait_ge(r_x_ready, i + 1)
                a.activation(X[0:n, i, :], PS[0:n, i % 8, 0:D], ACT.Copy).then_inc(r_x_evac, 1)
            a.wait_ge(r_x_evac, NTL)
            a.activation(sq7, X, ACT.Square).then_inc(router_act, 1)
            a.wait_ge(router_dve, ROUTER["deviations"])
            a.activation(tmp7, tmp7, ACT.Square).then_inc(router_act, 1)
            a.wait_ge(router_dve, ROUTER["squares"])
            a.activation(c7[:, 0:2 * NTL], c7[:, 0:2 * NTL], ACT.Sqrt).then_inc(router_act, 1)
            for g in range(NG):
                a.wait_ge(r_h1p, g + 1)
                a.activation(h1[:, g * GN:(g + 1) * GN], PS[:, 4 + g, 0:GN], ACT.Gelu, bias=r1b).then_inc(r_h1, 1)
            a.wait_ge(router_dve, ROUTER["shifted"])
            a.activation(small[0], small[0], ACT.Exp).then_inc(router_act, 1)
            for q in range(4):
                a.wait_ge(xe_ready, q + 1)
                bank = 2 if q % 2 else 6
                a.activation(xe[:, :, q * G8:(q + 1) * G8], PS[:, bank:bank + 2, 0:G8], ACT.Copy).then_inc(xe_evac, 1)

            def evacuate_turned(y, J):
                a.wait_ge(ex_turned, J + 1)
                if not isinstance(J, int) or J >= 1:
                    a.wait_ge(ex_down, 2 * J)
                a.activation(ex_hT[:, y, :], PS[:, 4 + y, :], ACT.Copy).then_inc(ex_turned_evac, 1)

            def body(i, first):
                for y in range(2):
                    J = 2 * i + y
                    if y or not first:
                        evacuate_turned(1 - y, J - 1)
                    a.wait_ge(ex_up, J + 1)
                    if not first:
                        a.wait_ge(ex_hid, J - 1)
                    a.activation(ex_sg[:, y, :], PS[:, 2 * y, :], ACT.Silu).then_inc(ex_sg_ready, 1)

            ex_loop(a, body)
            evacuate_turned(1, E7 // 2 - 1)
            ffn_act(7)
            ln_act(7)

        def block7_pool():
            po = nc.gpsimd
            po.wait_ge(xe_evac, 4)
            po.memset(ex_x[:, :, :, :, CAP:SP], 0.0).then_inc(ex_x_ready, 1)

            def body(i, first):
                for y in range(2):
                    J = 2 * i + y
                    if not first:
                        po.wait_ge(ex_up, J - 1)
                    for b in range(2):
                        e = 2 * J + b
                        src = xe[:, :, bass.ds(po.snap(e * CAP) if not first else e * CAP, CAP)]
                        ins = po.tensor_copy(ex_x[:, y, b, :, 0:CAP], src)
                    ins.then_inc(ex_x_ready, 1)

            ex_loop(po, body)

        def block7_dve():
            v = nc.vector
            block_before(v, 7)
            for k in range(KD):
                for g in range(NG):
                    ins = v.tensor_copy(compact(xc[:, k, g * GN:(g + 1) * GN]), hgroup(k, g))
            ins.then_inc(router_dve, 1)
            v.memset(X[:, NTL - 1, :], 0.0).then_inc(router_dve, 1)
            v.wait_ge(r_x_evac, NTL)
            dve_then(v.tensor_reduce(stat[:, :, 0], X, AX, ALU.add))
            dve_then(v.tensor_scalar(stat[:, :, 0], stat[:, :, 0], 1.0 / D, None, ALU.mult))
            v.tensor_tensor(tmp7, X, per(stat[:, :, 0], D), ALU.subtract).then_inc(router_dve, 1)
            v.tensor_reduce(stat[:, :, 2], X, AX, ALU.min)
            v.tensor_reduce(stat[:, :, 3], X, AX, ALU.max)
            dve_then(v.tensor_scalar(nz7, X, -1e-6, None, ALU.is_gt))
            dve_then(v.scalar_tensor_tensor(out=nz7, in0=X, scalar=1e-6, in1=nz7, op0=ALU.is_lt, op1=ALU.mult))
            v.wait_ge(router_act, ROUTER["squared"])
            dve_then(v.tensor_reduce(c7[:, 0:NTL], sq7, AX, ALU.add))
            v.wait_ge(router_act, ROUTER["deviations_squared"])
            dve_then(v.tensor_reduce(c7[:, NTL:2 * NTL], tmp7, AX, ALU.add))
            v.tensor_scalar(c7[:, NTL:2 * NTL], c7[:, NTL:2 * NTL], 1.0 / (D - 1), None,
                            ALU.mult).then_inc(router_dve, 1)
            v.wait_ge(router_dve, ROUTER["squares"])
            dve_then(v.tensor_reduce(stat[:, :, 5], nz7, AX, ALU.add))
            dve_then(v.tensor_scalar(stat[:, :, 5], stat[:, :, 5], 1.0 / D, None, ALU.mult))
            v.wait_ge(router_act, ROUTER["roots"])
            dve_then(v.tensor_copy(stat[:, :, 4], c7[:, 0:NTL]))
            v.tensor_copy(stat[:, :, 1], c7[:, NTL:2 * NTL]).then_inc(router_dve, 1)
            v.wait_ge(router_pe, ROUTER["stats_turned"])
            for b, n in flat(range(3), NT):
                ins = v.tensor_copy(statT[0:6, 512 * b:512 * b + n], PS[0:6, b, 0:n])
            ins.then_inc(router_dve, 1)
            v.wait_ge(router_dve, ROUTER["stats_copied"])
            v.memset(PS[:, 0, :], 0.0).then_inc(router_dve, 1)
            v.wait_ge(router_pe, ROUTER["logits"])
            lg = PS[:, 0, 0:NTL * E7].rearrange("q (i e) -> q i e", i=NTL)
            pr, score, weight, sel, gt, eq, pre, rst, t8 = small
            dve_then(v.tensor_reduce(c7[:, 0:NTL], lg, AX, ALU.max))
            v.tensor_tensor(pr, lg, per(c7[:, 0:NTL], E7), ALU.subtract).then_inc(router_dve, 1)
            v.wait_ge(router_act, ROUTER["exponentials"])
            dve_then(v.tensor_reduce(c7[:, 0:NTL], pr, AX, ALU.add))
            dve_then(v.reciprocal(c7[:, NTL:2 * NTL], c7[:, 0:NTL]))
            dve_then(v.tensor_tensor(pr, pr, per(c7[:, NTL:2 * NTL], E7), ALU.mult))
            choose_dve(pr, NTL, E7, 2, sel, (m8_7, gt, eq, pre, c7[:, 2 * NTL:3 * NTL]), rst)
            dve_then(v.tensor_tensor(t8, pr, sel, ALU.mult))
            dve_then(v.tensor_reduce(c7[:, 0:NTL], t8, AX, ALU.add))
            dve_then(v.reciprocal(c7[:, NTL:2 * NTL], c7[:, 0:NTL]))
            dve_then(v.tensor_tensor(weight, t8, per(c7[:, NTL:2 * NTL], E7), ALU.mult))
            dve_then(v.tensor_scalar(gt, sel, 1.0, None, ALU.subtract))
            v.tensor_tensor(score, t8, gt, ALU.add).then_inc(router_dve, 1)
            v.wait_ge(router_pe, ROUTER["scores_turned"])
            for j, dst in enumerate((scoreT, weightT)):
                for b, n in flat(range(3), NT):
                    ins = v.tensor_copy(dst[0:E7, 512 * b:512 * b + n], PS[0:E7, 1 + 3 * j + b, 0:n])
            dve_then(ins)
            S = lambda x: x[0:E7]
            cur, nxt = scoreT, wk0
            for _ in range(CAP_ROUNDS):
                dve_then(v.max(S(m8T), S(cur)))
                dve_then(v.match_replace(S(nxt), S(m8T), S(cur), -2.0))
                cur, nxt = nxt, (wk1 if nxt is wk0 else wk0)
            dve_then(v.max(S(m8T), S(cur)))
            thr = m8T[0:E7, CAP_REST - 1:CAP_REST]
            v.memset(S(nxt), 1.0)
            v.tensor_scalar(S(gtT), S(cur), thr, None, ALU.is_gt)
            dve_then(v.tensor_scalar(S(eqT), S(cur), thr, None, ALU.is_equal))
            v.tensor_tensor_scan(S(preT), S(nxt), S(eqT), 0.0, ALU.mult, ALU.add)
            dve_then(v.tensor_reduce(S(roomT), S(gtT), AX, ALU.add))
            dve_then(v.tensor_scalar(S(roomT), S(roomT), -1.0, float(CAP_REST), ALU.mult, ALU.add))
            dve_then(v.tensor_scalar(S(preT), S(preT), roomT[0:E7, 0:1], None, ALU.is_le))
            dve_then(v.tensor_tensor(S(eqT), S(eqT), S(preT), ALU.mult))
            dve_then(v.tensor_tensor(S(gtT), S(gtT), S(eqT), ALU.add))
            dve_then(v.tensor_tensor(S(eqT), S(cur), S(scoreT), ALU.not_equal))
            dve_then(v.tensor_tensor(S(gtT), S(gtT), S(eqT), ALU.add))
            dve_then(v.tensor_scalar(S(eqT), S(scoreT), -0.5, None, ALU.is_gt))
            dve_then(v.tensor_tensor(S(gtT), S(gtT), S(eqT), ALU.mult))
            dve_then(v.tensor_tensor_scan(S(preT), S(nxt), S(gtT), 0.0, ALU.mult, ALU.add))
            dve_then(v.tensor_tensor(S(preT), S(preT), S(gtT), ALU.mult))
            dve_then(v.tensor_scalar(S(slotT), S(preT), 1.0, None, ALU.subtract))
            v.tensor_tensor(S(keptW), S(weightT), S(gtT), ALU.mult).then_inc(router_dve, 1)
            for g in range(NG):
                v.wait_ge(r_gw, g + 1)
                v.tensor_scalar(gwT[:, g * GN:(g + 1) * GN], PS[0:16, g, 0:GN], 0.05, None,
                                ALU.mult).then_inc(r_gw_evac, 1)
            dve_then(v.memset(slot[:, NTL - 1, :], -1.0))
            v.wait_ge(router_pe, ROUTER["slots_turned"])
            v.tensor_copy(slot[:, 0:NTL - 1, :], PS[:, 4, 0:(NTL - 1) * E7].rearrange("q (i e) -> q i e", e=E7))
            dve_then(v.tensor_copy(slot[0:LASTN, NTL - 1, :], PS[0:LASTN, 4, (NTL - 1) * E7:NTL * E7]))
            v.memset(PS[:, 4, :], 0.0).then_inc(router_dve, 1)
            for q in range(4):
                if q >= 2:
                    v.wait_ge(xe_ready, q - 1)
                for i in range(NTL):
                    ins = v.tensor_tensor(pick[q % 2][:, i, :].rearrange("q (e c) -> q e c", c=CAP), bcast(const("iota"), 0, 8),
                                          per(slot[:, i, q * 8:(q + 1) * 8], CAP), ALU.is_equal)
                ins.then_inc(pick_ready, 1)
            v.wait_ge(router_dve, ROUTER["slots_copied"])
            ffn_begin_dve()

            ye_flat = ye.rearrange("q p n -> q (p n)")

            def evacuate(y, J):
                v.wait_ge(ex_down, 2 * J + 2)
                at = J * D
                dst = ye_flat[:, at:at + D] if isinstance(J, int) else ye_flat[:, bass.ds(at, D)]
                v.tensor_copy(dst, PS[:, 6 + y, 0:D]).then_inc(ex_out, 1)

            def body(i, first):
                for y in range(2):
                    J = 2 * i + y
                    v.wait_ge(ex_sg_ready, J + 1)
                    if not first:
                        v.wait_ge(ex_turned, J - 1)
                    v.tensor_tensor(ex_h[:, y, :], ex_sg[:, y, :], PS[:, 2 * y + 1, :], ALU.mult).then_inc(ex_hid, 1)
                    if y or not first:
                        evacuate(1 - y, J - 1)

            ex_loop(v, body)
            evacuate(1, E7 // 2 - 1)
            for q in range(E7 // 2):
                v.wait_ge(place_in_full[q % 2], 64 * (q // 2 + 1))
                if q >= 2:
                    v.wait_ge(sc_used, q - 1)
                v.scalar_tensor_tensor(out=place[:, q % 2, :], in0=place_in[q % 2][:, 0, :], scalar=const("slotno"),
                                       in1=place_in[q % 2][:, 1, :], op0=ALU.is_equal,
                                       op1=ALU.mult).then_inc(place_ready, 1)
            v.wait_ge(acc_begun, 4)
            v.wait_ge(sc_used, E7 // 2)
            for g in range(NG):
                sl = slice(g * GN, (g + 1) * GN)
                v.tensor_tensor(acc[:, :, sl], acc[:, :, sl], PS[:, 2 * g:2 * g + 2, 0:GN], ALU.add).then_inc(sc_added, 1)
            v.wait_ge(sc_added, NG)
            ffn_dve(7)
            ln_dve(7)

        yout = arena[:, 0:2560].rearrange("q (i n) -> q i n", i=10)
        turned = sem("turned")
        y_ready = sem("y_ready")
        out_rows = out.rearrange("a t d -> (a t) d")

        def finish_dve():
            v = nc.vector
            block_before(v, 8)
            for k in range(KD):
                for g in range(NG):
                    ins = v.tensor_copy(compact(xc[:, k, g * GN:(g + 1) * GN]), hgroup(k, g))
            ins.then_inc(turned, 1)

        def finish_pe():
            pe = nc.tensor
            pe.wait_ge(turned, 1)
            for i, n in TILES:
                if i >= 8:
                    pe.wait_ge(y_ready, i - 7)
                for k in range(KD):
                    mm = pe.transpose(PS[0:n, i % 8, k * P:(k + 1) * P], xc[:, k, i * P:i * P + n], ident)
                mm.then_inc(turned, 1)

        def finish_act():
            for i, n in TILES:
                nc.scalar.wait_ge(turned, i + 2)
                nc.scalar.activation(yout[0:n, i, :], PS[0:n, i % 8, 0:D], ACT.Copy).then_inc(y_ready, 1)

        def finish_sync():
            for i, n in TILES:
                nc.sync.wait_ge(y_ready, i + 1)
                nc.sync.dma_start(out_rows[i * P:i * P + n, :], yout[0:n, i, :]).then_inc(all_stored, 16)
            nc.sync.wait_ge(all_stored, 16 * len(TILES))

        @block.sync
        def _(sp):
            start_sync()
            tok_sync()
            block0_loads()
            block1_sync()
            block2_sync()
            block3_sync()
            block4_sync()
            block5_sync()
            block6_sync()
            block7_sync()
            finish_sync()

        @block.gpsimd
        def _(pool):
            start_pool()
            block3_pool()
            block5_pool()
            block4_pool()
            block7_pool()

        @block.tensor
        def _(pe):
            start_engine(pe)
            tok_pe()
            block0_pe()
            block1_pe()
            block2_pe()
            block3_pe()
            block4_pe()
            block5_pe()
            block6_pe()
            block7_pe()
            finish_pe()

        @block.scalar
        def _(act):
            start_engine(act)
            block0_act()
            block1_act()
            block2_act()
            block3_act()
            block4_act()
            block5_act()
            block6_act()
            block7_act()
            finish_act()

        @block.vector
        def _(dve):
            start_engine(dve)
            tok_dve()
            block0_dve()
            block1_dve()
            block2_dve()
            block3_dve()
            block4_dve()
            block5_dve()
            block6_dve()
            block7_dve()
            finish_dve()


def rows(w):
    k = w.shape[0] // P
    return w.reshape(k, P, w.shape[1]).transpose(1, 0, 2).reshape(P, -1)


def wide_heads(w):
    return np.pad(w.reshape(w.shape[0], HEADS, HD), ((0, 0), (0, 0), (0, HD))).reshape(w.shape[0], 2 * D)


def columns(b):
    return b.reshape(-1, P).T


def units(wg, wu, wd):
    e, _, f = wg.shape
    u = f // P
    g = wg.reshape(e, KD, P, u, P).transpose(0, 2, 3, 1, 4).reshape(e, P, u, KD * P)
    p = wu.reshape(e, KD, P, u, P).transpose(0, 2, 3, 1, 4).reshape(e, P, u, KD * P)
    d = wd.reshape(e, u, P, D).transpose(0, 2, 1, 3)
    return np.concatenate([g, p, d], 3).reshape(e, P, u * UNIT)


def lay_out(i):
    t = lambda w: np.swapaxes(w, -1, -2)
    a = {"consts": CONSTS}
    x = i["x"].reshape(NG, GI, 3, 6, 16, 6, 16).transpose(0, 2, 4, 6, 1, 3, 5).reshape(NG, 6, P, -1)
    a["patches"] = x.transpose(0, 2, 1, 3).reshape(NG, P, -1)
    side = np.concatenate([i["L0_tok_pos_embedding"][0], i["L0_tok_b"][None], i["L0_tok_cls_token"][0]])
    a["tok_w"] = np.concatenate([rows(t(i["L0_tok_W"])), rows(t(side))], 1)
    a["attn0"] = np.concatenate([rows(wide_heads(t(i["L0_attn_Wq"]))), rows(wide_heads(t(i["L0_attn_Wk"]))),
                                 rows(t(i["L0_attn_Wv"])), rows(t(i["L0_attn_Wout"])), columns(i["L0_attn_bout"])], 1)
    a["gates"] = np.concatenate([rows(i["L0_ffn_Wr"]), rows(t(i["L1_ffn_w_gate"]))], 1)
    a["ffn0"] = units(i["L0_ffn_Wg"], i["L0_ffn_Wu"], i["L0_ffn_Wd"])
    a["splat"] = np.concatenate([rows(t(i["L1_attn_splat_positions"])), rows(i["L1_attn_Wv"]), rows(i["L1_attn_Wo"])], 1)
    a["splat_side"] = np.concatenate([i["L1_attn_splat_positions"], i["L1_attn_splat_log_scales"][:, None],
                                      i["L1_attn_splat_amplitudes"][:, None]], 1)
    half = lambda w: t(w).reshape(D, 2, P).transpose(1, 0, 2)
    a["ffn1"] = units(np.concatenate([t(i["L1_ffn_w1_e"]), half(i["L1_ffn_w1_s"])]),
                      np.concatenate([t(i["L1_ffn_w3_e"]), half(i["L1_ffn_w3_s"])]),
                      np.concatenate([t(i["L1_ffn_w2_e"]), t(i["L1_ffn_w2_s"]).reshape(2, P, D)]))
    a["slots"] = np.concatenate([rows(i["L2_attn_Wq"]), rows(i["L2_attn_Wk"]), rows(i["L2_attn_Wv"]), rows(i["L2_attn_Wo"]),
                                 rows(np.concatenate([i["L2_attn_Wf1"], i["L2_attn_Wg1"]], 1))], 1)
    a["slots_2"] = np.concatenate([i["L2_attn_Wf2"], np.pad(i["L2_attn_Wg2"], ((0, 0), (0, D)))], 0)
    a["norm_w"] = i["L2_attn_norm_w"][None]
    a["ffn2"] = units(t(i["L2_ffn_w_gate"])[None], t(i["L2_ffn_w_up"])[None], t(i["L2_ffn_w_down"])[None])[0]
    w, b = i["L3_attn_Wqkv_w"], i["L3_attn_Wqkv_b"]
    conv = i["L3_attn_conv_w"]
    wide = lambda v: columns(wide_heads(v[None])[0])
    a["attn3"] = np.concatenate(
        [rows(wide_heads(t(w[0:D]))), rows(wide_heads(t(w[D:2 * D]))), rows(t(w[2 * D:])), rows(t(i["L3_attn_out_w"]))]
        + [rows(wide_heads(t(conv[:, :, tap]))) for tap in range(3)]
        + [wide(b[0:D]), wide(b[D:2 * D]), wide(i["L3_attn_conv_b"]), columns(i["L3_attn_out_b"])], 1)
    a["v_bias"] = b[None, 2 * D:]
    up = t(i["L3_ffn_w_up"]).reshape(32, KD, P, 1024).transpose(0, 2, 1, 3).reshape(32, P, -1)
    down = t(i["L3_ffn_w_down"]).reshape(32, 4, P, D).transpose(0, 2, 1, 3).reshape(32, P, -1)
    a["experts"] = np.concatenate([up, down], 2)
    r1 = t(i["L3_ffn_r1_w"])
    a["router"] = np.concatenate([rows(r1[0:D]), t(i["L3_ffn_r2_w"]), i["L3_ffn_r1_b"][:, None]], 1)
    a["router_stats"] = r1[D:]
    gate, upper = np.split(t(i["L3_ffn_a_up"]), 2, axis=-1)
    a["ffn3"] = units(gate, upper, t(i["L3_ffn_a_down"]))
    return {k: np.ascontiguousarray(v) for k, v in a.items()}


def kernel(**inputs):
    import concourse.bacc as bacc
    from concourse.bass_utils import run_bass_kernel_spmd

    arrays = {f"in_{k}": v for k, v in lay_out({k: np.asarray(v) for k, v in inputs.items()}).items()}
    nc = bacc.Bacc("TRN2", target_bir_lowering=False, num_devices=1)
    inp = {k[3:]: nc.dram_tensor(k, v.shape, mybir.dt.from_np(v.dtype), kind="ExternalInput").ap()
           for k, v in arrays.items()}
    out = nc.dram_tensor("out", (B, T, D), F32, kind="ExternalOutput").ap()
    scratch = nc.dram_tensor("scratch", (3, 32, NT), F32, kind="Internal").ap()
    tower(nc, inp, out, scratch)
    r = run_bass_kernel_spmd(nc, [arrays], core_ids=[0])
    return r.results[0]["out"]
```
